# Optimizing a Trainium2 kernel written in Bass

```python
import numpy as np
import jax
import jax.numpy as jnp

def _softmax(x, axis=-1):
    return jax.nn.softmax(x, axis=axis)

def _gelu(x):
    return jax.nn.gelu(x, approximate=True)

def _silu(x):
    return jax.nn.silu(x)

def _sigmoid(x):
    return jax.nn.sigmoid(x)

def _layernorm(x, axis=-1, eps=1e-05):
    m = jnp.mean(x, axis=axis, keepdims=True)
    v = jnp.var(x, axis=axis, keepdims=True)
    return (x - m) / jnp.sqrt(v + eps)

def _scatter_add(tgt, idx, src, axis=0):
    return tgt.at[idx].add(src)

def _segment_sum(src, seg, n):
    return jax.ops.segment_sum(src, seg, n)
kernel_name = 'mk_adaln_attn_ffn_d1_seqx_r4_c226a1'

def setup_inputs(seed: int=0):
    np.random.seed(seed)
    _w = jnp.asarray

    def _rec_inputs():
        import jax
        import jax.numpy as jnp
        _rk = jax.random.key(seed)
        x = -0.0001538 + 1 * jax.random.normal(jax.random.fold_in(_rk, 1), (8, 512, 256), jnp.float32)
        _lenS = 512 - jax.random.randint(jax.random.fold_in(_rk, 7), (8,), 0, max(1, 512 // 4) + 1, jnp.int32)
        _lenS2 = 512 - jax.random.randint(jax.random.fold_in(_rk, 8), (8,), 0, max(1, 512 // 4) + 1, jnp.int32)
        cond_1024 = 0.00782532 + 1.00527 * jax.random.normal(jax.random.fold_in(_rk, 11), (8, 256), jnp.float32)
        return (x, cond_1024)
    x, cond_1024 = _rec_inputs()

    def _L0_cond_setup():
        import jax, jax.numpy as jnp
        import numpy as np
        NUM_EXPERTS = 4
        TOP_K = 2
        key = jax.random.key(seed)
        ks = jax.random.split(key, 16)
        B, L, D, E, H = (8, 192, 256, NUM_EXPERTS, 1024)
        s = 0.02
        return {'context_c': jax.random.normal(ks[0], (B, L, D), jnp.float32), 'time_cond': jax.random.normal(ks[1], (B, D), jnp.float32), 'gate_w': jax.random.normal(ks[2], (3 * D, E), jnp.float32) * s, 'gate_b': jnp.zeros((E,), jnp.float32), 'time_w': jax.random.normal(ks[3], (D, 2 * E), jnp.float32) * s, 'time_b': jnp.zeros((2 * E,), jnp.float32), 'ew1': jax.random.normal(ks[4], (E, D, H), jnp.float32) * s, 'eb1': jnp.zeros((E, H), jnp.float32), 'ew2': jax.random.normal(ks[5], (E, H, D), jnp.float32) * s, 'eb2': jnp.zeros((E, D), jnp.float32), 'sw1': jax.random.normal(ks[6], (D, H), jnp.float32) * s, 'sb1': jnp.zeros((H,), jnp.float32), 'sw2': jax.random.normal(ks[7], (H, D), jnp.float32) * s, 'sb2': jnp.zeros((D,), jnp.float32)}
    _L0_cond_all = _L0_cond_setup()
    _L0_cond_in = {k: v for k, v in _L0_cond_all.items() if k in ('gate_w', 'gate_b', 'time_w', 'time_b', 'ew1', 'eb1', 'ew2', 'eb2', 'sw1', 'sb1', 'sw2', 'sb2')}
    del _L0_cond_all

    def _L0_attn_setup():
        import jax, jax.numpy as jnp
        import numpy as np
        B, S, D = (8, 1024, 256)
        H, DK, DV, L = (8, 64, 64, 64)
        key = jax.random.key(seed)
        ks = jax.random.split(key, 6)
        x = jax.random.normal(ks[0], (B, S, D), dtype=jnp.float32)
        sd = 1.0 / np.sqrt(D)
        Wq = jax.random.normal(ks[1], (D, H * DK), dtype=jnp.float32) * sd
        Wk = jax.random.normal(ks[2], (D, H * DK), dtype=jnp.float32) * sd
        Wv = jax.random.normal(ks[3], (D, H * DV), dtype=jnp.float32) * sd
        betas = jax.random.normal(ks[4], (1, H, 1, DV), dtype=jnp.float32)
        Wo = jax.random.normal(ks[5], (H * DV, D), dtype=jnp.float32) * (1.0 / np.sqrt(H * DV))
        return {'x': x, 'Wq': Wq, 'Wk': Wk, 'Wv': Wv, 'betas': betas, 'Wo': Wo}
    _L0_attn_all = _L0_attn_setup()
    _L0_attn_in = {k: v for k, v in _L0_attn_all.items() if k in ('Wq', 'Wk', 'Wv', 'betas', 'Wo')}
    del _L0_attn_all

    def _L0_cond2_setup():
        import math
        import jax, jax.numpy as jnp
        import numpy as np
        EPS = 1e-07
        MAX_TANH_ARG = 1.0 - 1e-05

        def _norm(x):
            return jnp.sqrt(jnp.sum(x * x, axis=-1, keepdims=True)).clip(EPS)

        def logmap0(x):
            n = _norm(x)
            return jnp.arctanh(jnp.clip(n, EPS, MAX_TANH_ARG)) * x / n

        def expmap0(v):
            n = _norm(v)
            return jnp.tanh(n) * v / n

        def mobius_add(x, y):
            x2 = jnp.sum(x * x, -1, keepdims=True)
            y2 = jnp.sum(y * y, -1, keepdims=True)
            xy = jnp.sum(x * y, -1, keepdims=True)
            num = (1 + 2 * xy + y2) * x + (1 - x2) * y
            den = (1 + 2 * xy + x2 * y2).clip(EPS)
            return num / den

        def plin(x, w, b):
            return expmap0(logmap0(x) @ w + b)

        def layer_norm(x, eps=1e-06):
            m = x.mean(-1, keepdims=True)
            v = ((x - m) ** 2).mean(-1, keepdims=True)
            return (x - m) / jnp.sqrt(v + eps)

        def _beta(a, b):
            return math.exp(math.lgamma(a) + math.lgamma(b) - math.lgamma(a + b))
        D, H, FF = (256, 16, 1024)
        HD = D // H
        BETA_N = _beta(D / 2, 0.5)
        BETA_H = _beta(HD / 2, 0.5)

        def _to_heads(p):
            B, S, _ = p.shape
            t = logmap0(p).reshape(B, S, H, HD) * (BETA_H / BETA_N)
            return expmap0(jnp.transpose(t, (0, 2, 1, 3)))

        def _from_heads(ph):
            B, _, S, _ = ph.shape
            t = logmap0(ph) * (BETA_N / BETA_H)
            t = jnp.transpose(t, (0, 2, 1, 3)).reshape(B, S, D)
            return expmap0(t)
        key = jax.random.key(seed)
        ks = jax.random.split(key, 20)
        B, S = (4, 256)
        x = expmap0(0.02 * jax.random.normal(ks[0], (B, S, D), jnp.float32))
        t_emb = jax.random.normal(ks[1], (B, 1, D), jnp.float32)
        g = lambda k, sh: 0.02 * jax.random.normal(k, sh, jnp.float32)
        return {'x': x, 't_emb': t_emb, 'w_q': g(ks[2], (D, D)), 'b_q': jnp.zeros((D,), jnp.float32), 'w_k': g(ks[3], (D, D)), 'b_k': jnp.zeros((D,), jnp.float32), 'w_v': g(ks[4], (D, D)), 'b_v': jnp.zeros((D,), jnp.float32), 'w_o': g(ks[5], (D, D)), 'b_o': jnp.zeros((D,), jnp.float32), 'w_f1': g(ks[6], (D, FF)), 'b_f1': jnp.zeros((FF,), jnp.float32), 'w_f2': g(ks[7], (FF, D)), 'b_f2': jnp.zeros((D,), jnp.float32), 'w_ada': g(ks[8], (D, 6 * D)), 'b_ada': jnp.zeros((6 * D,), jnp.float32)}
    _L0_cond2_all = _L0_cond2_setup()
    _L0_cond2_in = {k: v for k, v in _L0_cond2_all.items() if k in ('w_q', 'b_q', 'w_k', 'b_k', 'w_v', 'b_v', 'w_o', 'b_o', 'w_f1', 'b_f1', 'w_f2', 'b_f2', 'w_ada', 'b_ada')}
    del _L0_cond2_all

    def _L0_ffn_setup():
        import jax, jax.numpy as jnp
        import numpy as np
        DIM = 256
        DEPTH = 2
        HEADS = 8
        DIM_HEAD = 64
        WINDOW = 128
        INNER = HEADS * DIM_HEAD
        HID = int(DIM * 4 * 2 / 3)
        B, N = (2, 2048)
        QK_SCALE = 8.0

        def shift_token(t):
            t1, t2 = jnp.split(t, 2, axis=-1)
            t2 = jnp.pad(t2, ((0, 0), (1, 0), (0, 0)))[:, :-1]
            return jnp.concatenate([t1, t2], axis=-1)

        def l2norm(t):
            return t / jnp.clip(jnp.linalg.norm(t, axis=-1, keepdims=True), 1e-12)

        def rotate_half(x):
            x1, x2 = jnp.split(x, 2, axis=-1)
            return jnp.concatenate([-x2, x1], axis=-1)

        def rotary_xpos(q, k):
            n = q.shape[-2]
            half_idx = jnp.arange(0, DIM_HEAD, 2, dtype=jnp.float32)
            inv_freq = 1.0 / 10000.0 ** (half_idx / DIM_HEAD)
            t = jnp.arange(n, dtype=jnp.float32)
            freqs = t[:, None] * inv_freq[None, :]
            freqs = jnp.concatenate([freqs, freqs], axis=-1)
            base = (half_idx + 0.4 * DIM_HEAD) / (1.4 * DIM_HEAD)
            power = (t - n // 2) / float(WINDOW // 2)
            scale = base[None, :] ** power[:, None]
            scale = jnp.concatenate([scale, scale], axis=-1)
            cos, sin = (jnp.cos(freqs), jnp.sin(freqs))
            q = q * cos * scale + rotate_half(q) * sin * scale
            k = k * cos / scale + rotate_half(k) * sin / scale
            return (q, k)

        def local_attention(q, k, v):
            b, h, n, d = q.shape
            w = n // WINDOW
            bq = q.reshape(b, h, w, WINDOW, d) * QK_SCALE
            bk = k.reshape(b, h, w, WINDOW, d)
            bv = v.reshape(b, h, w, WINDOW, d)

            def look_around(t):
                p = jnp.pad(t, ((0, 0), (0, 0), (1, 0), (0, 0), (0, 0)))
                return jnp.concatenate([p[:, :, :w], p[:, :, 1:]], axis=3)
            bk, bv = (look_around(bk), look_around(bv))
            bt = jnp.arange(n).reshape(w, WINDOW)
            btp = jnp.pad(bt, ((1, 0), (0, 0)), constant_values=-1)
            btk = jnp.concatenate([btp[:w], btp[1:]], axis=1)
            sim = jnp.einsum('bhwid,bhwjd->bhwij', bq, bk)
            i = bt[:, :, None]
            j = btk[:, None, :]
            mask = (i < j) | (i > j + WINDOW) | (j == -1)
            sim = jnp.where(mask, -jnp.finfo(sim.dtype).max, sim)
            attn = jax.nn.softmax(sim, axis=-1)
            out = jnp.einsum('bhwij,bhwjd->bhwid', attn, bv)
            return out.reshape(b, h, n, d)

        def _layer(x, wqkv, qs, ksc, wo, lg, lb, w1, b1, w2, b2):
            b, n, _ = x.shape
            h = shift_token(x)
            qkv = h @ wqkv
            q, k, v = jnp.split(qkv, 3, axis=-1)
            to_heads = lambda t: t.reshape(b, n, HEADS, DIM_HEAD).transpose(0, 2, 1, 3)
            q, k, v = (to_heads(q), to_heads(k), to_heads(v))
            q = l2norm(q) * qs
            k = l2norm(k) * ksc
            q, k = rotary_xpos(q, k)
            o = local_attention(q, k, v)
            o = o.transpose(0, 2, 1, 3).reshape(b, n, INNER)
            x = x + o @ wo
            h = shift_token(x)
            mu = h.mean(-1, keepdims=True)
            var = h.var(-1, keepdims=True)
            h = (h - mu) / jnp.sqrt(var + 1e-05) * lg + lb
            h = h @ w1 + b1
            a, g = jnp.split(h, 2, axis=-1)
            h = a * jax.nn.gelu(g, approximate=False)
            x = x + h @ w2 + b2
            return x
        key = jax.random.key(seed)
        ks = jax.random.split(key, 6)
        return {'x': jax.random.normal(ks[0], (B, N, DIM), jnp.float32), 'wqkv': jax.random.normal(ks[1], (DEPTH, DIM, 3 * INNER), jnp.float32) * 0.02, 'q_scale': jnp.ones((DEPTH, DIM_HEAD), jnp.float32), 'k_scale': jnp.ones((DEPTH, DIM_HEAD), jnp.float32), 'wo': jax.random.normal(ks[2], (DEPTH, INNER, DIM), jnp.float32) * 0.02, 'ln_g': jnp.ones((DEPTH, DIM), jnp.float32), 'ln_b': jnp.zeros((DEPTH, DIM), jnp.float32), 'w1': jax.random.normal(ks[3], (DEPTH, DIM, 2 * HID), jnp.float32) * 0.02, 'b1': jnp.zeros((DEPTH, 2 * HID), jnp.float32), 'w2': jax.random.normal(ks[4], (DEPTH, HID, DIM), jnp.float32) * 0.02, 'b2': jnp.zeros((DEPTH, DIM), jnp.float32)}
    _L0_ffn_all = _L0_ffn_setup()
    _L0_ffn_in = {k: v for k, v in _L0_ffn_all.items() if k in ('wqkv', 'q_scale', 'k_scale', 'wo', 'ln_g', 'ln_b', 'w1', 'b1', 'w2', 'b2')}
    del _L0_ffn_all
    return {'x': x, 'cond_1024': cond_1024, 'L0_cond_gate_w': _L0_cond_in['gate_w'], 'L0_cond_gate_b': _L0_cond_in['gate_b'], 'L0_cond_time_w': _L0_cond_in['time_w'], 'L0_cond_time_b': _L0_cond_in['time_b'], 'L0_cond_ew1': _L0_cond_in['ew1'], 'L0_cond_eb1': _L0_cond_in['eb1'], 'L0_cond_ew2': _L0_cond_in['ew2'], 'L0_cond_eb2': _L0_cond_in['eb2'], 'L0_cond_sw1': _L0_cond_in['sw1'], 'L0_cond_sb1': _L0_cond_in['sb1'], 'L0_cond_sw2': _L0_cond_in['sw2'], 'L0_cond_sb2': _L0_cond_in['sb2'], 'L0_attn_Wq': _L0_attn_in['Wq'], 'L0_attn_Wk': _L0_attn_in['Wk'], 'L0_attn_Wv': _L0_attn_in['Wv'], 'L0_attn_betas': _L0_attn_in['betas'], 'L0_attn_Wo': _L0_attn_in['Wo'], 'L0_cond2_w_q': _L0_cond2_in['w_q'], 'L0_cond2_b_q': _L0_cond2_in['b_q'], 'L0_cond2_w_k': _L0_cond2_in['w_k'], 'L0_cond2_b_k': _L0_cond2_in['b_k'], 'L0_cond2_w_v': _L0_cond2_in['w_v'], 'L0_cond2_b_v': _L0_cond2_in['b_v'], 'L0_cond2_w_o': _L0_cond2_in['w_o'], 'L0_cond2_b_o': _L0_cond2_in['b_o'], 'L0_cond2_w_f1': _L0_cond2_in['w_f1'], 'L0_cond2_b_f1': _L0_cond2_in['b_f1'], 'L0_cond2_w_f2': _L0_cond2_in['w_f2'], 'L0_cond2_b_f2': _L0_cond2_in['b_f2'], 'L0_cond2_w_ada': _L0_cond2_in['w_ada'], 'L0_cond2_b_ada': _L0_cond2_in['b_ada'], 'L0_ffn_wqkv': _L0_ffn_in['wqkv'], 'L0_ffn_q_scale': _L0_ffn_in['q_scale'], 'L0_ffn_k_scale': _L0_ffn_in['k_scale'], 'L0_ffn_wo': _L0_ffn_in['wo'], 'L0_ffn_ln_g': _L0_ffn_in['ln_g'], 'L0_ffn_ln_b': _L0_ffn_in['ln_b'], 'L0_ffn_w1': _L0_ffn_in['w1'], 'L0_ffn_b1': _L0_ffn_in['b1'], 'L0_ffn_w2': _L0_ffn_in['w2'], 'L0_ffn_b2': _L0_ffn_in['b2']}

def reference(x, cond_1024, L0_cond_gate_w, L0_cond_gate_b, L0_cond_time_w, L0_cond_time_b, L0_cond_ew1, L0_cond_eb1, L0_cond_ew2, L0_cond_eb2, L0_cond_sw1, L0_cond_sb1, L0_cond_sw2, L0_cond_sb2, L0_attn_Wq, L0_attn_Wk, L0_attn_Wv, L0_attn_betas, L0_attn_Wo, L0_cond2_w_q, L0_cond2_b_q, L0_cond2_w_k, L0_cond2_b_k, L0_cond2_w_v, L0_cond2_b_v, L0_cond2_w_o, L0_cond2_b_o, L0_cond2_w_f1, L0_cond2_b_f1, L0_cond2_w_f2, L0_cond2_b_f2, L0_cond2_w_ada, L0_cond2_b_ada, L0_ffn_wqkv, L0_ffn_q_scale, L0_ffn_k_scale, L0_ffn_wo, L0_ffn_ln_g, L0_ffn_ln_b, L0_ffn_w1, L0_ffn_b1, L0_ffn_w2, L0_ffn_b2):
    import jax
    import jax.numpy as jnp

    def _L0_cond_ref(context_c, time_cond, gate_w, gate_b, time_w, time_b, ew1, eb1, ew2, eb2, sw1, sb1, sw2, sb2):
        import jax, jax.numpy as jnp
        import numpy as np
        NUM_EXPERTS = 4
        TOP_K = 2
        B, L, D = context_c.shape
        E, K = (NUM_EXPERTS, TOP_K)
        L_head = L_wrist = L // 3
        head = context_c[:, :L_head]
        wrist = context_c[:, L_head:L_head + L_wrist]
        proprio = context_c[:, L_head + L_wrist:]
        full_agg = context_c.mean(axis=1)
        hp_agg = jnp.concatenate([head, proprio], axis=1).mean(axis=1)
        wp_agg = jnp.concatenate([wrist, proprio], axis=1).mean(axis=1)
        gate_in = jnp.concatenate([full_agg, hp_agg, wp_agg], axis=-1)
        gate_logits = gate_in @ gate_w + gate_b
        mod = jax.nn.silu(time_cond) @ time_w + time_b
        scale, shift = jnp.split(mod, 2, axis=-1)
        gate_logits = gate_logits * (1.0 + scale) + shift
        gate_scores = jax.nn.softmax(gate_logits, axis=-1)
        topk_w, topk_i = jax.lax.top_k(gate_scores, K)
        topk_w = topk_w / (topk_w.sum(axis=-1, keepdims=True) + 1e-08)
        onehot = (topk_i[..., None] == jnp.arange(E)[None, None, :]).astype(context_c.dtype)
        w_be = jnp.sum(topk_w[..., None] * onehot, axis=1)
        mask = np.ones((E, L), dtype=np.float32)
        mask[1, L_head:L_head + L_wrist] = 0.0
        mask[2, :L_head] = 0.0
        mask = jnp.asarray(mask)
        out = jnp.zeros_like(context_c)
        for e in range(E):
            h = jax.nn.gelu(context_c @ ew1[e] + eb1[e], approximate=True)
            y = h @ ew2[e] + eb2[e]
            out = out + w_be[:, e][:, None, None] * mask[e][None, :, None] * y
        shared = jax.nn.gelu(context_c @ sw1 + sb1, approximate=True) @ sw2 + sb2
        return out + shared

    def _L0_attn_ref(x, Wq, Wk, Wv, betas, Wo):
        import jax, jax.numpy as jnp
        import numpy as np
        B, S, D = (8, 1024, 256)
        H, DK, DV, L = (8, 64, 64, 64)
        b, s, d = x.shape
        n_seq = s // L
        xs = x.reshape(b, n_seq, L, d)

        def proj(W, dh):
            p = xs @ W
            return p.reshape(b, n_seq, L, H, dh).transpose(1, 0, 3, 2, 4)
        q = proj(Wq, DK)
        k = proj(Wk, DK)
        v = proj(Wv, DV)
        scale = 1.0 / np.sqrt(DK)
        gate = jax.nn.sigmoid(betas)
        mem0 = jnp.zeros((b, H, DK, DV), dtype=x.dtype)
        z0 = jnp.ones((b, H, DK, 1), dtype=x.dtype) / DK

        def step(carry, inp):
            mem, z = carry
            q_s, k_s, v_s = inp
            sq = jax.nn.elu(q_s) + 1.0
            att_mem = sq @ mem / (sq @ z)
            sk = jax.nn.elu(k_s) + 1.0
            mem = mem + jnp.einsum('bhlk,bhlv->bhkv', sk, v_s)
            z = z + sk.sum(axis=-2, keepdims=True).transpose(0, 1, 3, 2)
            att_dot = jax.nn.softmax(jnp.einsum('bhik,bhjk->bhij', q_s, k_s) * scale, axis=-1)
            att = att_dot @ v_s
            att = gate * att_mem + (1.0 - gate) * att
            return ((mem, z), att)
        _, outs = jax.lax.scan(step, (mem0, z0), (q, k, v))
        out = outs.transpose(1, 0, 3, 2, 4).reshape(b, s, H * DV)
        return out @ Wo

    def _L0_cond2_ref(x, t_emb, w_q, b_q, w_k, b_k, w_v, b_v, w_o, b_o, w_f1, b_f1, w_f2, b_f2, w_ada, b_ada):
        import math
        import jax, jax.numpy as jnp
        import numpy as np
        EPS = 1e-07
        MAX_TANH_ARG = 1.0 - 1e-05

        def _norm(x):
            return jnp.sqrt(jnp.sum(x * x, axis=-1, keepdims=True)).clip(EPS)

        def logmap0(x):
            n = _norm(x)
            return jnp.arctanh(jnp.clip(n, EPS, MAX_TANH_ARG)) * x / n

        def expmap0(v):
            n = _norm(v)
            return jnp.tanh(n) * v / n

        def mobius_add(x, y):
            x2 = jnp.sum(x * x, -1, keepdims=True)
            y2 = jnp.sum(y * y, -1, keepdims=True)
            xy = jnp.sum(x * y, -1, keepdims=True)
            num = (1 + 2 * xy + y2) * x + (1 - x2) * y
            den = (1 + 2 * xy + x2 * y2).clip(EPS)
            return num / den

        def plin(x, w, b):
            return expmap0(logmap0(x) @ w + b)

        def layer_norm(x, eps=1e-06):
            m = x.mean(-1, keepdims=True)
            v = ((x - m) ** 2).mean(-1, keepdims=True)
            return (x - m) / jnp.sqrt(v + eps)

        def _beta(a, b):
            return math.exp(math.lgamma(a) + math.lgamma(b) - math.lgamma(a + b))
        D, H, FF = (256, 16, 1024)
        HD = D // H
        BETA_N = _beta(D / 2, 0.5)
        BETA_H = _beta(HD / 2, 0.5)

        def _to_heads(p):
            B, S, _ = p.shape
            t = logmap0(p).reshape(B, S, H, HD) * (BETA_H / BETA_N)
            return expmap0(jnp.transpose(t, (0, 2, 1, 3)))

        def _from_heads(ph):
            B, _, S, _ = ph.shape
            t = logmap0(ph) * (BETA_N / BETA_H)
            t = jnp.transpose(t, (0, 2, 1, 3)).reshape(B, S, D)
            return expmap0(t)
        ada = t_emb @ w_ada + b_ada
        sh_msa, sc_msa, g_msa, sh_mlp, sc_mlp, g_mlp = jnp.split(ada, 6, axis=-1)
        residual = x
        xn = layer_norm(logmap0(x))
        xm = expmap0(xn * (1 + sc_msa) + sh_msa)
        q = _to_heads(plin(xm, w_q, b_q))
        k = _to_heads(plin(xm, w_k, b_k))
        v = _to_heads(plin(xm, w_v, b_v))
        qt, kt, vt = (logmap0(q), logmap0(k), logmap0(v))
        scores = jnp.einsum('bhqd,bhkd->bhqk', qt, kt) / math.sqrt(HD)
        attn = jax.nn.softmax(scores, axis=-1)
        out_h = expmap0(jnp.einsum('bhqk,bhkd->bhqd', attn, vt))
        attn_out = plin(_from_heads(out_h), w_o, b_o)
        attn_t = g_msa * logmap0(attn_out)
        x = mobius_add(residual, expmap0(attn_t))
        residual = x
        xn = layer_norm(logmap0(x))
        xm = expmap0(xn * (1 + sc_mlp) + sh_mlp)
        ff = plin(plin(xm, w_f1, b_f1), w_f2, b_f2)
        ff_t = g_mlp * logmap0(ff)
        return mobius_add(residual, expmap0(ff_t))

    def _L0_ffn_ref(x, wqkv, q_scale, k_scale, wo, ln_g, ln_b, w1, b1, w2, b2):
        import jax, jax.numpy as jnp
        import numpy as np
        DIM = 256
        DEPTH = 2
        HEADS = 8
        DIM_HEAD = 64
        WINDOW = 128
        INNER = HEADS * DIM_HEAD
        HID = int(DIM * 4 * 2 / 3)
        B, N = (2, 2048)
        QK_SCALE = 8.0

        def shift_token(t):
            t1, t2 = jnp.split(t, 2, axis=-1)
            t2 = jnp.pad(t2, ((0, 0), (1, 0), (0, 0)))[:, :-1]
            return jnp.concatenate([t1, t2], axis=-1)

        def l2norm(t):
            return t / jnp.clip(jnp.linalg.norm(t, axis=-1, keepdims=True), 1e-12)

        def rotate_half(x):
            x1, x2 = jnp.split(x, 2, axis=-1)
            return jnp.concatenate([-x2, x1], axis=-1)

        def rotary_xpos(q, k):
            n = q.shape[-2]
            half_idx = jnp.arange(0, DIM_HEAD, 2, dtype=jnp.float32)
            inv_freq = 1.0 / 10000.0 ** (half_idx / DIM_HEAD)
            t = jnp.arange(n, dtype=jnp.float32)
            freqs = t[:, None] * inv_freq[None, :]
            freqs = jnp.concatenate([freqs, freqs], axis=-1)
            base = (half_idx + 0.4 * DIM_HEAD) / (1.4 * DIM_HEAD)
            power = (t - n // 2) / float(WINDOW // 2)
            scale = base[None, :] ** power[:, None]
            scale = jnp.concatenate([scale, scale], axis=-1)
            cos, sin = (jnp.cos(freqs), jnp.sin(freqs))
            q = q * cos * scale + rotate_half(q) * sin * scale
            k = k * cos / scale + rotate_half(k) * sin / scale
            return (q, k)

        def local_attention(q, k, v):
            b, h, n, d = q.shape
            w = n // WINDOW
            bq = q.reshape(b, h, w, WINDOW, d) * QK_SCALE
            bk = k.reshape(b, h, w, WINDOW, d)
            bv = v.reshape(b, h, w, WINDOW, d)

            def look_around(t):
                p = jnp.pad(t, ((0, 0), (0, 0), (1, 0), (0, 0), (0, 0)))
                return jnp.concatenate([p[:, :, :w], p[:, :, 1:]], axis=3)
            bk, bv = (look_around(bk), look_around(bv))
            bt = jnp.arange(n).reshape(w, WINDOW)
            btp = jnp.pad(bt, ((1, 0), (0, 0)), constant_values=-1)
            btk = jnp.concatenate([btp[:w], btp[1:]], axis=1)
            sim = jnp.einsum('bhwid,bhwjd->bhwij', bq, bk)
            i = bt[:, :, None]
            j = btk[:, None, :]
            mask = (i < j) | (i > j + WINDOW) | (j == -1)
            sim = jnp.where(mask, -jnp.finfo(sim.dtype).max, sim)
            attn = jax.nn.softmax(sim, axis=-1)
            out = jnp.einsum('bhwij,bhwjd->bhwid', attn, bv)
            return out.reshape(b, h, n, d)

        def _layer(x, wqkv, qs, ksc, wo, lg, lb, w1, b1, w2, b2):
            b, n, _ = x.shape
            h = shift_token(x)
            qkv = h @ wqkv
            q, k, v = jnp.split(qkv, 3, axis=-1)
            to_heads = lambda t: t.reshape(b, n, HEADS, DIM_HEAD).transpose(0, 2, 1, 3)
            q, k, v = (to_heads(q), to_heads(k), to_heads(v))
            q = l2norm(q) * qs
            k = l2norm(k) * ksc
            q, k = rotary_xpos(q, k)
            o = local_attention(q, k, v)
            o = o.transpose(0, 2, 1, 3).reshape(b, n, INNER)
            x = x + o @ wo
            h = shift_token(x)
            mu = h.mean(-1, keepdims=True)
            var = h.var(-1, keepdims=True)
            h = (h - mu) / jnp.sqrt(var + 1e-05) * lg + lb
            h = h @ w1 + b1
            a, g = jnp.split(h, 2, axis=-1)
            h = a * jax.nn.gelu(g, approximate=False)
            x = x + h @ w2 + b2
            return x
        for l in range(DEPTH):
            x = _layer(x, wqkv[l], q_scale[l], k_scale[l], wo[l], ln_g[l], ln_b[l], w1[l], b1[l], w2[l], b2[l])
        return x
    x = x + _L0_attn_ref(_L0_cond_ref(x, cond_1024, L0_cond_gate_w, L0_cond_gate_b, L0_cond_time_w, L0_cond_time_b, L0_cond_ew1, L0_cond_eb1, L0_cond_ew2, L0_cond_eb2, L0_cond_sw1, L0_cond_sb1, L0_cond_sw2, L0_cond_sb2), L0_attn_Wq, L0_attn_Wk, L0_attn_Wv, L0_attn_betas, L0_attn_Wo)
    x = x + _L0_ffn_ref(_L0_cond2_ref(x, cond_1024[:, None, :], L0_cond2_w_q, L0_cond2_b_q, L0_cond2_w_k, L0_cond2_b_k, L0_cond2_w_v, L0_cond2_b_v, L0_cond2_w_o, L0_cond2_b_o, L0_cond2_w_f1, L0_cond2_b_f1, L0_cond2_w_f2, L0_cond2_b_f2, L0_cond2_w_ada, L0_cond2_b_ada), L0_ffn_wqkv, L0_ffn_q_scale, L0_ffn_k_scale, L0_ffn_wo, L0_ffn_ln_g, L0_ffn_ln_b, L0_ffn_w1, L0_ffn_b1, L0_ffn_w2, L0_ffn_b2)
    return x

_drawn_inputs = setup_inputs


def setup_inputs(seed=0):
    import zlib

    import numpy as np

    out = dict(_drawn_inputs(seed))
    spreads = {'L0_cond_gate_b': (0.0, 0.421),
     'L0_cond_time_b': (0.0, 0.1),
     'L0_cond_eb1': (0.0, 0.409),
     'L0_cond_eb2': (0.0, 0.1),
     'L0_cond_sb1': (0.0, 0.1),
     'L0_cond_sb2': (0.0, 0.1),
     'L0_cond2_b_q': (0.0, 0.8),
     'L0_cond2_b_k': (0.0, 0.8),
     'L0_cond2_b_v': (0.0, 0.307),
     'L0_cond2_b_o': (0.0, 0.1),
     'L0_cond2_b_f1': (0.0, 0.34),
     'L0_cond2_b_f2': (0.0, 0.1),
     'L0_cond2_b_ada': (0.0, 0.273),
     'L0_ffn_q_scale': (1.0, 0.6),
     'L0_ffn_k_scale': (1.0, 0.6),
     'L0_ffn_ln_g': (1.0, 0.6),
     'L0_ffn_ln_b': (0.0, 0.8),
     'L0_ffn_b1': (0.0, 0.409),
     'L0_ffn_b2': (0.0, 0.1)}
    factors = {'L0_cond_gate_w': 8.0,
     'L0_cond_ew1': 8.0,
     'L0_cond_sw1': 6.613,
     'L0_attn_Wq': 8.0,
     'L0_attn_Wk': 8.0,
     'L0_attn_betas': 5.336,
     'L0_cond2_w_q': 8.0,
     'L0_cond2_w_k': 8.0,
     'L0_cond2_w_v': 6.01}
    for name, (base, spread) in spreads.items():
        noise = np.random.default_rng([zlib.crc32(name.encode()), seed]).standard_normal(out[name].shape)
        drawn = base * np.exp(spread * noise) if base else spread * noise
        out[name] = jnp.asarray(drawn.astype(out[name].dtype))
    for name, factor in factors.items():
        out[name] = (out[name] * factor).astype(out[name].dtype)
    return out
```

```python
import math
from contextlib import ExitStack

import numpy as np

import concourse.bass as bass
from concourse import mybir

F32 = mybir.dt.float32
I32 = mybir.dt.int32
BF16 = mybir.dt.bfloat16
ALU = mybir.AluOpType
ACT = mybir.ActivationFunctionType
AX = mybir.AxisListType

P = 128
B = 8
L = 512
D = 256
KD = D // P
NT = L // P


class Chain:

    def __init__(self, eng, sem, base=0):
        self.eng, self.sem, self.base, self.n = eng, sem, base, 0

    def mark(self, ins):
        ins.then_inc(self.sem, 1)
        self.n += 1
        return self.n

    def wait(self, n):
        self.eng.wait_ge(self.sem, self.base + n)

    def link(self, ins):
        self.wait(self.mark(ins))


def moe_attention(nc, io, x1):
    E, H1 = 4, 1024
    M1 = H1 // P
    LH = L // 3
    SEGS = [(0, LH), (LH, 2 * LH), (2 * LH, L)]
    NH, DH = 8, 64
    SEG = 64
    NSEG = L // SEG
    NC = NH * DH // P
    J = 3 * M1
    VA = DH + 1

    with ExitStack() as ctx:
        def sb(name, shape, dt=F32):
            return ctx.enter_context(nc.sbuf_tensor(name, shape, dt))

        def sem(name):
            return ctx.enter_context(nc.semaphore(name))

        sw1 = sb("sw1", [P, KD, H1])
        sw2 = sb("sw2", [P, M1, D])
        wq = sb("wq", [P, KD, NC * P])
        wk = sb("wk", [P, KD, NC * P])
        wv = sb("wv", [P, KD, NC * P])
        wo = sb("wo", [P, NC, D])
        sb1 = sb("sb1", [P, M1])
        eb2 = sb("eb2", [E + 1, D])
        mask5 = sb("mask5", [E + 1, L])
        ident = sb("ident", [P, P])
        gate = sb("gate", [P, NC * P])
        gate1 = sb("gate1", [P, NC * P])
        rw1 = sb("rw1", [P, 2, KD, H1])
        rw2 = sb("rw2", [P, 2, M1, D])
        rb1 = sb("rb1", [P, 2, M1])
        condT = sb("condT", [P, KD, B])
        gwt = sb("gwt", [P, 3 * KD, E])
        gbt = sb("gbt", [1, E])
        twt = sb("twt", [P, KD, 2 * E])
        tbt = sb("tbt", [1, 2 * E])
        ones = sb("ones", [E, P])
        sums = sb("sums", [P, 3, KD, B])
        gin = sb("gin", [P, 3, KD, B])
        sil = sb("sil", [P, 2, KD, B])
        lg = sb("lg", [B, 16, E])
        col = sb("col", [B, 16])
        cnt = sb("cnt", [B, 2, E])
        junk = sb("junk", [B, 2, E])
        ohw = sb("ohw", [B, 2, E])
        idx = sb("idx", [B, 2], I32)
        idxrow = sb("idxrow", [1, 2 * B], I32)
        slotw = sb("slotw", [E, 2, B])
        w5 = sb("w5", [E + 1, B])
        wcol = sb("wcol", [E, 2, P])
        wm5 = sb("wm5", [E + 1, L])
        xT = sb("xT", [P, KD, L])
        hid = sb("hid", [P, 3, L])
        cT = sb("cT", [P, KD, L])
        qT = sb("qT", [P, NC, L])
        sqT = sb("sqT", [P, NC, L])
        kT = sb("kT", [P, NC, L])
        ktok = sb("ktok", [P, NT, NC * P])
        sk = sb("sk", [P, NT, NC * P])
        vtok = sb("vtok", [P, NT, NH, VA])
        neg = sb("neg", [P, 2, L])
        mem = sb("mem", [P, NSEG, NC, VA])
        xres = sb("xres", [P, NT, D])
        shifted = sb("shifted", [P, 2, 4, SEG])
        prob = sb("prob", [P, NH + 1, SEG])
        rs9 = sb("rs9", [P, NH + 1])
        pT = sb("pT", [P, NH, P])
        att = sb("att", [P, 2, NC * P])
        attm = sb("attm", [P, NC * P])
        attT = sb("attT", [P, NC, P])
        mx = sb("mx", [P, 2, 4])
        rsum = sb("rsum", [P, 2, 4])
        rden = sb("rden", [P, 2, 4])
        x1t = sb("x1t", [P, 2, D])

        ps = ctx.enter_context(nc.psum_tensor("ps", [P, 8, 512], F32))
        s_ps = ps[:, 2:4, 0:256].rearrange("p a (c k) -> p a c k", k=SEG)
        pT_ps = ps[:, 6:8, :].rearrange("p a (h q) -> p (a h) q", q=P)
        pv_ps = ps[:, 4, :]
        am_ps = [ps[:, 5, 0:NC * VA].rearrange("p (c v) -> p c v", v=VA),
                 ps[:, 1, 0:NC * VA].rearrange("p (c v) -> p c v", v=VA)]
        aT_ps = ps[:, 0, :].rearrange("p (k q) -> p k q", q=P)
        wo_ps = ps[:, 0, 0:D]

        ld_route = sem("ld_route")
        ld_w = sem("ld_w")
        ld_xs = sem("ld_xs")
        ld_x = sem("ld_x")
        ld_res = sem("ld_res")
        ld_r = [sem("ld_r0"), sem("ld_r1")]
        st_idx = sem("st_idx")
        st_x1 = [sem("st_x1a"), sem("st_x1b")]
        summed = sem("summed")
        v_c = sem("v_c")
        v_l = sem("v_l")
        a_pre = sem("a_pre")
        gin_ok = sem("gin_ok")
        sil_ok = sem("sil_ok")
        lg_ps = sem("lg_ps")
        lg_ex = sem("lg_ex")
        idx_ok = sem("idx_ok")
        ohw_ok = sem("ohw_ok")
        ohwT = sem("ohwT")
        slot_ok = sem("slot_ok")
        wcol_ok = sem("wcol_ok")
        wmb_ok = sem("wmb_ok")
        h_mm = sem("h_mm")
        h_act = sem("h_act")
        h_w = sem("h_w")
        o_mm = sem("o_mm")
        c_act = sem("c_act")
        c_dve = sem("c_dve")
        pp_mm = sem("pp_mm")
        pp_ev = sem("pp_ev")
        mn_ok = sem("mn_ok")
        ex_ok = sem("ex_ok")
        fm_ok = sem("fm_ok")
        u_mm = sem("u_mm")
        mem_ok = sem("mem_ok")
        s_mm = sem("s_mm")
        s_sub = sem("s_sub")
        sum_ok = sem("sum_ok")
        p_ok = sem("p_ok")
        pT_mm = sem("pT_mm")
        pT_a = sem("pT_a")
        pT_v = sem("pT_v")
        am_mm = sem("am_mm")
        pv_mm = sem("pv_mm")
        att_ok = sem("att_ok")
        aT_mm = sem("aT_mm")
        aT_ok = sem("aT_ok")
        wo_mm = sem("wo_mm")
        x1_ok = sem("x1_ok")

        block = ctx.enter_context(nc.Block())

        @block.sync
        def _(sp):
            for dst, name in ((condT, "condT"), (gwt, "gate_w"), (gbt, "gate_b"), (twt, "time_w"),
                              (tbt, "time_b"), (ident, "ident")):
                sp.dma_start(dst[:], io[name]).then_inc(ld_route, 16)
            with sp.Fori(0, B) as b:
                sp.wait_ge(summed, b)
                sp.dma_start(xT[:], io["xT"][bass.ds(b, 1)].rearrange("a p c l -> p (a c) l")).then_inc(ld_xs, 16)
            for dst, name in ((sw1, "sw1"), (sw2, "sw2"), (wq, "wq"), (wk, "wk"), (wv, "wv"), (wo, "wo"),
                              (sb1, "sb1"), (eb2, "eb2"), (mask5, "mask5"), (gate, "betas")):
                sp.dma_start(dst[:], io[name]).then_inc(ld_w, 16)
            sp.wait_ge(idx_ok, 1)
            sp.dma_start(idxrow[:], idx[:]).then_inc(st_idx, 16)
            sp.wait_ge(st_idx, 16)
            with sp.Fori(0, B) as b:
                for r in range(2):
                    e = sp.value_load(idxrow[0:1, bass.ds(b * 2 + r, 1)], min_val=0, max_val=E - 1)
                    if r == 0:
                        sp.wait_ge(o_mm, b * J)
                    sp.dma_start(rw1[:, r], io["ew1"][bass.ds(e, 1)].rearrange("a p k n -> p (a k) n")).then_inc(ld_r[r], 16)
                    sp.dma_start(rw2[:, r], io["ew2"][bass.ds(e, 1)].rearrange("a p k n -> p (a k) n")).then_inc(ld_r[r], 16)
                    sp.dma_start(rb1[:, r], io["eb1"][bass.ds(e, 1)].rearrange("a p m -> p (a m)")).then_inc(ld_r[r], 16)
                sp.dma_start(xT[:], io["xT"][bass.ds(b, 1)].rearrange("a p c l -> p (a c) l")).then_inc(ld_x, 16)
                sp.wait_ge(x1_ok, b * NT)
                sp.dma_start(xres[:], io["x"][bass.ds(b, 1)].rearrange("a (t p) d -> p (a t) d", p=P)).then_inc(ld_res, 16)
                for t in range(NT):
                    sp.wait_ge(x1_ok, b * NT + t + 1)
                    sp.dma_start(x1[bass.ds(b, 1)].rearrange("a (t p) d -> t p (a d)", p=P)[t], x1t[:, t % 2]).then_inc(st_x1[t % 2], 16)
            for s in st_x1:
                sp.wait_ge(s, 16 * B * NT // 2)

        @block.gpsimd
        def _(pool):
            pass

        @block.scalar
        def _(act):
            a = nc.scalar
            act.wait_ge(ld_route, 6 * 16)
            a.activation(sil[:, 0], condT[:], ACT.Exp, scale=-1.0).then_inc(a_pre, 1)
            act.wait_ge(lg_ex, 1)
            a.activation(lg[:, 5, :], lg[:, 4, :], ACT.Exp).then_inc(a_pre, 1)
            act.wait_ge(ld_w, 10 * 16)
            a.activation(gate1[:], gate[:], ACT.Exp, scale=-1.0).then_inc(a_pre, 1)
            with act.Fori(0, B) as b:
                for j in range(J):
                    act.wait_ge(h_mm, b * J + j + 1)
                    if j == 0:
                        act.wait_ge(ld_r[0], b * 48 + 48)
                    if j == M1:
                        act.wait_ge(ld_r[1], b * 48 + 48)
                    if j >= 3:
                        act.wait_ge(o_mm, b * J + j - 2)
                    bias = rb1[:, j // M1, j % M1:j % M1 + 1] if j < 2 * M1 else sb1[:, j % M1:j % M1 + 1]
                    a.activation(hid[:, j % 3], ps[:, j % 2], ACT.Gelu_apprx_tanh, bias=bias).then_inc(h_act, 1)
                act.wait_ge(o_mm, b * J + J)
                a.activation(cT[:, 0], ps[:, 2], ACT.Copy).then_inc(c_act, 1)

                n_ex = 0

                def feature_exp():
                    nonlocal n_ex
                    act.wait_ge(mn_ok, b * 8 + n_ex + 1)
                    ins = a.activation(neg[:, n_ex % 2], neg[:, n_ex % 2], ACT.Exp)
                    ins.then_inc(ex_ok, 1)
                    n_ex += 1

                for n in range(16):
                    act.wait_ge(pp_mm, b * 16 + n + 1)
                    if n < 4:
                        src, dst = ps[:, n % 2], qT[:, n]
                    elif n < 12 and n % 2 == 0:
                        src, dst = ps[:, n % 2], ktok[:, (n - 4) // 2]
                    elif n < 12:
                        src = ps[:, n % 2].rearrange("p (h v) -> p h v", v=DH)
                        dst = vtok[:, (n - 4) // 2, :, 0:DH]
                    else:
                        src = ps[:, n % 2].rearrange("p (c q) -> p c q", q=P)
                        dst = kT[:, :, (n - 12) * P:(n - 11) * P]
                    a.activation(dst, src, ACT.Copy).then_inc(pp_ev, 1)
                    if n in (1, 2, 3, 4, 6, 8, 10, 12):
                        feature_exp()
                for t in range(NT):
                    act.wait_ge(s_sub, b * NT + t + 1)
                    if t:
                        act.wait_ge(sum_ok, b * NT + t)
                    for s in range(2):
                        r = slice(64 * s, 64 * s + 64)
                        ins = a.activation(prob[r, s:s + NH], shifted[r].rearrange("p a c k -> p (a c) k"), ACT.Exp, scale=DH ** -0.5)
                    ins.then_inc(p_ok, 1)
                    act.wait_ge(pT_mm, b * NT + t + 1)
                    if t:
                        act.wait_ge(pv_mm, b * NT + t)
                    a.activation(pT[0:64, :, 0:64], pT_ps[0:64, :, 0:64], ACT.Copy).then_inc(pT_a, 1)
                    if t >= 1:
                        act.wait_ge(aT_mm, b * NT + t)
                        if t >= 2:
                            act.wait_ge(wo_mm, b * NT + t - 1)
                        a.activation(attT[:], aT_ps, ACT.Copy).then_inc(aT_ok, 1)
                act.wait_ge(aT_mm, b * NT + NT)
                act.wait_ge(wo_mm, b * NT + NT - 1)
                a.activation(attT[:], aT_ps, ACT.Copy).then_inc(aT_ok, 1)

        @block.vector
        def _(dve):
            v = nc.vector
            ch = Chain(dve, v_c)
            v.memset(ones[:], 1.0).then_inc(slot_ok, 1)
            ch.mark(v.memset(mem[:, 0], 0.0))
            ch.mark(v.memset(pT[:], 0.0))
            ch.mark(v.memset(prob[:], 0.0))
            ch.mark(v.memset(vtok[:], 1.0))
            ch.link(v.memset(w5[:], 1.0))
            ch.link(v.memset(mem[:, 0, :, DH:VA], 1.0 / DH))
            with dve.Fori(0, B) as b:
                dve.wait_ge(ld_xs, b * 16 + 16)
                for s, (lo, hi) in enumerate(SEGS):
                    ins = v.tensor_reduce(sums[:, s, :, bass.ds(b, 1)].rearrange("p c a -> p (c a)"), xT[:, :, lo:hi], AX.X, ALU.add)
                ins.then_inc(summed, 1)
            dve.wait_ge(summed, B)
            ch.link(v.tensor_tensor(gin[:, 1], sums[:, 0], sums[:, 2], ALU.add))
            ch.link(v.tensor_tensor(gin[:, 2], sums[:, 1], sums[:, 2], ALU.add))
            ch.link(v.tensor_tensor(gin[:, 0], gin[:, 1], sums[:, 1], ALU.add))
            ch.link(v.tensor_scalar(gin[:, 0], gin[:, 0], 1.0 / L, None, ALU.mult))
            ch.link(v.tensor_scalar(gin[:, 1:3], gin[:, 1:3], 1.0 / (L - LH), None, ALU.mult))
            dve.wait_ge(a_pre, 1)
            ch.link(v.tensor_scalar(sil[:, 0], sil[:, 0], 1.0, None, ALU.add))
            ch.link(v.reciprocal(sil[:, 0], sil[:, 0]))
            v.tensor_tensor(sil[:, 1], sil[:, 0], condT[:], ALU.mult).then_inc(gin_ok, 1)
            dve.wait_ge(lg_ps, 1)
            ch.link(v.tensor_scalar(lg[:, 0], ps[0:B, 4, 8:8 + E], 1.0, None, ALU.add))
            ch.link(v.tensor_tensor(lg[:, 1], lg[:, 0], ps[0:B, 4, 0:E], ALU.mult))
            ch.link(v.tensor_tensor(lg[:, 2], lg[:, 1], ps[0:B, 4, 8 + E:8 + 2 * E], ALU.add))
            ch.link(v.tensor_reduce(col[:, 0:1], lg[:, 2], AX.X, ALU.max))
            v.tensor_scalar(lg[:, 4], lg[:, 2], col[:, 0:1], None, ALU.subtract).then_inc(lg_ex, 1)
            dve.wait_ge(a_pre, 2)
            ch.link(v.tensor_reduce(col[:, 1:2], lg[:, 5], AX.X, ALU.add))
            ch.link(v.reciprocal(col[:, 2:3], col[:, 1:2]))
            sc = lg[:, 6]
            ch.link(v.tensor_scalar(sc, lg[:, 5], col[:, 2:3], None, ALU.mult))
            for e in range(E):
                ch.link(v.tensor_scalar(lg[:, 7], sc, lg[:, 6, e:e + 1], None, ALU.is_gt))
                if e:
                    ch.link(v.tensor_scalar(lg[:, 7, 0:e], lg[:, 6, 0:e], lg[:, 6, e:e + 1], None, ALU.is_ge))
                ch.link(v.tensor_reduce(lg[:, 8, e:e + 1], lg[:, 7], AX.X, ALU.add))
            ch.link(v.memset(lg[:, 9, 0:1], 0.0))
            for e in range(1, E):
                ch.link(v.memset(lg[:, 9, e:e + 1], float(e)))
            for r in range(2):
                ch.link(v.tensor_scalar(cnt[:, r], lg[:, 8], float(r), None, ALU.is_equal))
                ch.link(v.tensor_tensor(junk[:, r], cnt[:, r], sc, ALU.mult))
                ch.link(v.tensor_reduce(col[:, 4 + r:5 + r], junk[:, r], AX.X, ALU.add))
                ch.link(v.tensor_tensor(lg[:, 10], cnt[:, r], lg[:, 9], ALU.mult))
                ch.link(v.tensor_reduce(col[:, 6 + r:7 + r], lg[:, 10], AX.X, ALU.add))
            v.tensor_copy(idx[:], col[:, 6:8]).then_inc(idx_ok, 1)
            ch.link(v.tensor_tensor(col[:, 8:9], col[:, 4:5], col[:, 5:6], ALU.add))
            ch.link(v.tensor_scalar(col[:, 8:9], col[:, 8:9], 1e-8, None, ALU.add))
            ch.link(v.reciprocal(col[:, 9:10], col[:, 8:9]))
            v.tensor_scalar(ohw[:], junk[:], col[:, 9:10], None, ALU.mult).then_inc(ohw_ok, 1)
            dve.wait_ge(ohwT, 1)
            ch.link(v.tensor_copy(slotw[:], ps[0:E, 5, 0:2 * B].rearrange("p (r b) -> p r b", r=2)))
            ch.link(v.tensor_tensor(w5[0:E], slotw[:, 0], slotw[:, 1], ALU.add))
            dve.wait_ge(a_pre, 3)
            ch.link(v.tensor_scalar(gate[:], gate1[:], 1.0, None, ALU.add))
            ch.link(v.reciprocal(gate[:], gate[:]))
            ch.link(v.tensor_scalar(gate1[:], gate[:], -1.0, 1.0, ALU.mult, ALU.add))

            LINKS = 5 * NT - 0
            with dve.Fori(0, B) as b:
                lc = Chain(dve, v_l, b * LINKS)
                dve.wait_ge(o_mm, b * J)
                for r in range(2):
                    v.tensor_scalar(wcol[:, r], ones[:], slotw[:, r, bass.ds(b, 1)], None, ALU.mult)
                v.tensor_scalar(wm5[:], mask5[:], w5[:, bass.ds(b, 1)], None, ALU.mult).then_inc(wcol_ok, 1)
                dve.wait_ge(wmb_ok, b + 1)
                for j in range(2 * M1):
                    dve.wait_ge(h_act, b * J + j + 1)
                    v.tensor_tensor(hid[:, j % 3], hid[:, j % 3], ps[:, 4 + j // M1], ALU.mult).then_inc(h_w, 1)
                dve.wait_ge(o_mm, b * J + J)
                v.tensor_copy(cT[:, 1], ps[:, 3]).then_inc(c_dve, 1)
                feats = [(qT[:, c], sqT[:, c], c + 1) for c in range(NC)] + \
                        [(ktok[:, t], sk[:, t], 5 + 2 * t) for t in range(NT)]

                def low(n):
                    dve.wait_ge(pp_ev, b * 16 + feats[n][2])
                    v.tensor_scalar(neg[:, n % 2], feats[n][0], 0.0, None, ALU.min).then_inc(mn_ok, 1)

                low(0)
                for n in range(8):
                    if n + 1 < 8:
                        if n:
                            dve.wait_ge(fm_ok, b * 8 + n)
                        low(n + 1)
                    dve.wait_ge(ex_ok, b * 8 + n + 1)
                    v.scalar_tensor_tensor(out=feats[n][1], in0=feats[n][0], scalar=0.0, in1=neg[:, n % 2],
                                           op0=ALU.max, op1=ALU.add).then_inc(fm_ok, 1)
                for n in range(NSEG - 1):
                    dve.wait_ge(u_mm, b * 7 + n + 1)
                    if n:
                        dve.wait_ge(mem_ok, b * 7 + n)
                    v.tensor_tensor(mem[:, n + 1], mem[:, n], ps[:, 4 + n % 2, 0:NC * VA].rearrange("p (c v) -> p c v", v=VA),
                                    ALU.add).then_inc(mem_ok, 1)

                def finish(t):
                    dve.wait_ge(wo_mm, b * NT + t + 1)
                    dve.wait_ge(st_x1[t % 2], b * 32 + 16 * (t // 2))
                    v.tensor_tensor(x1t[:, t % 2], xres[:, t], wo_ps, ALU.add).then_inc(x1_ok, 1)

                dve.wait_ge(ld_res, b * 16 + 16)
                for t in range(NT):
                    dve.wait_ge(s_mm, b * NT + t + 1)
                    lc.link(v.tensor_reduce(mx[:], s_ps, AX.X, ALU.max))
                    v.tensor_tensor(shifted[:], s_ps, mx[:].unsqueeze(3).broadcast_to([P, 2, 4, SEG]), ALU.subtract).then_inc(s_sub, 1)
                    if t >= 2:
                        finish(t - 2)
                    dve.wait_ge(p_ok, b * NT + t + 1)
                    v.tensor_reduce(rs9[:], prob[:], AX.X, ALU.add).then_inc(sum_ok, 1)
                    dve.wait_ge(sum_ok, b * NT + t + 1)
                    for s in range(2):
                        r = slice(64 * s, 64 * s + 64)
                        v.reciprocal(rsum[r], rs9[r, s:s + NH].rearrange("p (a c) -> p a c", a=2))
                    dve.wait_ge(pT_mm, b * NT + t + 1)
                    if t:
                        dve.wait_ge(pv_mm, b * NT + t)
                    v.tensor_copy(pT[64:128, :, 64:128], pT_ps[64:128, :, 64:128]).then_inc(pT_v, 1)
                    dve.wait_ge(am_mm, b * NT + t + 1)
                    v.reciprocal(rden[:, 0], am_ps[0][:, :, DH])
                    lc.link(v.reciprocal(rden[:, 1], am_ps[1][:, :, DH]))
                    am = attm[:].rearrange("p (a c v) -> p a c v", a=2, v=DH)
                    for par in range(2):
                        ins = v.tensor_tensor(am[:, par], am_ps[par][:, :, 0:DH],
                                              rden[:, par].unsqueeze(2).broadcast_to([P, 4, DH]), ALU.mult)
                    lc.link(ins)
                    lc.link(v.tensor_tensor(attm[:], attm[:], gate[:], ALU.mult))
                    dve.wait_ge(pv_mm, b * NT + t + 1)
                    if t >= 2:
                        dve.wait_ge(aT_mm, b * NT + t - 1)
                    o = att[:, t % 2].rearrange("p (h v) -> p h v", v=DH)
                    lc.link(v.tensor_tensor(o, pv_ps.rearrange("p (h v) -> p h v", v=DH),
                                            rsum[:].rearrange("p a c -> p (a c)").unsqueeze(2).broadcast_to([P, NH, DH]), ALU.mult))
                    v.tensor_tensor(att[:, t % 2], att[:, t % 2], gate1[:], ALU.mult).then_inc(att_ok, 1)
                    dve.wait_ge(att_ok, b * 2 * NT + 2 * t + 1)
                    v.tensor_tensor(att[:, t % 2], att[:, t % 2], attm[:], ALU.add).then_inc(att_ok, 1)
                finish(NT - 2)
                finish(NT - 1)
                assert lc.n == LINKS, lc.n

        @block.tensor
        def _(pe):
            te = nc.tensor
            pe.wait_ge(ld_route, 6 * 16)
            pe.wait_ge(gin_ok, 1)
            pe.wait_ge(slot_ok, 1)
            g = gin[:].rearrange("p s c b -> p (s c) b")
            for k in range(3 * KD):
                te.matmul(ps[0:B, 4, 0:E], g[:, k], gwt[:, k], start=(k == 0), stop=False)
            te.matmul(ps[0:B, 4, 0:E], ones[0:1, 0:B], gbt[:], start=False, stop=True)
            for k in range(KD):
                te.matmul(ps[0:B, 4, 8:8 + 2 * E], sil[:, 1, k], twt[:, k], start=(k == 0), stop=False)
            te.matmul(ps[0:B, 4, 8:8 + 2 * E], ones[0:1, 0:B], tbt[:], start=False, stop=True).then_inc(lg_ps, 1)
            pe.wait_ge(ohw_ok, 1)
            for r in range(2):
                ins = te.transpose(ps[0:E, 5, r * B:(r + 1) * B], ohw[:, r], ident[0:B, 0:B])
            ins.then_inc(ohwT, 1)
            pe.wait_ge(ld_w, 10 * 16)

            with pe.Fori(0, B) as b:
                pe.wait_ge(wcol_ok, b + 1)
                pe.wait_ge(x1_ok, b * NT)
                pe.wait_ge(aT_ok, b * NT)
                for r in range(2):
                    ins = te.matmul(ps[:, 4 + r], wcol[:, r], mask5[0:E], start=True, stop=True)
                ins.then_inc(wmb_ok, 1)
                for c in range(KD):
                    te.matmul(ps[:, 2 + c], eb2[:, c * P:(c + 1) * P], wm5[:], start=True, stop=False)
                pe.wait_ge(ld_x, b * 16 + 16)

                def second(j):
                    if j < 2 * M1:
                        pe.wait_ge(h_w, b * 2 * M1 + j + 1)
                    else:
                        pe.wait_ge(h_act, b * J + j + 1)
                    w2 = rw2[:, j // M1] if j < 2 * M1 else sw2
                    for c in range(KD):
                        ins = te.matmul(ps[:, 2 + c], w2[:, j % M1, c * P:(c + 1) * P], hid[:, j % 3],
                                        start=False, stop=(j == J - 1))
                    ins.then_inc(o_mm, 1)

                for j in range(J):
                    if j < 2 * M1 and j % M1 == 0:
                        pe.wait_ge(ld_r[j // M1], b * 48 + 48)
                    if j >= 2:
                        pe.wait_ge(h_act, b * J + j - 1)
                    w1 = rw1[:, j // M1] if j < 2 * M1 else sw1
                    for k in range(KD):
                        ins = te.matmul(ps[:, j % 2], w1[:, k, j % M1 * P:(j % M1 + 1) * P], xT[:, k],
                                        start=(k == 0), stop=(k == KD - 1))
                    ins.then_inc(h_mm, 1)
                    if j:
                        second(j - 1)
                second(J - 1)

                pe.wait_ge(c_act, b + 1)
                pe.wait_ge(c_dve, b + 1)
                for n in range(16):
                    if n >= 2:
                        pe.wait_ge(pp_ev, b * 16 + n - 1)
                    if n < 4:
                        for k in range(KD):
                            ins = te.matmul(ps[:, n % 2], wq[:, k, n * P:(n + 1) * P], cT[:, k],
                                            start=(k == 0), stop=(k == KD - 1))
                    elif n < 12:
                        t = (n - 4) // 2
                        w = wv if n % 2 else wk
                        for k in range(KD):
                            ins = te.matmul(ps[:, n % 2], cT[:, k, t * P:(t + 1) * P], w[:, k],
                                            start=(k == 0), stop=(k == KD - 1))
                    else:
                        t = n - 12
                        for c in range(NC):
                            ins = te.transpose(ps[:, n % 2, c * P:(c + 1) * P], ktok[:, t, c * P:(c + 1) * P], ident[:])
                    ins.then_inc(pp_mm, 1)

                def scores(t):
                    for s in range(2):
                        for h in range(NH):
                            r, c = 64 * (h % 2), h // 2
                            q = slice(t * P + s * SEG, t * P + (s + 1) * SEG)
                            rows, qs = slice(64 * s, 64 * s + 64), q
                            if s == 0 and h == 0:
                                rows, qs = slice(0, P), slice(t * P, (t + 1) * P)
                            ins = te.matmul(s_ps[rows, h % 2, c], qT[r:r + 64, c, qs], kT[r:r + 64, c, q],
                                            start=True, stop=True)
                    ins.then_inc(s_mm, 1)

                def memory_read(t):
                    for s in range(2):
                        for h in range(NH):
                            r, c = 64 * (h % 2), h // 2
                            q = slice(t * P + s * SEG, t * P + (s + 1) * SEG)
                            rows, qs = slice(64 * s, 64 * s + 64), q
                            if s == 0 and h == 0:
                                rows, qs = slice(0, P), slice(t * P, (t + 1) * P)
                            ins = te.matmul(am_ps[h % 2][rows, c], sqT[r:r + 64, c, qs],
                                            mem[r:r + 64, 2 * t + s, c], start=True, stop=True)
                    ins.then_inc(am_mm, 1)

                def project(t):
                    pe.wait_ge(att_ok, b * 2 * NT + 2 * t + 2)
                    if t:
                        pe.wait_ge(x1_ok, b * NT + t)
                    for k in range(NC):
                        ins = te.transpose(aT_ps[:, k], att[:, t % 2, k * P:(k + 1) * P], ident[:])
                    ins.then_inc(aT_mm, 1)
                    pe.wait_ge(aT_ok, b * NT + t + 1)
                    for k in range(NC):
                        ins = te.matmul(wo_ps, attT[:, k], wo[:, k], start=(k == 0), stop=(k == NC - 1))
                    ins.then_inc(wo_mm, 1)

                pe.wait_ge(pp_ev, b * 16 + 16)
                scores(0)
                for n in range(NSEG - 1):
                    s, t = n % 2, n // 2
                    if n % 2 == 0:
                        pe.wait_ge(fm_ok, b * 8 + 5 + t)
                    if n >= 2:
                        pe.wait_ge(mem_ok, b * 7 + n - 1)
                    for h in range(NH):
                        r, c = 64 * (h % 2), h // 2
                        m = P if h == 0 else DH
                        ins = te.matmul(ps[r:r + m, 4 + n % 2, c * VA:(c + 1) * VA],
                                        sk[64 * s:64 * s + 64, t, h * DH:h * DH + m],
                                        vtok[64 * s:64 * s + 64, t, h], start=True, stop=True)
                    ins.then_inc(u_mm, 1)
                pe.wait_ge(mem_ok, b * 7 + 7)
                memory_read(0)
                for t in range(NT):
                    pe.wait_ge(p_ok, b * NT + t + 1)
                    if t:
                        pe.wait_ge(pT_a, b * NT + t)
                        pe.wait_ge(pT_v, b * NT + t)
                    for o in range(NH):
                        ins = te.transpose(pT_ps[:, o], prob[:, o:o + 2].rearrange("p o k -> p (o k)"), ident[:])
                    ins.then_inc(pT_mm, 1)
                    if t + 1 < NT:
                        scores(t + 1)
                    pe.wait_ge(pT_a, b * NT + t + 1)
                    pe.wait_ge(pT_v, b * NT + t + 1)
                    if t:
                        pe.wait_ge(att_ok, b * 2 * NT + 2 * t)
                    for h in range(NH):
                        o = (h % 2) * 4 + h // 2
                        ins = te.matmul(pv_ps[:, o * DH:(o + 1) * DH], pT[:, o], vtok[:, t, h, 0:DH], start=True, stop=True)
                    ins.then_inc(pv_mm, 1)
                    if t:
                        project(t - 1)
                    if t + 1 < NT:
                        pe.wait_ge(att_ok, b * 2 * NT + 2 * t + 2)
                        memory_read(t + 1)
                project(NT - 1)


def _beta(a, b):
    return math.exp(math.lgamma(a) + math.lgamma(b) - math.lgamma(a + b))


def ball_block(nc, io, x1, xs):
    NH, DH = 16, 16
    FF = 1024
    MF = FF // P
    EPS = 1e-7
    BALL = float(np.float32(1.0 - 1e-5))
    C = math.atanh(BALL)
    R = _beta(DH / 2, 0.5) / _beta(D / 2, 0.5)
    assert math.sqrt(NH) * C / R < C * 0.999
    SL = 8
    U = NT * NH
    ROOTS = [(NT, 0.5), (NT, -0.5), (NT, -0.5)] + [(3 * NH + 3, -0.5)] * NT + \
            [(NT, -0.5), (NT, 0.5), (NT, 0.5), (NT, -0.5), (NT, -0.5), (NT, -0.5), (NT, -0.5), (NT, 0.5)]
    NR = len(ROOTS)

    with ExitStack() as ctx:
        def sb(name, shape, dt=F32):
            return ctx.enter_context(nc.sbuf_tensor("b_" + name, shape, dt))

        def sem(name):
            return ctx.enter_context(nc.semaphore("b_" + name))

        wqkv = sb("wqkv", [P, KD, 3 * D])
        wo = sb("wo", [P, KD, D])
        wf1 = sb("wf1", [P, KD, FF])
        wf2 = sb("wf2", [P, MF, D])
        wada = sb("wada", [P, KD, 6 * D])
        bada = sb("bada", [1, 6 * D])
        bqkv = sb("bqkv", [P, 3 * D])
        bo = sb("bo", [P, D])
        bf2 = sb("bf2", [P, D])
        bf1 = sb("bf1", [P, MF])
        condT = sb("condT", [P, KD, B])
        ident = sb("ident", [P, P])
        identb = sb("identb", [P, P], BF16)
        ones = sb("ones", [P, 8])
        ada = sb("ada", [B, 6 * D])
        mod = sb("mod", [P, 6, D])
        x = sb("x", [P, NT, D])
        xb = sb("xb", [P, NT, D])
        u = sb("u", [P, NT, D])
        uT = sb("uT", [P, KD, L])
        y = sb("y", [P, 2, 3 * D])
        ysq = sb("ysq", [P, 3 * NH, DH])
        z = sb("z", [P, 2, 2, NH, DH])
        r1 = sb("r1", [P, 2, NH, DH])
        stack = sb("stack", [P, 2, 2, NH, SL, DH], BF16)
        val = sb("val", [P, NT, D])
        qS = sb("qS", [P, NH, L], BF16)
        kS = sb("kS", [P, NH, L], BF16)
        nmx = sb("nmx", [P, 4])
        pr = sb("pr", [P, 3, L])
        rs = sb("rs", [P, 2, NH])
        ri = sb("ri", [P, 2, NH])
        pT = sb("pT", [P, 2, NT, P])
        ot = sb("ot", [P, 2, D])
        oT = sb("oT", [P, KD, P])
        ya = sb("ya", [P, 2, D])
        w = sb("w", [P, NT, D])
        junk = sb("junk", [P, 2, D])
        junkv = sb("junkv", [P, D])
        fT = sb("fT", [P, MF, L])
        fsq = sb("fsq", [P, MF, L])
        outt = sb("outt", [P, 2, D])
        st = sb("st", [P, NT, 6])
        mv = sb("mv", [P, NT, 2])
        mv2 = sb("mv2", [P, NT, 2])
        hn = sb("hn", [P, 3 * NH + 3])
        hf = sb("hf", [P, 3 * NH + 3])
        rin = sb("rin", [P, 3 * NH + 3])
        rout = sb("rout", [P, 3 * NH + 3])
        expo = sb("expo", [P, 2, 3 * NH + 3])
        sv = sb("sv", [P, 24, NT])
        carrier = sb("carrier", [P, 1])

        ps = ctx.enter_context(nc.psum_tensor("b_ps", [P, 8, 512], F32))
        ps_flat = ps[:].rearrange("p a n -> p (a n)")

        ld_w = sem("ld_w")
        ld_x = sem("ld_x")
        ld_m = sem("ld_m")
        ada_mm = sem("ada_mm")
        ada_ok = sem("ada_ok")
        ada_st = sem("ada_st")
        const_ok = sem("const_ok")
        root_ask = sem("root_ask")
        root_ok = sem("root_ok")
        ln_ask = sem("ln_ask")
        ln_ok = sem("ln_ok")
        th_ask = sem("th_ask")
        th_ok = sem("th_ok")
        u_ok = sem("u_ok")
        usq_ok = sem("usq_ok")
        us_ok = sem("us_ok")
        u_mm = sem("u_mm")
        uT_a = sem("uT_a")
        uT_v = sem("uT_v")
        qkv_mm = sem("qkv_mm")
        y_ok = sem("y_ok")
        ysq_ok = sem("ysq_ok")
        z_ok = sem("z_ok")
        top_ok = sem("top_ok")
        r1_ok = sem("r1_ok")
        mid_ok = sem("mid_ok")
        low_ok = sem("low_ok")
        stq_mm = sem("stq_mm")
        qS_ok = sem("qS_ok")
        kS_ok = sem("kS_ok")
        s_mm = sem("s_mm")
        mx_ok = sem("mx_ok")
        p_ok = sem("p_ok")
        pT_mm = sem("pT_mm")
        pT_a = sem("pT_a")
        pT_v = sem("pT_v")
        pv_mm = sem("pv_mm")
        o_ok = sem("o_ok")
        oT_mm = sem("oT_mm")
        oT_ok = sem("oT_ok")
        wo_mm = sem("wo_mm")
        w_ok = sem("w_ok")
        wsq_ok = sem("wsq_ok")
        f_mm = sem("f_mm")
        f_v = sem("f_v")
        f_a = sem("f_a")
        fn_mm = sem("fn_mm")
        f2_mm = sem("f2_mm")
        out_ok = sem("out_ok")
        st_x = [sem("st_x0"), sem("st_x1")]
        v_c = sem("v_c")
        ada_dram = nc.dram_tensor("ada", (B, 6 * D), F32, kind="Internal").ap()
        block = ctx.enter_context(nc.Block())
        NWL = 12

        def by_act(n):
            return n % 3 == 0

        @block.sync
        def _(sp):
            for dst, name in ((condT, "condT"), (wada, "wada"), (bada, "bada"), (wqkv, "bwqkv"), (bqkv, "bqkv"), (ident, "ident"),
                              (wo, "bwo"), (bo, "bo"), (wf1, "wf1"), (bf1, "bf1"), (wf2, "wf2"), (bf2, "bf2")):
                sp.dma_start(dst[:], io[name]).then_inc(ld_w, 16)
            sp.wait_ge(ada_ok, 1)
            sp.dma_start(ada_dram, ada[:]).then_inc(ada_st, 16)
            sp.wait_ge(ada_st, 16)
            with sp.Fori(0, B) as b:
                sp.wait_ge(out_ok, b * NT)
                sp.dma_start(x[:], x1[bass.ds(b, 1)].rearrange("a (t p) d -> p (a t) d", p=P)).then_inc(ld_x, 16)
                sp.dma_start(mod[:], ada_dram[bass.ds(b, 1)].broadcast_to([P, 6 * D]).rearrange("p (s d) -> p s d", s=6)).then_inc(ld_m, 16)
                for t in range(NT):
                    sp.wait_ge(out_ok, b * NT + t + 1)
                    sp.dma_start(xs[bass.ds(b, 1)].rearrange("a (t p) d -> t p (a d)", p=P)[t], outt[:, t % 2]).then_inc(st_x[t % 2], 16)
            for s in st_x:
                sp.wait_ge(s, 16 * B * NT // 2)

        @block.gpsimd
        def _(pool):
            g = nc.gpsimd
            g.memset(expo[:, 0], 0.5).then_inc(const_ok, 1)
            g.memset(expo[:, 1], -0.5).then_inc(const_ok, 1)
            g.memset(ones[:], 1.0).then_inc(const_ok, 1)
            pool.wait_ge(const_ok, 3)
            with pool.Fori(0, B) as b:
                for n, (width, e) in enumerate(ROOTS):
                    pool.wait_ge(root_ask, b * NR + n + 1)
                    g.tensor_tensor(rout[:, 0:width], rin[:, 0:width], expo[:, int(e < 0), 0:width], ALU.pow).then_inc(root_ok, 1)

        @block.scalar
        def _(act):
            a = nc.scalar
            act.wait_ge(ada_mm, 1)
            a.activation(ada[:], ps_flat[0:B, 0:6 * D], ACT.Copy).then_inc(ada_ok, 1)
            act.wait_ge(ld_w, NWL * 16)
            a.activation(identb[:], ident[:], ACT.Copy).then_inc(ada_ok, 1)
            with act.Fori(0, B) as b:
                def squares(n, src, cols, ask, done):
                    act.wait_ge(ask, n)
                    act.wait_ge(done, n - 1)
                    for k, (s, c) in enumerate(zip(src, cols)):
                        ins = a.activation(junk[:, k], s, ACT.Square, accum_out=c)
                    ins.then_inc(done, 1)

                def log_and_rows(h):
                    act.wait_ge(ln_ask, b * 2 + h + 1)
                    a.activation(sv[:, 5], sv[:, 4], ACT.Ln).then_inc(ln_ok, 1)
                    for t in range(NT):
                        squares((b * 2 + h) * NT + t + 1, [u[:, t]], [sv[:, 12, t:t + 1]], u_ok, usq_ok)
                    act.wait_ge(u_mm, b * 2 + h + 1)
                    a.activation(uT[:, 0], ps[:, 0], ACT.Copy).then_inc(uT_a, 1)

                log_and_rows(0)

                def queries_out(t):
                    act.wait_ge(stq_mm, b * NT + t + 1)
                    a.activation(qS[:, :, t * P:(t + 1) * P], ps[:, 6:8].bitcast(BF16).rearrange("p a (h q) -> p (a h) q", q=P), ACT.Copy).then_inc(qS_ok, 1)

                def parts(t, src, slots, ask, done):
                    act.wait_ge(ask, b * NT + t + 1)
                    for qk in range(2):
                        dst = stack[:, t % 2, qk][:, :, slots[qk]]
                        n = dst.shape[2]
                        ins = a.activation(dst, src[:, qk].unsqueeze(2).broadcast_to([P, NH, n, DH]), ACT.Copy)
                    ins.then_inc(done, 1)

                for t in range(NT):
                    act.wait_ge(y_ok, b * NT + t + 1)
                    if t:
                        act.wait_ge(z_ok, b * NT + t)
                    a.activation(ysq[:], y[:, t % 2].rearrange("p (h v) -> p h v", v=DH), ACT.Square).then_inc(ysq_ok, 1)
                    if t:
                        queries_out(t - 1)
                    parts(t, z[:, t % 2], (slice(0, 3), slice(0, 8, 3)), z_ok, top_ok)
                    parts(t, r1, (slice(3, 6), slice(1, 8, 3)), r1_ok, mid_ok)
                queries_out(NT - 1)

                def heads_turned(t):
                    act.wait_ge(oT_mm, b * NT + t + 1)
                    a.activation(oT[:], ps[:, 7, 0:D].rearrange("p (k q) -> p k q", q=P), ACT.Copy).then_inc(oT_ok, 1)

                def move(n):
                    if by_act(n):
                        act.wait_ge(pT_mm, b * U + n + 1)
                        if n >= 2:
                            act.wait_ge(pv_mm, b * U + n - 1)
                        a.activation(pT[:, n % 2], ps[:, 3 + n % 2].rearrange("p (k q) -> p k q", q=P), ACT.Copy).then_inc(pT_a, 1)

                def update_squares(t):
                    squares(b * 2 * NT + t + 1, [ya[:, t % 2], w[:, t]], [sv[:, 13, t:t + 1], sv[:, 14, t:t + 1]], w_ok, wsq_ok)

                for n in range(U):
                    t, h = n // NH, n % NH
                    act.wait_ge(mx_ok, b * U + n + 1)
                    if n >= 3:
                        act.wait_ge(pT_mm, b * U + n - 2)
                    if t >= 2 and h == 0:
                        act.wait_ge(o_ok, b * NT + t - 1)
                    a.activation(pr[:, n % 3], ps[:, n % 3], ACT.Exp, bias=nmx[:, n % 4:n % 4 + 1],
                                 accum_out=rs[:, t % 2, h:h + 1]).then_inc(p_ok, 1)
                    if n:
                        move(n - 1)
                    if t and h == 4:
                        heads_turned(t - 1)
                    if t and h == 8:
                        update_squares(t - 1)
                move(U - 1)
                heads_turned(NT - 1)
                update_squares(NT - 1)
                act.wait_ge(th_ask, b * 2 + 1)
                a.activation(sv[:, 17], sv[:, 16], ACT.Tanh).then_inc(th_ok, 1)
                log_and_rows(1)
                for m in range(MF):
                    act.wait_ge(f_v, b * MF + m + 1)
                    a.activation(fsq[:, m], fT[:, m], ACT.Square).then_inc(f_a, 1)
                for t in range(NT):
                    squares(b * 2 * NT + NT + t + 1, [ya[:, t % 2], w[:, t]], [sv[:, 13, t:t + 1], sv[:, 14, t:t + 1]], w_ok, wsq_ok)
                act.wait_ge(th_ask, b * 2 + 2)
                a.activation(sv[:, 17], sv[:, 16], ACT.Tanh).then_inc(th_ok, 1)

        @block.vector
        def _(dve):
            v = nc.vector
            dve.wait_ge(ld_w, NWL * 16)
            dve.wait_ge(const_ok, 3)
            with dve.Fori(0, B) as b:
                LINKS = 193
                ch = Chain(dve, v_c, b * LINKS)
                asked = [0]

                def ts(out, in0, s1, s2, op0, op1=None):
                    if op1 is None:
                        ch.link(v.tensor_scalar(out, in0, s1, None, op0))
                    else:
                        ch.link(v.tensor_scalar(out, in0, s1, s2, op0, op1))

                def tt(out, in0, in1, op):
                    ch.link(v.tensor_tensor(out, in0, in1, op))

                def ask(ins):
                    ins.then_inc(root_ask, 1)
                    asked[0] += 1

                def answer():
                    dve.wait_ge(root_ok, b * NR + asked[0])

                def root(src, width, low, meanwhile=None):
                    ask(v.tensor_scalar(rin[:, 0:width], src, low, None, ALU.max))
                    if meanwhile:
                        meanwhile()
                    answer()

                SCALE1, N2 = sv[:, 10], sv[:, 11]

                def row_factors(h, src, mvt):
                    for t in range(NT):
                        n = ch.mark(v.bn_stats(st[:, t], src[:, t]))
                    ch.wait(n)
                    v.memset(carrier[:], 0.0)
                    for t in range(NT):
                        n = ch.mark(v.bn_aggr(mvt[:, t], st[:, t]))
                    ch.wait(n)
                    tt(sv[:, 0], mvt[:, :, 0], mvt[:, :, 0], ALU.mult)
                    tt(sv[:, 0], sv[:, 0], mvt[:, :, 1], ALU.add)
                    ts(N2, sv[:, 0], float(D), None, ALU.mult)
                    root(N2, NT, EPS * EPS)
                    ts(sv[:, 1], rout[:, 0:NT], 1.0, None, ALU.mult)
                    ts(sv[:, 2], sv[:, 1], BALL, None, ALU.min)
                    ts(sv[:, 3], sv[:, 2], -1.0, 1.0, ALU.mult, ALU.add)
                    ch.link(v.reciprocal(sv[:, 3], sv[:, 3]))
                    ts(sv[:, 0], sv[:, 2], 1.0, None, ALU.add)
                    v.tensor_tensor(sv[:, 4], sv[:, 0], sv[:, 3], ALU.mult).then_inc(ln_ask, 1)
                    tt(sv[:, 6], sv[:, 2], sv[:, 2], ALU.mult)
                    ts(sv[:, 7], sv[:, 6], 1.0 / 11, 1.0 / 9, ALU.mult, ALU.add)
                    for c in (7, 5, 3, 1):
                        tt(sv[:, 7], sv[:, 7], sv[:, 6], ALU.mult)
                        ts(sv[:, 7], sv[:, 7], 1.0 / c, None, ALU.add)
                    ts(sv[:, 8], sv[:, 1], 0.25, None, ALU.is_lt)
                    ch.link(v.reciprocal(sv[:, 1], sv[:, 1]))
                    dve.wait_ge(ln_ok, b * 2 + h + 1)
                    ts(sv[:, 9], sv[:, 5], 0.5, None, ALU.mult)
                    tt(sv[:, 9], sv[:, 9], sv[:, 1], ALU.mult)
                    tt(sv[:, 7], sv[:, 7], sv[:, 9], ALU.subtract)
                    tt(sv[:, 7], sv[:, 7], sv[:, 8], ALU.mult)
                    tt(sv[:, 9], sv[:, 9], sv[:, 7], ALU.add)
                    tt(sv[:, 0], sv[:, 9], sv[:, 9], ALU.mult)
                    tt(sv[:, 0], sv[:, 0], mvt[:, :, 1], ALU.mult)
                    root_plus(sv[:, 0], 1e-6)
                    tt(SCALE1, sv[:, 9], rout[:, 0:NT], ALU.mult)

                def root_plus(src, eps):
                    ask(v.tensor_scalar(rin[:, 0:NT], src, eps, None, ALU.add))
                    answer()

                def modulate(h, src, mvt):
                    sh, sc = mod[:, 3 * h], mod[:, 3 * h + 1]
                    for t in range(NT):
                        ch.link(v.scalar_tensor_tensor(out=u[:, t], in0=src[:, t], scalar=mvt[:, t, 0:1], in1=sc,
                                                       op0=ALU.subtract, op1=ALU.mult))
                        v.scalar_tensor_tensor(out=u[:, t], in0=u[:, t], scalar=SCALE1[:, t:t + 1], in1=sh,
                                               op0=ALU.mult, op1=ALU.add).then_inc(u_ok, 1)

                def limit(out, n):
                    ts(out, rout[:, 0:n], C, 1.0, ALU.mult, ALU.min)

                def turned_rows(h):
                    dve.wait_ge(u_mm, b * 2 + h + 1)
                    v.tensor_copy(uT[:, 1], ps[:, 1]).then_inc(uT_v, 1)

                def update(h, t, factor, bias, src):
                    if t >= 2:
                        dve.wait_ge(wsq_ok, (b * 2 + h) * NT + t - 1)
                    if factor is None:
                        ch.link(v.tensor_tensor(ya[:, t % 2], ps[:, 7, 0:D], bias, ALU.add))
                    else:
                        ch.link(v.scalar_tensor_tensor(out=ya[:, t % 2], in0=ps[:, 6 + t % 2, 0:D], scalar=factor, in1=bias,
                                                       op0=ALU.mult, op1=ALU.add))
                    v.tensor_tensor(w[:, t], ya[:, t % 2], mod[:, 3 * h + 2], ALU.mult).then_inc(w_ok, 1)
                    dve.wait_ge(w_ok, (b * 2 + h) * NT + t + 1)
                    tt(junkv[:], src[:, t], w[:, t], ALU.mult)
                    ch.mark(v.tensor_reduce(sv[:, 15, t:t + 1], junkv[:], AX.X, ALU.add))

                def mobius(h):
                    dve.wait_ge(wsq_ok, (b * 2 + h + 1) * NT)
                    root(sv[:, 13], NT, EPS * EPS)
                    limit(sv[:, 18], NT)
                    tt(sv[:, 0], sv[:, 18], sv[:, 18], ALU.mult)
                    tt(sv[:, 0], sv[:, 0], sv[:, 14], ALU.mult)
                    root(sv[:, 0], NT, EPS * EPS)
                    v.tensor_scalar(sv[:, 16], rout[:, 0:NT], 1.0, None, ALU.mult).then_inc(th_ask, 1)
                    dve.wait_ge(th_ask, b * 2 + h + 1)
                    ch.link(v.reciprocal(sv[:, 19], sv[:, 16]))
                    tt(sv[:, 19], sv[:, 19], sv[:, 18], ALU.mult)
                    dve.wait_ge(th_ok, b * 2 + h + 1)
                    tt(sv[:, 19], sv[:, 19], sv[:, 17], ALU.mult)
                    tt(sv[:, 0], sv[:, 17], sv[:, 17], ALU.mult)
                    tt(sv[:, 1], sv[:, 15], sv[:, 19], ALU.mult)
                    ts(sv[:, 1], sv[:, 1], 2.0, 1.0, ALU.mult, ALU.add)
                    tt(sv[:, 2], N2, sv[:, 0], ALU.mult)
                    tt(sv[:, 2], sv[:, 2], sv[:, 1], ALU.add)
                    ts(sv[:, 2], sv[:, 2], EPS, None, ALU.max)
                    ch.link(v.reciprocal(sv[:, 2], sv[:, 2]))
                    tt(sv[:, 1], sv[:, 1], sv[:, 0], ALU.add)
                    tt(sv[:, 20], sv[:, 1], sv[:, 2], ALU.mult)
                    ts(sv[:, 3], N2, -1.0, 1.0, ALU.mult, ALU.add)
                    tt(sv[:, 3], sv[:, 3], sv[:, 2], ALU.mult)
                    tt(sv[:, 21], sv[:, 3], sv[:, 19], ALU.mult)

                dve.wait_ge(ld_x, b * 16 + 16)
                dve.wait_ge(ld_m, b * 16 + 16)
                for h in range(2):
                    ts(mod[:, 3 * h + 1], mod[:, 3 * h + 1], 1.0, None, ALU.add)
                row_factors(0, x, mv)
                modulate(0, x, mv)
                dve.wait_ge(usq_ok, (b * 2 + 1) * NT)
                root(sv[:, 12], NT, EPS * EPS, meanwhile=lambda: turned_rows(0))
                limit(sv[:, 22], NT)

                def projected(t):
                    dve.wait_ge(qkv_mm, b * NT + t + 1)
                    v.scalar_tensor_tensor(out=y[:, t % 2], in0=ps_flat[:, 1024 * (1 + t % 2):1024 * (1 + t % 2) + 3 * D],
                                           scalar=sv[:, 22, t:t + 1], in1=bqkv[:], op0=ALU.mult, op1=ALU.add).then_inc(y_ok, 1)

                def keys_out(t):
                    dve.wait_ge(stq_mm, b * NT + t + 1)
                    v.tensor_copy(kS[:, :, t * P:(t + 1) * P], ps[:, 0:2].bitcast(BF16).rearrange("p a (h q) -> p (a h) q", q=P)).then_inc(kS_ok, 1)

                projected(0)
                for t in range(NT):
                    dve.wait_ge(ysq_ok, b * NT + t + 1)
                    ch.link(v.tensor_reduce(hn[:, 0:3 * NH], ysq[:], AX.X, ALU.add))
                    ch.link(v.tensor_reduce(hn[:, 3 * NH:], hn[:, 0:3 * NH].rearrange("p (s h) -> p s h", s=3), AX.X, ALU.add))
                    root(hn[:], 3 * NH + 3, EPS * EPS, meanwhile=(lambda: projected(t + 1)) if t + 1 < NT else None)
                    ts(hf[:], rout[:], C, None, ALU.mult)
                    ts(hf[:, 3 * NH:], hf[:, 3 * NH:], 1.0, R, ALU.min, ALU.mult)
                    tt(hf[:, 0:3 * NH].rearrange("p (s h) -> p s h", s=3), hf[:, 0:3 * NH].rearrange("p (s h) -> p s h", s=3),
                       hf[:, 3 * NH:].unsqueeze(2).broadcast_to([P, 3, NH]), ALU.min)
                    ts(hf[:, 0:NH], hf[:, 0:NH], DH ** -0.5, None, ALU.mult)
                    ch.mark(v.tensor_tensor(val[:, t].rearrange("p (h v) -> p h v", v=DH),
                                            y[:, t % 2, 2 * D:].rearrange("p (h v) -> p h v", v=DH),
                                            hf[:, 2 * NH:3 * NH].unsqueeze(2).broadcast_to([P, NH, DH]), ALU.mult))
                    zt = z[:, t % 2].rearrange("p a h v -> p (a h) v")
                    v.tensor_tensor(zt, y[:, t % 2, 0:2 * D].rearrange("p (h v) -> p h v", v=DH),
                                    hf[:, 0:2 * NH].unsqueeze(2).broadcast_to([P, 2 * NH, DH]), ALU.mult).then_inc(z_ok, 1)
                    if t:
                        keys_out(t - 1)
                    dve.wait_ge(z_ok, b * NT + t + 1)
                    dve.wait_ge(top_ok, b * NT + t + 1)
                    sk = stack[:, t % 2]
                    v.tensor_tensor(r1[:], z[:, t % 2], sk[:, :, :, 0], ALU.subtract).then_inc(r1_ok, 1)
                    dve.wait_ge(r1_ok, b * NT + t + 1)
                    dve.wait_ge(mid_ok, b * NT + t + 1)
                    v.tensor_tensor(sk[:, 0, :, 6:8], r1[:, 0].unsqueeze(2).broadcast_to([P, NH, 2, DH]),
                                    sk[:, 0, :, 3:5], ALU.subtract)
                    v.tensor_tensor(sk[:, 1, :, 2:6:3], r1[:, 1].unsqueeze(2).broadcast_to([P, NH, 2, DH]),
                                    sk[:, 1, :, 1:5:3], ALU.subtract).then_inc(low_ok, 1)
                keys_out(NT - 1)

                def maximum(n):
                    dve.wait_ge(s_mm, b * U + n + 1)
                    if n >= 4:
                        dve.wait_ge(p_ok, b * U + n - 3)
                    v.tensor_reduce(nmx[:, n % 4:n % 4 + 1], ps[:, n % 3], AX.X, ALU.max, negate=True).then_inc(mx_ok, 1)

                def move(n):
                    if not by_act(n):
                        dve.wait_ge(pT_mm, b * U + n + 1)
                        if n >= 2:
                            dve.wait_ge(pv_mm, b * U + n - 1)
                        v.tensor_copy(pT[:, n % 2], ps[:, 3 + n % 2].rearrange("p (k q) -> p k q", q=P)).then_inc(pT_v, 1)

                def heads(t):
                    dve.wait_ge(p_ok, b * U + (t + 1) * NH)
                    ch.link(v.reciprocal(ri[:, t % 2], rs[:, t % 2]))
                    ts(ri[:, t % 2], ri[:, t % 2], 1.0 / R, None, ALU.mult)
                    dve.wait_ge(pv_mm, b * U + (t + 1) * NH)
                    if t >= 2:
                        dve.wait_ge(oT_mm, b * NT + t - 1)
                    v.tensor_tensor(ot[:, t % 2].rearrange("p (h v) -> p h v", v=DH), ps[:, 5 + t % 2, 0:D].rearrange("p (h v) -> p h v", v=DH),
                                    ri[:, t % 2].unsqueeze(2).broadcast_to([P, NH, DH]), ALU.mult).then_inc(o_ok, 1)

                def attention_update(t):
                    dve.wait_ge(wo_mm, b * NT + t + 1)
                    update(0, t, None, bo[:], x)

                maximum(0)
                maximum(1)
                for n in range(U):
                    t, h = n // NH, n % NH
                    if n + 2 < U:
                        maximum(n + 2)
                    move(n)
                    if t and h == 1:
                        heads(t - 1)
                    if t and h == 6:
                        attention_update(t - 1)
                heads(NT - 1)
                attention_update(NT - 1)
                mobius(0)
                for t in range(NT):
                    ts(xb[:, t], x[:, t], sv[:, 20, t:t + 1], None, ALU.mult)
                    ch.link(v.scalar_tensor_tensor(out=xb[:, t], in0=w[:, t], scalar=sv[:, 21, t:t + 1], in1=xb[:, t],
                                                   op0=ALU.mult, op1=ALU.add))

                row_factors(1, xb, mv2)
                modulate(1, xb, mv2)
                dve.wait_ge(usq_ok, (b * 2 + 2) * NT)
                root(sv[:, 12], NT, EPS * EPS)
                limit(sv[:, 22], NT)
                for t in range(NT):
                    v.tensor_scalar(u[:, t], u[:, t], sv[:, 22, t:t + 1], None, ALU.mult).then_inc(us_ok, 1)
                turned_rows(1)
                for m in range(MF):
                    dve.wait_ge(f_mm, b * MF + m + 1)
                    v.tensor_scalar(fT[:, m], ps[:, 2 + m % 3], bf1[:, m:m + 1], None, ALU.add).then_inc(f_v, 1)
                dve.wait_ge(fn_mm, b + 1)
                root(ps[:, 5, 0:NT], NT, EPS * EPS)
                limit(sv[:, 23], NT)
                for t in range(NT):
                    dve.wait_ge(f2_mm, b * NT + t + 1)
                    update(1, t, sv[:, 23, t:t + 1], bf2[:], xb)
                mobius(1)
                for t in range(NT):
                    dve.wait_ge(st_x[t % 2], b * 32 + 16 * (t // 2))
                    ts(xb[:, t], xb[:, t], sv[:, 20, t:t + 1], None, ALU.mult)
                    v.scalar_tensor_tensor(out=outt[:, t % 2], in0=w[:, t], scalar=sv[:, 21, t:t + 1], in1=xb[:, t],
                                           op0=ALU.mult, op1=ALU.add).then_inc(out_ok, 1)
                assert ch.n == LINKS, ch.n
                assert asked[0] == NR, asked

        @block.tensor
        def _(pe):
            te = nc.tensor
            pe.wait_ge(ld_w, NWL * 16)
            pe.wait_ge(const_ok, 3)
            for s in range(3):
                cols = slice(512 * s, 512 * s + 512)
                for k in range(KD):
                    te.matmul(ps[0:B, s], condT[:, k], wada[:, k, cols], start=(k == 0), stop=False)
                ins = te.matmul(ps[0:B, s], ones[0:1, 0:B], bada[:, cols], start=False, stop=True)
            ins.then_inc(ada_mm, 1)
            pe.wait_ge(ada_ok, 2)
            with pe.Fori(0, B) as b:
                def turn_rows(h, ready):
                    for t in range(NT):
                        pe.wait_ge(*ready(t))
                        for c in range(KD):
                            ins = te.transpose(ps[:, c, t * P:(t + 1) * P], u[:, t, c * P:(c + 1) * P], ident[:])
                    ins.then_inc(u_mm, 1)
                    pe.wait_ge(uT_a, b * 2 + h + 1)
                    pe.wait_ge(uT_v, b * 2 + h + 1)

                turn_rows(0, lambda t: (u_ok, b * 2 * NT + t + 1))

                def qkv(t):
                    if t >= 2:
                        pe.wait_ge(y_ok, b * NT + t - 1)
                    for lo, hi, bank in ((0, 512, 2 + 2 * (t % 2)), (512, 768, 3 + 2 * (t % 2))):
                        for k in range(KD):
                            ins = te.matmul(ps[:, bank, 0:hi - lo], uT[:, k, t * P:(t + 1) * P], wqkv[:, k, lo:hi],
                                            start=(k == 0), stop=(k == KD - 1))
                    ins.then_inc(qkv_mm, 1)

                def turn_stacks(t):
                    pe.wait_ge(low_ok, b * NT + t + 1)
                    pe.wait_ge(qS_ok, b * NT + t)
                    pe.wait_ge(kS_ok, b * NT + t)
                    for s, bank in ((0, 6), (1, 0)):
                        dst = ps[:, bank:bank + 2].bitcast(BF16).rearrange("p a (h q) -> p (a h) q", q=P)
                        for h in range(NH):
                            ins = te.transpose(dst[:, h], stack[:, t % 2, s, h].rearrange("p s v -> p (s v)"), identb[:])
                    ins.then_inc(stq_mm, 1)

                qkv(0)
                for t in range(NT):
                    if t + 1 < NT:
                        qkv(t + 1)
                    turn_stacks(t)

                def scores(n):
                    t, h = n // NH, n % NH
                    if n < 3:
                        pe.wait_ge(kS_ok, b * NT + NT)
                        pe.wait_ge(qS_ok, b * NT + NT)
                        pe.wait_ge(y_ok, b * NT + NT)
                    else:
                        pe.wait_ge(p_ok, b * U + n - 2)
                    te.matmul(ps[:, n % 3], qS[:, h, t * P:(t + 1) * P], kS[:, h], start=True, stop=True).then_inc(s_mm, 1)

                def values(n):
                    t, h = n // NH, n % NH
                    if by_act(n):
                        pe.wait_ge(pT_a, b * NA + n // 3 + 1)
                    else:
                        pe.wait_ge(pT_v, b * (U - NA) + n - n // 3)
                    for k in range(NT):
                        ins = te.matmul(ps[:, 5 + t % 2, h * DH:(h + 1) * DH], pT[:, n % 2, k], val[:, k, h * DH:(h + 1) * DH],
                                        start=(k == 0), stop=(k == NT - 1))
                    ins.then_inc(pv_mm, 1)

                NA = sum(by_act(n) for n in range(U))

                def project(t):
                    pe.wait_ge(o_ok, b * NT + t + 1)
                    pe.wait_ge(w_ok, b * 2 * NT + t)
                    for k in range(KD):
                        ins = te.transpose(ps[:, 7, k * P:(k + 1) * P], ot[:, t % 2, k * P:(k + 1) * P], ident[:])
                    ins.then_inc(oT_mm, 1)
                    pe.wait_ge(oT_ok, b * NT + t + 1)
                    for k in range(KD):
                        ins = te.matmul(ps[:, 7, 0:D], oT[:, k], wo[:, k], start=(k == 0), stop=(k == KD - 1))
                    ins.then_inc(wo_mm, 1)

                for n in range(3):
                    scores(n)
                for n in range(U):
                    t, h = n // NH, n % NH
                    pe.wait_ge(p_ok, b * U + n + 1)
                    for k in range(NT):
                        ins = te.transpose(ps[:, 3 + n % 2, k * P:(k + 1) * P], pr[:, n % 3, k * P:(k + 1) * P], ident[:])
                    ins.then_inc(pT_mm, 1)
                    if n + 3 < U:
                        scores(n + 3)
                    if n:
                        values(n - 1)
                    if t and h == 4:
                        project(t - 1)
                values(U - 1)
                project(NT - 1)

                turn_rows(1, lambda t: (us_ok, b * NT + t + 1))
                for m in range(MF):
                    if m >= 3:
                        pe.wait_ge(f_v, b * MF + m - 2)
                    for k in range(KD):
                        ins = te.matmul(ps[:, 2 + m % 3], wf1[:, k, m * P:(m + 1) * P], uT[:, k], start=(k == 0), stop=(k == KD - 1))
                    ins.then_inc(f_mm, 1)
                pe.wait_ge(f_a, b * MF + MF)
                for t in range(NT):
                    for m in range(MF):
                        ins = te.matmul(ps[:, 5, t:t + 1], fsq[:, m, t * P:(t + 1) * P], ones[:, 0:1], start=(m == 0), stop=(m == MF - 1))
                ins.then_inc(fn_mm, 1)
                for t in range(NT):
                    if t >= 2:
                        pe.wait_ge(w_ok, b * 2 * NT + NT + t - 1)
                    for m in range(MF):
                        ins = te.matmul(ps[:, 6 + t % 2, 0:D], fT[:, m, t * P:(t + 1) * P], wf2[:, m], start=(m == 0), stop=(m == MF - 1))
                    ins.then_inc(f2_mm, 1)


def window_layers(nc, io, xs, x1, out):
    NL = 2
    NH, DH = 8, 64
    NC = NH * DH // P
    HID = int(D * 4 * 2 / 3)
    MH = -(-HID // P)
    LAST = HID - (MH - 1) * P
    U = 2 * NT
    QK_SCALE = 8.0

    with ExitStack() as ctx:
        def sb(name, shape, dt=F32):
            return ctx.enter_context(nc.sbuf_tensor(name, shape, dt))

        def sem(name):
            return ctx.enter_context(nc.semaphore(name))

        wqkv = sb("wqkv", [P, KD, 3 * NC * P])
        wo = sb("wwo", [P, NC, D])
        w1 = sb("w1", [P, KD, 2 * HID])
        w2 = sb("w2", [P, MH, D])
        b1 = sb("b1", [P, 2, MH])
        lnp = sb("lnp", [P, 2, KD])
        qks = sb("qks", [P, 2, 2, DH])
        rot = sb("rot", [P, 2, NT, 2, DH])
        rots = sb("rots", [P, 2, NT, 2, DH])
        wmask = sb("wmask", [P, 2 * P])
        ident = sb("wident", [P, P])
        last = sb("last", [P, NL])
        xin = sb("xin", [P, NT, D])
        xadd = sb("xadd", [P, NT, D])
        hT = sb("hT", [P, KD, L])
        sq = sb("sq", [P, 2 * NH, DH])
        n2 = sb("n2", [P, 2, 2 * NH])
        t1 = sb("t1", [P, 2, NH, DH])
        t2 = sb("t2", [P, 2, NH, DH])
        qk = sb("qk", [P, 2, 2, NH, DH])
        vt = sb("vt", [P, NT, NC * P])
        qT = sb("wqT", [P, NC, L])
        kT = sb("wkT", [P, NC, L])
        sm = sb("sm", [P, 2, 4, 2 * P])
        mx = sb("wmx", [P, 2, 4])
        nmx = sb("nmx", [P, 2, 4])
        pr = sb("pr", [P, 2, 4, 2 * P])
        rs = sb("rs", [P, 2, 2, 4])
        ri = sb("ri", [P, 2, 2, 4])
        pT = sb("wpT", [P, 4, 2, P])
        ot = sb("ot", [P, 2, NC, 2, DH])
        oT = sb("oT", [P, NC, P])
        xm = sb("xm", [P, NT, D])
        hs = sb("hs", [P, NT, P])
        st = sb("st", [P, NT, 2, 6])
        mv = sb("mv", [P, NT, 2])
        ve = sb("ve", [P, 2, NT])
        mhalf = sb("mhalf", [P, 2 * NH])
        xn = sb("xn", [P, NT, D])
        xnT = sb("xnT", [P, KD, L])
        gl = sb("gl", [P, 2, L])
        h2T = sb("h2T", [P, MH, L])
        yt = sb("yt", [P, 2, D])
        yl = sb("yl", [P, 2, D])
        carrier = sb("carrier", [P, 1])

        ps = ctx.enter_context(nc.psum_tensor("wps", [P, 8, 512], F32))
        NW = 6
        ld_c = sem("ld_c")
        ld_w = sem("wld_w")
        ld_x = sem("wld_x")
        ld_a = sem("ld_a")
        x_mm = sem("x_mm")
        hT_a = sem("hT_a")
        hT_v = sem("hT_v")
        qkv_mm = sem("qkv_mm")
        v_ev = sem("v_ev")
        sq_ok = sem("sq_ok")
        qk_rd = sem("qk_rd")
        qk_ok = sem("qk_ok")
        qk_mm = sem("qk_mm")
        qT_ok = sem("qT_ok")
        kT_ok = sem("kT_ok")
        s_mm = sem("ws_mm")
        sm_ok = sem("sm_ok")
        p_ok = sem("wp_ok")
        pT_mm = sem("wpT_mm")
        pT_a = sem("wpT_a")
        pT_v = sem("wpT_v")
        pv_mm = sem("wpv_mm")
        o_ok = sem("o_ok")
        oT_mm = sem("oT_mm")
        oT_ok = sem("oT_ok")
        wo_mm = sem("wwo_mm")
        xm_ok = sem("xm_ok")
        sh_ok = sem("sh_ok")
        xn_ok = sem("xn_ok")
        xn_mm = sem("xn_mm")
        xnT_ok = sem("xnT_ok")
        g_mm = sem("g_mm")
        g_act = sem("g_act")
        h2_ok = sem("h2_ok")
        y_mm = sem("y_mm")
        y_ok = sem("y_ok")
        st_y = [sem("st_y0"), sem("st_y1")]
        st_o = [sem("st_o0"), sem("st_o1")]
        n2_ok = sem("n2_ok")
        nr_ok = sem("nr_ok")
        mh_ok = sem("mh_ok")
        v_w = sem("v_w")
        v_t = sem("v_t")
        block = ctx.enter_context(nc.Block())

        @block.sync
        def _(sp):
            for dst, name in ((rot, "rot"), (wmask, "wmask"), (ident, "ident"), (last, "last")):
                sp.dma_start(dst[:], io[name]).then_inc(ld_c, 16)
            with sp.Fori(0, NL) as l:
                for s in range(2):
                    sp.wait_ge(st_y[s], l * (16 * B * NT // 2))
                for dst, name in ((wqkv, "wqkv"), (wo, "wwo"), (w1, "w1"), (b1, "b1"), (lnp, "lnp"), (qks, "qks")):
                    d = dst[:]
                    if len(d.shape) > 3:
                        d = d.rearrange("p a b c -> p a (b c)")
                    src = io[name][bass.ds(l, 1)]
                    sp.dma_start(d, src.rearrange("l p a b -> p (l a) b")).then_inc(ld_w, 16)
                sp.dma_start(w2[:, 0:MH - 1], io["w2"][bass.ds(l, 1)].rearrange("l p a b -> p (l a) b")[:, 0:MH - 1]).then_inc(ld_w, 16)
                sp.dma_start(w2[0:LAST + 1, MH - 1], io["w2"][bass.ds(l, 1)].rearrange("l p a b -> p (l a) b")[0:LAST + 1, MH - 1]).then_inc(ld_w, 16)
                with sp.Fori(0, B) as b:
                    i = l * B + b
                    sp.wait_ge(xm_ok, i * NT)
                    sp.dma_start(xin[:], xs[bass.ds(i, 1)].rearrange("a (t p) d -> p (a t) d", p=P)).then_inc(ld_x, 16)
                    sp.wait_ge(y_ok, i * NT)
                    sp.dma_start(xadd[:], x1[bass.ds(b, 1)].rearrange("a (t p) d -> p (a t) d", p=P)).then_inc(ld_a, 16)
                    for t in range(NT):
                        sp.wait_ge(xm_ok, i * NT + t + 1)
                        sp.dma_start(hs[1:P, t], xm[0:P - 1, t, P:D]).then_inc(sh_ok, 16)
                        if t:
                            sp.dma_start(hs[0:1, t], xm[P - 1:P, t - 1, P:D]).then_inc(sh_ok, 16)
                    for t in range(NT):
                        sp.wait_ge(y_ok, i * NT + t + 1)
                        sp.dma_start(xs[bass.ds(i + B, 1)].rearrange("a (t p) d -> t p (a d)", p=P)[t], yt[:, t % 2]).then_inc(st_y[t % 2], 16)
                        sp.dma_start(out[bass.ds(b, 1)].rearrange("a (t p) d -> t p (a d)", p=P)[t], yl[:, t % 2]).then_inc(st_o[t % 2], 16)
            for s in st_y + st_o:
                sp.wait_ge(s, NL * 16 * B * NT // 2)

        @block.scalar
        def _(act):
            a = nc.scalar
            with act.Fori(0, NL) as l:
                with act.Fori(0, B) as b:
                    i = l * B + b
                    act.wait_ge(ld_w, (l + 1) * (16 * 8))
                    act.wait_ge(x_mm, i + 1)
                    a.activation(hT[:, 0], ps[:, 6], ACT.Copy).then_inc(hT_a, 1)

                    def turned_q(t):
                        act.wait_ge(qk_mm, i * NT + t + 1)
                        a.activation(qT[:, :, t * P:(t + 1) * P], ps[:, 6].rearrange("p (c q) -> p c q", q=P),
                                     ACT.Copy).then_inc(qT_ok, 1)

                    for t in range(NT):
                        act.wait_ge(qkv_mm, i * NT + t + 1)
                        act.wait_ge(qk_rd, i * NT + t)
                        k0 = 3 * (t % 2)
                        a.activation(sq[:], ps[:, k0:k0 + 2].rearrange("p a (h v) -> p (a h) v", v=DH), ACT.Square).then_inc(sq_ok, 1)
                        a.activation(vt[:, t], ps[:, k0 + 2], ACT.Copy).then_inc(v_ev, 1)
                        if t:
                            turned_q(t - 1)
                    turned_q(NT - 1)

                    def heads_out(t):
                        act.wait_ge(oT_mm, i * NT + t + 1)
                        if t:
                            act.wait_ge(wo_mm, i * NT + t)
                        a.activation(oT[:], ps[:, 7].rearrange("p (c q) -> p c q", q=P), ACT.Copy).then_inc(oT_ok, 1)

                    for u in range(U):
                        t, g = u // 2, u % 2
                        lo = P if t == 0 else 0
                        act.wait_ge(sm_ok, i * U + u + 1)
                        if u >= 2:
                            act.wait_ge(pT_mm, i * U + u - 1)
                        if t >= 2:
                            act.wait_ge(o_ok, i * U + u - 3)
                        for h in range(4):
                            ins = a.activation(pr[:, g, h, lo:], sm[:, g, h, lo:], ACT.Exp, bias=nmx[:, g, h:h + 1],
                                               scale=QK_SCALE, accum_out=rs[:, t % 2, g, h:h + 1])
                        ins.then_inc(p_ok, 1)
                        act.wait_ge(pT_mm, i * U + u + 1)
                        if u:
                            act.wait_ge(pv_mm, i * U + u)
                        a.activation(pT[:, 0:2, lo // P:], ps[:, 4].rearrange("p (h k q) -> p h k q", h=2, k=2)[:, :, lo // P:],
                                     ACT.Copy).then_inc(pT_a, 1)
                        if u >= 2 and g == 0:
                            heads_out(t - 1)
                    heads_out(NT - 1)
                    for m in range(MH):
                        n = P if m < MH - 1 else LAST
                        act.wait_ge(g_mm, i * MH + m + 1)
                        if m >= 2:
                            act.wait_ge(h2_ok, i * MH + m - 1)
                        a.activation(gl[0:n, m % 2], ps[0:n, m % 2], ACT.Gelu, bias=b1[0:n, 1, m:m + 1]).then_inc(g_act, 1)

        @block.vector
        def _(dve):
            v = nc.vector
            pre = Chain(dve, v_w)
            pre.mark(v.memset(hT[:, 1, 0:1], 0.0))
            pre.mark(v.memset(hs[:, 0], 0.0))
            pre.link(v.memset(h2T[0:64, MH - 1], 1.0))
            dve.wait_ge(ld_c, 4 * 16)
            LL = 3

            def carry_wait():
                v.memset(carrier[:], 0.0)

            with dve.Fori(0, NL) as l:
                lw = Chain(dve, v_w, l * LL + pre.n)
                dve.wait_ge(ld_w, (l + 1) * (16 * 8))
                for s in range(2):
                    ins = v.tensor_tensor(rots[:, s], rot[:, s],
                                          qks[:, s].unsqueeze(1).broadcast_to([P, NT, 2, DH]), ALU.mult)
                    lw.mark(ins)
                lw.mark(v.memset(st[:], 0.0))
                with dve.Fori(0, B) as b:
                    i = l * B + b
                    dve.wait_ge(v_w, l * LL + LL + pre.n)
                    LINKS = 3 * NT + 2 * U + NT + 1 + NT
                    ch = Chain(dve, v_t, i * LINKS)
                    dve.wait_ge(x_mm, i + 1)
                    v.tensor_copy(hT[:, 1, 1:L], ps[:, 7, 0:L - 1]).then_inc(hT_v, 1)

                    def turned_k(t):
                        dve.wait_ge(qk_mm, i * NT + t + 1)
                        v.tensor_copy(kT[:, :, t * P:(t + 1) * P], ps[:, 7].rearrange("p (c q) -> p c q", q=P)).then_inc(kT_ok, 1)

                    for t in range(NT):
                        k0 = 3 * (t % 2)
                        dve.wait_ge(sq_ok, i * NT + t + 1)
                        ch.link(v.tensor_reduce(n2[:, 0], sq[:], AX.X, ALU.add))
                        v.tensor_scalar(n2[:, 0], n2[:, 0], 1e-24, None, ALU.max).then_inc(n2_ok, 1)
                        if t:
                            turned_k(t - 1)
                        dve.wait_ge(nr_ok, i * (NT + 1) + t + 1)
                        v.tensor_tensor(t1[:], ps[:, k0:k0 + 2].rearrange("p a (h v) -> p a h v", v=DH),
                                        n2[:, 1].rearrange("p (a h) -> p a h", a=2).unsqueeze(3).broadcast_to([P, 2, NH, DH]),
                                        ALU.mult).then_inc(qk_rd, 1)
                        dve.wait_ge(qk_rd, i * NT + t + 1)
                        if t >= 2:
                            dve.wait_ge(qk_mm, i * NT + t - 1)
                        q = qk[:, t % 2]
                        ch.mark(v.tensor_tensor(q, t1[:], rots[:, 0, t].unsqueeze(2).broadcast_to([P, 2, NH, DH]), ALU.mult))
                        hf = DH // 2
                        for s in range(2):
                            ins = v.tensor_tensor(t2[:, :, :, s * hf:(s + 1) * hf], t1[:, :, :, (1 - s) * hf:(2 - s) * hf],
                                                  rots[:, 1, t, :, s * hf:(s + 1) * hf].unsqueeze(2).broadcast_to([P, 2, NH, hf]), ALU.mult)
                        ch.link(ins)
                        v.tensor_tensor(q, q, t2[:], ALU.add).then_inc(qk_ok, 1)
                    turned_k(NT - 1)

                    def rows_after_attention(t):
                        dve.wait_ge(wo_mm, i * NT + t + 1)
                        v.tensor_tensor(xm[:, t], xin[:, t], ps[:, 7, 0:D], ALU.add).then_inc(xm_ok, 1)

                    def scores_max(u):
                        t, g = u // 2, u % 2
                        lo = P if t == 0 else 0
                        dve.wait_ge(s_mm, i * U + u + 1)
                        if u >= 2:
                            dve.wait_ge(p_ok, i * U + u - 1)
                        sp_ = ps[:, 2 * g:2 * g + 2].rearrange("p a (h k) -> p (a h) k", k=2 * P)
                        carry_wait()
                        for h in range(4):
                            ins = v.tensor_tensor_reduce(out=sm[:, g, h, lo:], in0=sp_[:, h, lo:], in1=wmask[:, lo:],
                                                         scale=1.0, scalar=-3.0e38, op0=ALU.add, op1=ALU.max,
                                                         accum_out=mx[:, g, h:h + 1])
                        ch.link(ins)
                        v.tensor_scalar(nmx[:, g], mx[:, g], -QK_SCALE, None, ALU.mult).then_inc(sm_ok, 1)

                    scores_max(0)
                    for u in range(U):
                        t, g = u // 2, u % 2
                        lo = P if t == 0 else 0
                        if u + 1 < U:
                            scores_max(u + 1)
                        dve.wait_ge(pT_mm, i * U + u + 1)
                        if u:
                            dve.wait_ge(pv_mm, i * U + u)
                        v.tensor_copy(pT[:, 2:4, lo // P:], ps[:, 5].rearrange("p (h k q) -> p h k q", h=2, k=2)[:, :, lo // P:]).then_inc(pT_v, 1)
                        dve.wait_ge(p_ok, i * U + u + 1)
                        ch.mark(v.reciprocal(ri[:, t % 2, g], rs[:, t % 2, g]))
                        dve.wait_ge(pv_mm, i * U + u + 1)
                        ch.wait(ch.n)
                        if t >= 2:
                            dve.wait_ge(oT_mm, i * NT + t - 1)
                        v.tensor_tensor(ot[:, t % 2, :, g], ps[:, 6, g * 256:(g + 1) * 256].rearrange("p (c v) -> p c v", v=DH),
                                        ri[:, t % 2, g].unsqueeze(2).broadcast_to([P, 4, DH]), ALU.mult).then_inc(o_ok, 1)
                        if g == 0 and t:
                            rows_after_attention(t - 1)
                    rows_after_attention(NT - 1)
                    dve.wait_ge(sh_ok, i * (16 * 7) + 16 * 7)
                    for t in range(NT):
                        if t == 0:
                            carry_wait()
                        v.bn_stats(st[:, t, 0], xm[:, t, 0:P])
                        n = ch.mark(v.bn_stats(st[:, t, 1], hs[:, t]))
                    ch.wait(n)
                    carry_wait()
                    for t in range(NT):
                        ins = v.bn_aggr(mv[:, t], st[:, t].rearrange("p a b -> p (a b)"))
                    ch.link(ins)
                    v.tensor_scalar(ve[:, 0], mv[:, :, 1], 1e-5, None, ALU.add).then_inc(n2_ok, 1)
                    dve.wait_ge(nr_ok, (i + 1) * (NT + 1))
                    for t in range(NT):
                        v.tensor_scalar(xn[:, t, 0:P], xm[:, t, 0:P], mv[:, t, 0:1], ve[:, 1, t:t + 1], ALU.subtract, ALU.mult)
                        v.tensor_scalar(xn[:, t, P:D], hs[:, t], mv[:, t, 0:1], ve[:, 1, t:t + 1], ALU.subtract, ALU.mult).then_inc(xn_ok, 1)
                    dve.wait_ge(xn_mm, i + 1)
                    for c in range(KD):
                        ins = v.tensor_scalar(xnT[:, c], ps[:, 4 + c], lnp[:, 0, c:c + 1], lnp[:, 1, c:c + 1], ALU.mult, ALU.add)
                    ins.then_inc(xnT_ok, 1)
                    for m in range(MH):
                        n = P if m < MH - 1 else LAST
                        dve.wait_ge(g_act, i * MH + m + 1)
                        v.scalar_tensor_tensor(out=h2T[0:n, m], in0=ps[0:n, 2 + m % 2], scalar=b1[0:n, 0, m:m + 1],
                                               in1=gl[0:n, m % 2], op0=ALU.add, op1=ALU.mult).then_inc(h2_ok, 1)
                    dve.wait_ge(ld_a, i * 16 + 16)
                    for t in range(NT):
                        dve.wait_ge(y_mm, i * NT + t + 1)
                        for s in (st_y, st_o):
                            dve.wait_ge(s[t % 2], i * 32 + 16 * (t // 2))
                        ch.link(v.tensor_tensor(yt[:, t % 2], xm[:, t], ps[:, 6 + t % 2, 0:D], ALU.add))
                        v.scalar_tensor_tensor(out=yl[:, t % 2], in0=xadd[:, t], scalar=last[:, bass.ds(l, 1)], in1=yt[:, t % 2],
                                               op0=ALU.mult, op1=ALU.add).then_inc(y_ok, 1)
                    assert ch.n == LINKS, ch.n

        @block.tensor
        def _(pe):
            te = nc.tensor
            pe.wait_ge(ld_c, 4 * 16)
            with pe.Fori(0, NL) as l:
                with pe.Fori(0, B) as b:
                    i = l * B + b
                    pe.wait_ge(ld_w, (l + 1) * (16 * 8))
                    pe.wait_ge(ld_x, i * 16 + 16)
                    pe.wait_ge(y_ok, i * NT)
                    for c in range(KD):
                        for t in range(NT):
                            ins = te.transpose(ps[:, 6 + c, t * P:(t + 1) * P], xin[:, t, c * P:(c + 1) * P], ident[:])
                    ins.then_inc(x_mm, 1)
                    pe.wait_ge(hT_a, i + 1)
                    pe.wait_ge(hT_v, i + 1)

                    def qkv(t):
                        if t >= 2:
                            pe.wait_ge(qk_rd, i * NT + t - 1)
                            pe.wait_ge(v_ev, i * NT + t - 1)
                        for s in range(3):
                            for k in range(KD):
                                ins = te.matmul(ps[:, 3 * (t % 2) + s], hT[:, k, t * P:(t + 1) * P], wqkv[:, k, s * 512:(s + 1) * 512],
                                                start=(k == 0), stop=(k == KD - 1))
                        ins.then_inc(qkv_mm, 1)

                    def turn(t):
                        pe.wait_ge(qk_ok, i * NT + t + 1)
                        pe.wait_ge(qT_ok, i * NT + t)
                        pe.wait_ge(kT_ok, i * NT + t)
                        for s in range(2):
                            flat = qk[:, t % 2, s].rearrange("p h v -> p (h v)")
                            for c in range(NC):
                                ins = te.transpose(ps[:, 6 + s, c * P:(c + 1) * P], flat[:, c * P:(c + 1) * P], ident[:])
                        ins.then_inc(qk_mm, 1)

                    qkv(0)
                    for t in range(NT):
                        if t + 1 < NT:
                            qkv(t + 1)
                        turn(t)

                    def scores(u):
                        t, g = u // 2, u % 2
                        lo = P if t == 0 else 0
                        if u >= 2:
                            pe.wait_ge(sm_ok, i * U + u - 1)
                        if u == 0:
                            pe.wait_ge(qk_rd, i * NT + NT)
                            pe.wait_ge(v_ev, i * NT + NT)
                            pe.wait_ge(qT_ok, i * NT + NT)
                            pe.wait_ge(kT_ok, i * NT + NT)
                        sp_ = ps[:, 2 * g:2 * g + 2].rearrange("p a (h k) -> p (a h) k", k=2 * P)
                        for h in range(4):
                            ins = te.matmul(sp_[:, h, lo:], qT[64 * g:64 * g + 64, h, t * P:(t + 1) * P],
                                            kT[64 * g:64 * g + 64, h, t * P - P + lo:(t + 1) * P], start=True, stop=True)
                        ins.then_inc(s_mm, 1)

                    def project(t):
                        pe.wait_ge(o_ok, i * U + 2 * t + 2)
                        if t:
                            pe.wait_ge(xm_ok, i * NT + t)
                        flat = ot[:, t % 2].rearrange("p c g v -> p (c g v)")
                        for c in range(NC):
                            ins = te.transpose(ps[:, 7, c * P:(c + 1) * P], flat[:, c * P:(c + 1) * P], ident[:])
                        ins.then_inc(oT_mm, 1)
                        pe.wait_ge(oT_ok, i * NT + t + 1)
                        for c in range(NC):
                            ins = te.matmul(ps[:, 7, 0:D], oT[:, c], wo[:, c], start=(c == 0), stop=(c == NC - 1))
                        ins.then_inc(wo_mm, 1)

                    scores(0)
                    scores(1)
                    for u in range(U):
                        t, g = u // 2, u % 2
                        k0 = 1 if t == 0 else 0
                        pe.wait_ge(p_ok, i * U + u + 1)
                        if u:
                            pe.wait_ge(pT_a, i * U + u)
                            pe.wait_ge(pT_v, i * U + u)
                        for h in range(4):
                            for k in range(k0, 2):
                                ins = te.transpose(ps[:, 4 + h // 2, (h % 2 * 2 + k) * P:(h % 2 * 2 + k + 1) * P],
                                                   pr[:, g, h, k * P:(k + 1) * P], ident[:])
                        ins.then_inc(pT_mm, 1)
                        if u + 2 < U:
                            scores(u + 2)
                        pe.wait_ge(pT_a, i * U + u + 1)
                        pe.wait_ge(pT_v, i * U + u + 1)
                        if u:
                            pe.wait_ge(o_ok, i * U + u)
                        for h in range(4):
                            for k in range(k0, 2):
                                c0 = (2 * h + g) * DH
                                ins = te.matmul(ps[:, 6, g * 256 + h * DH:g * 256 + (h + 1) * DH], pT[:, h, k],
                                                vt[:, t - 1 + k, c0:c0 + DH], start=(k == k0), stop=(k == 1))
                        ins.then_inc(pv_mm, 1)
                        if g == 0 and t:
                            project(t - 1)
                    project(NT - 1)
                    for t in range(NT):
                        pe.wait_ge(xn_ok, i * NT + t + 1)
                        for c in range(KD):
                            ins = te.transpose(ps[:, 4 + c, t * P:(t + 1) * P], xn[:, t, c * P:(c + 1) * P], ident[:])
                    ins.then_inc(xn_mm, 1)
                    pe.wait_ge(xnT_ok, i + 1)
                    for m in range(MH):
                        n = P if m < MH - 1 else LAST
                        if m >= 2:
                            pe.wait_ge(h2_ok, i * MH + m - 1)
                        for part, bank in ((1, m % 2), (0, 2 + m % 2)):
                            for k in range(KD):
                                ins = te.matmul(ps[0:n, bank], w1[:, k, part * HID + m * P:part * HID + m * P + n], xnT[:, k],
                                                start=(k == 0), stop=(k == KD - 1))
                        ins.then_inc(g_mm, 1)
                    pe.wait_ge(h2_ok, i * MH + MH)
                    pe.wait_ge(xm_ok, i * NT + NT)
                    for t in range(NT):
                        if t >= 2:
                            pe.wait_ge(y_ok, i * NT + t - 1)
                        for m in range(MH):
                            n = P if m < MH - 1 else LAST + 1
                            ins = te.matmul(ps[:, 6 + t % 2, 0:D], h2T[0:n, m, t * P:(t + 1) * P], w2[0:n, m],
                                            start=(m == 0), stop=(m == MH - 1))
                        ins.then_inc(y_mm, 1)

        @block.gpsimd
        def _(pool):
            g = nc.gpsimd
            g.memset(mhalf[:], -0.5).then_inc(mh_ok, 1)
            pool.wait_ge(mh_ok, 1)
            with pool.Fori(0, NL * B) as i:
                for t in range(NT):
                    pool.wait_ge(n2_ok, i * (NT + 1) + t + 1)
                    g.tensor_tensor(n2[:, 1], n2[:, 0], mhalf[:], ALU.pow).then_inc(nr_ok, 1)
                pool.wait_ge(n2_ok, (i + 1) * (NT + 1))
                g.tensor_tensor(ve[:, 1], ve[:, 0], mhalf[:, 0:NT], ALU.pow).then_inc(nr_ok, 1)


def _chunks(w):
    k, n = w.shape
    return np.ascontiguousarray(w.reshape(k // P, P, n).transpose(1, 0, 2))


def _tokens_mask():
    m = np.ones((5, L), np.float32)
    m[1, L // 3:2 * (L // 3)] = 0
    m[2, :L // 3] = 0
    return m


def lay_out(i):
    g = {}
    g["x"] = i["x"]
    g["xT"] = np.ascontiguousarray(i["x"].reshape(B, L, KD, P).transpose(0, 3, 2, 1))
    g["condT"] = np.ascontiguousarray(i["cond_1024"].reshape(B, KD, P).transpose(2, 1, 0))
    g["gate_w"] = _chunks(i["L0_cond_gate_w"])
    g["gate_b"] = i["L0_cond_gate_b"][None]
    g["time_w"] = _chunks(i["L0_cond_time_w"])
    g["time_b"] = i["L0_cond_time_b"][None]
    g["ident"] = np.eye(P, dtype=np.float32)
    g["ew1"] = np.stack([_chunks(w) for w in i["L0_cond_ew1"]])
    g["ew2"] = np.stack([_chunks(w) for w in i["L0_cond_ew2"]])
    g["eb1"] = np.ascontiguousarray(i["L0_cond_eb1"].reshape(4, 8, P).transpose(0, 2, 1))
    g["sw1"] = _chunks(i["L0_cond_sw1"])
    g["sw2"] = _chunks(i["L0_cond_sw2"])
    g["sb1"] = np.ascontiguousarray(i["L0_cond_sb1"].reshape(8, P).T)
    g["eb2"] = np.concatenate([i["L0_cond_eb2"], i["L0_cond_sb2"][None]])
    g["mask5"] = _tokens_mask()
    order = [0, 2, 4, 6, 1, 3, 5, 7]
    g["wq"], g["wk"], g["wv"] = (_chunks(i[f"L0_attn_W{n}"]) for n in "qkv")
    g["wo"] = _chunks(i["L0_attn_Wo"].reshape(8, 64, D)[order].reshape(512, D))
    g["betas"] = np.ascontiguousarray(np.broadcast_to(i["L0_attn_betas"].reshape(8, 64)[order].reshape(1, 512), (P, 512)))
    c2 = {k[9:]: v for k, v in i.items() if k.startswith("L0_cond2_")}
    g["wada"], g["bada"] = _chunks(c2["w_ada"]), c2["b_ada"][None]
    g["bwqkv"] = _chunks(np.concatenate([c2["w_q"], c2["w_k"], c2["w_v"]], 1))
    g["bqkv"] = np.broadcast_to(np.concatenate([c2["b_q"], c2["b_k"], c2["b_v"]]), (P, 3 * D))
    g["bwo"], g["wf1"], g["wf2"] = (_chunks(c2[n]) for n in ("w_o", "w_f1", "w_f2"))
    g["bo"], g["bf2"] = (np.broadcast_to(c2[n], (P, D)) for n in ("b_o", "b_f2"))
    g["bf1"] = np.ascontiguousarray(c2["b_f1"].reshape(8, P).T)
    def pad(v, n=6 * P):
        return np.concatenate([v, np.zeros((n - v.shape[0],) + v.shape[1:], v.dtype)])

    hid = i["L0_ffn_w2"].shape[1]
    g["wqkv"] = np.stack([_chunks(w) for w in i["L0_ffn_wqkv"]])
    g["wwo"] = np.stack([_chunks(w) for w in i["L0_ffn_wo"]])
    g["w1"] = np.stack([_chunks(w) for w in i["L0_ffn_w1"]])
    g["b1"] = np.stack([np.stack([pad(v[:hid]).reshape(6, P).T, pad(v[hid:]).reshape(6, P).T], 1) for v in i["L0_ffn_b1"]])
    g["w2"] = np.stack([_chunks(pad(np.concatenate([w, v[None]]))) for w, v in zip(i["L0_ffn_w2"], i["L0_ffn_b2"])])
    g["lnp"] = np.stack([np.stack([w.reshape(2, P).T, v.reshape(2, P).T], 1) for w, v in zip(i["L0_ffn_ln_g"], i["L0_ffn_ln_b"])])
    qk = np.stack([i["L0_ffn_q_scale"], i["L0_ffn_k_scale"]], 1)
    qk = np.stack([qk, np.roll(qk, 32, axis=2)], 1).reshape(2, 1, 2, 128)
    g["qks"] = np.broadcast_to(qk, (2, P, 2, 128))
    g.update(_window_constants())
    return g


def _window_constants():
    f = np.float32
    half = np.arange(0, 64, 2, dtype=f)
    inv_freq = (f(1.0) / f(10000.0) ** (half / f(64))).astype(f)
    t = np.arange(L, dtype=f)
    freqs = t[:, None] * inv_freq[None]
    freqs = np.concatenate([freqs, freqs], -1)
    base = (half + f(0.4 * 64)) / f(1.4 * 64)
    scale = base[None] ** ((t - L // 2) / f(64))[:, None]
    scale = np.concatenate([scale, scale], -1).astype(f)
    sign = np.concatenate([-np.ones(32, f), np.ones(32, f)])
    cos, sin = np.cos(freqs), np.sin(freqs) * sign
    rot = np.stack([np.stack([cos * scale, cos / scale], 1), np.stack([sin * scale, sin / scale], 1)])
    rot = rot.reshape(2, NT, P, 2, 64).transpose(2, 0, 1, 3, 4).astype(f)
    q, k = np.arange(P)[:, None], np.arange(P)[None]
    mask = np.concatenate([np.where(k >= q, 0, -1e30), np.where(k <= q, 0, -1e30)], 1).astype(f)
    return {"rot": np.ascontiguousarray(rot), "wmask": mask, "last": np.broadcast_to(np.array([[0, 1]], f), (P, 2))}


STAGES = "123"


def program(nc, io, out):
    x1 = nc.dram_tensor("x1", (B, L, D), F32, kind="Internal").ap() if "x1" not in io else io["x1"]
    xs = nc.dram_tensor("xs", (3 * B, L, D), F32, kind="Internal").ap() if "xs" not in io else io["xs"]
    if "1" in STAGES:
        moe_attention(nc, io, x1)
    if "2" in STAGES:
        ball_block(nc, io, x1, xs)
    if "3" in STAGES:
        window_layers(nc, io, xs, x1, out)


def kernel(**inputs):
    import concourse.bacc as bacc
    from concourse.bass_utils import run_bass_kernel_spmd

    nc = bacc.Bacc("TRN2", target_bir_lowering=False, num_devices=1)
    arrays = {f"in_{k}": np.ascontiguousarray(v) for k, v in lay_out({k: np.asarray(v) for k, v in inputs.items()}).items()}
    io = {k[3:]: nc.dram_tensor(k, v.shape, mybir.dt.from_np(v.dtype), kind="ExternalInput").ap() for k, v in arrays.items()}
    out = nc.dram_tensor("out_x", (B, L, D), F32, kind="ExternalOutput").ap()
    program(nc, io, out)
    r = run_bass_kernel_spmd(nc, [arrays], core_ids=[0])
    return r.results[0]["out_x"]
```

```python
import math
from contextlib import ExitStack

import numpy as np

import concourse.bass as bass
from concourse import mybir

F32 = mybir.dt.float32
I32 = mybir.dt.int32
BF16 = mybir.dt.bfloat16
ALU = mybir.AluOpType
ACT = mybir.ActivationFunctionType
AX = mybir.AxisListType

P = 128
B = 8
L = 512
D = 256
KD = D // P
NT = L // P


class Chain:

    def __init__(self, eng, sem, base=0):
        self.eng, self.sem, self.base, self.n = eng, sem, base, 0

    def mark(self, ins):
        ins.then_inc(self.sem, 1)
        self.n += 1
        return self.n

    def wait(self, n):
        self.eng.wait_ge(self.sem, self.base + n)

    def link(self, ins):
        self.wait(self.mark(ins))


def moe_attention(nc, io, x1):
    E, H1 = 4, 1024
    M1 = H1 // P
    LH = L // 3
    SEGS = [(0, LH), (LH, 2 * LH), (2 * LH, L)]
    NH, DH = 8, 64
    SEG = 64
    NSEG = L // SEG
    NC = NH * DH // P
    J = 3 * M1
    VA = DH + 1

    with ExitStack() as ctx:
        def sb(name, shape, dt=F32):
            return ctx.enter_context(nc.sbuf_tensor(name, shape, dt))

        def sem(name):
            return ctx.enter_context(nc.semaphore(name))

        sw1 = sb("sw1", [P, KD, H1])
        sw2 = sb("sw2", [P, M1, D])
        wq = sb("wq", [P, KD, NC * P])
        wk = sb("wk", [P, KD, NC * P])
        wv = sb("wv", [P, KD, NC * P])
        wo = sb("wo", [P, NC, D])
        sb1 = sb("sb1", [P, M1])
        eb2 = sb("eb2", [E + 1, D])
        mask5 = sb("mask5", [E + 1, L])
        ident = sb("ident", [P, P])
        gate = sb("gate", [P, NC * P])
        gate1 = sb("gate1", [P, NC * P])
        rw1 = sb("rw1", [P, 2, KD, H1])
        rw2 = sb("rw2", [P, 2, M1, D])
        rb1 = sb("rb1", [P, 2, M1])
        condT = sb("condT", [P, KD, B])
        gwt = sb("gwt", [P, 3 * KD, E])
        gbt = sb("gbt", [1, E])
        twt = sb("twt", [P, KD, 2 * E])
        tbt = sb("tbt", [1, 2 * E])
        ones = sb("ones", [E, P])
        sums = sb("sums", [P, 3, KD, B])
        gin = sb("gin", [P, 3, KD, B])
        sil = sb("sil", [P, 2, KD, B])
        lg = sb("lg", [B, 16, E])
        col = sb("col", [B, 16])
        cnt = sb("cnt", [B, 2, E])
        junk = sb("junk", [B, 2, E])
        ohw = sb("ohw", [B, 2, E])
        idx = sb("idx", [B, 2], I32)
        idxrow = sb("idxrow", [1, 2 * B], I32)
        slotw = sb("slotw", [E, 2, B])
        w5 = sb("w5", [E + 1, B])
        wcol = sb("wcol", [E, 2, P])
        wm5 = sb("wm5", [E + 1, L])
        xT = sb("xT", [P, KD, L])
        hid = sb("hid", [P, 3, L])
        cT = sb("cT", [P, KD, L])
        qT = sb("qT", [P, NC, L])
        sqT = sb("sqT", [P, NC, L])
        kT = sb("kT", [P, NC, L])
        ktok = sb("ktok", [P, NT, NC * P])
        sk = sb("sk", [P, NT, NC * P])
        vtok = sb("vtok", [P, NT, NH, VA])
        neg = sb("neg", [P, 2, L])
        mem = sb("mem", [P, NSEG, NC, VA])
        xres = sb("xres", [P, NT, D])
        shifted = sb("shifted", [P, 2, 4, SEG])
        prob = sb("prob", [P, NH + 1, SEG])
        rs9 = sb("rs9", [P, NH + 1])
        pT = sb("pT", [P, NH, P])
        att = sb("att", [P, 2, NC * P])
        attm = sb("attm", [P, NC * P])
        attT = sb("attT", [P, NC, P])
        mx = sb("mx", [P, 2, 4])
        rsum = sb("rsum", [P, 2, 4])
        rden = sb("rden", [P, 2, 4])
        x1t = sb("x1t", [P, 2, D])

        ps = ctx.enter_context(nc.psum_tensor("ps", [P, 8, 512], F32))
        s_ps = ps[:, 2:4, 0:256].rearrange("p a (c k) -> p a c k", k=SEG)
        pT_ps = ps[:, 6:8, :].rearrange("p a (h q) -> p (a h) q", q=P)
        pv_ps = ps[:, 4, :]
        am_ps = [ps[:, 5, 0:NC * VA].rearrange("p (c v) -> p c v", v=VA),
                 ps[:, 1, 0:NC * VA].rearrange("p (c v) -> p c v", v=VA)]
        aT_ps = ps[:, 0, :].rearrange("p (k q) -> p k q", q=P)
        wo_ps = ps[:, 0, 0:D]

        ld_route = sem("ld_route")
        ld_w = sem("ld_w")
        ld_xs = sem("ld_xs")
        ld_x = sem("ld_x")
        ld_res = sem("ld_res")
        ld_r = [sem("ld_r0"), sem("ld_r1")]
        st_idx = sem("st_idx")
        st_x1 = [sem("st_x1a"), sem("st_x1b")]
        summed = sem("summed")
        v_c = sem("v_c")
        v_l = sem("v_l")
        a_pre = sem("a_pre")
        gin_ok = sem("gin_ok")
        sil_ok = sem("sil_ok")
        lg_ps = sem("lg_ps")
        lg_ex = sem("lg_ex")
        idx_ok = sem("idx_ok")
        ohw_ok = sem("ohw_ok")
        ohwT = sem("ohwT")
        slot_ok = sem("slot_ok")
        wcol_ok = sem("wcol_ok")
        wmb_ok = sem("wmb_ok")
        h_mm = sem("h_mm")
        h_act = sem("h_act")
        h_w = sem("h_w")
        o_mm = sem("o_mm")
        c_act = sem("c_act")
        c_dve = sem("c_dve")
        pp_mm = sem("pp_mm")
        pp_ev = sem("pp_ev")
        mn_ok = sem("mn_ok")
        ex_ok = sem("ex_ok")
        fm_ok = sem("fm_ok")
        u_mm = sem("u_mm")
        mem_ok = sem("mem_ok")
        s_mm = sem("s_mm")
        s_sub = sem("s_sub")
        sum_ok = sem("sum_ok")
        p_ok = sem("p_ok")
        pT_mm = sem("pT_mm")
        pT_a = sem("pT_a")
        pT_v = sem("pT_v")
        am_mm = sem("am_mm")
        pv_mm = sem("pv_mm")
        att_ok = sem("att_ok")
        aT_mm = sem("aT_mm")
        aT_ok = sem("aT_ok")
        wo_mm = sem("wo_mm")
        x1_ok = sem("x1_ok")

        block = ctx.enter_context(nc.Block())

        @block.sync
        def _(sp):
            for dst, name in ((condT, "condT"), (gwt, "gate_w"), (gbt, "gate_b"), (twt, "time_w"),
                              (tbt, "time_b"), (ident, "ident")):
                sp.dma_start(dst[:], io[name]).then_inc(ld_route, 16)
            with sp.Fori(0, B) as b:
                sp.wait_ge(summed, b)
                sp.dma_start(xT[:], io["xT"][bass.ds(b, 1)].rearrange("a p c l -> p (a c) l")).then_inc(ld_xs, 16)
            for dst, name in ((sw1, "sw1"), (sw2, "sw2"), (wq, "wq"), (wk, "wk"), (wv, "wv"), (wo, "wo"),
                              (sb1, "sb1"), (eb2, "eb2"), (mask5, "mask5"), (gate, "betas")):
                sp.dma_start(dst[:], io[name]).then_inc(ld_w, 16)
            sp.wait_ge(idx_ok, 1)
            sp.dma_start(idxrow[:], idx[:]).then_inc(st_idx, 16)
            sp.wait_ge(st_idx, 16)
            with sp.Fori(0, B) as b:
                for r in range(2):
                    e = sp.value_load(idxrow[0:1, bass.ds(b * 2 + r, 1)], min_val=0, max_val=E - 1)
                    if r == 0:
                        sp.wait_ge(o_mm, b * J)
                    sp.dma_start(rw1[:, r], io["ew1"][bass.ds(e, 1)].rearrange("a p k n -> p (a k) n")).then_inc(ld_r[r], 16)
                    sp.dma_start(rw2[:, r], io["ew2"][bass.ds(e, 1)].rearrange("a p k n -> p (a k) n")).then_inc(ld_r[r], 16)
                    sp.dma_start(rb1[:, r], io["eb1"][bass.ds(e, 1)].rearrange("a p m -> p (a m)")).then_inc(ld_r[r], 16)
                sp.dma_start(xT[:], io["xT"][bass.ds(b, 1)].rearrange("a p c l -> p (a c) l")).then_inc(ld_x, 16)
                sp.wait_ge(x1_ok, b * NT)
                sp.dma_start(xres[:], io["x"][bass.ds(b, 1)].rearrange("a (t p) d -> p (a t) d", p=P)).then_inc(ld_res, 16)
                for t in range(NT):
                    sp.wait_ge(x1_ok, b * NT + t + 1)
                    sp.dma_start(x1[bass.ds(b, 1)].rearrange("a (t p) d -> t p (a d)", p=P)[t], x1t[:, t % 2]).then_inc(st_x1[t % 2], 16)
            for s in st_x1:
                sp.wait_ge(s, 16 * B * NT // 2)

        @block.gpsimd
        def _(pool):
            pass

        @block.scalar
        def _(act):
            a = nc.scalar
            act.wait_ge(ld_route, 6 * 16)
            a.activation(sil[:, 0], condT[:], ACT.Exp, scale=-1.0).then_inc(a_pre, 1)
            act.wait_ge(lg_ex, 1)
            a.activation(lg[:, 5, :], lg[:, 4, :], ACT.Exp).then_inc(a_pre, 1)
            act.wait_ge(ld_w, 10 * 16)
            a.activation(gate1[:], gate[:], ACT.Exp, scale=-1.0).then_inc(a_pre, 1)
            with act.Fori(0, B) as b:
                for j in range(J):
                    act.wait_ge(h_mm, b * J + j + 1)
                    if j == 0:
                        act.wait_ge(ld_r[0], b * 48 + 48)
                    if j == M1:
                        act.wait_ge(ld_r[1], b * 48 + 48)
                    if j >= 3:
                        act.wait_ge(o_mm, b * J + j - 2)
                    bias = rb1[:, j // M1, j % M1:j % M1 + 1] if j < 2 * M1 else sb1[:, j % M1:j % M1 + 1]
                    a.activation(hid[:, j % 3], ps[:, j % 2], ACT.Gelu_apprx_tanh, bias=bias).then_inc(h_act, 1)
                act.wait_ge(o_mm, b * J + J)
                a.activation(cT[:, 0], ps[:, 2], ACT.Copy).then_inc(c_act, 1)

                n_ex = 0

                def feature_exp():
                    nonlocal n_ex
                    act.wait_ge(mn_ok, b * 8 + n_ex + 1)
                    ins = a.activation(neg[:, n_ex % 2], neg[:, n_ex % 2], ACT.Exp)
                    ins.then_inc(ex_ok, 1)
                    n_ex += 1

                for n in range(16):
                    act.wait_ge(pp_mm, b * 16 + n + 1)
                    if n < 4:
                        src, dst = ps[:, n % 2], qT[:, n]
                    elif n < 12 and n % 2 == 0:
                        src, dst = ps[:, n % 2], ktok[:, (n - 4) // 2]
                    elif n < 12:
                        src = ps[:, n % 2].rearrange("p (h v) -> p h v", v=DH)
                        dst = vtok[:, (n - 4) // 2, :, 0:DH]
                    else:
                        src = ps[:, n % 2].rearrange("p (c q) -> p c q", q=P)
                        dst = kT[:, :, (n - 12) * P:(n - 11) * P]
                    a.activation(dst, src, ACT.Copy).then_inc(pp_ev, 1)
                    if n in (1, 2, 3, 4, 6, 8, 10, 12):
                        feature_exp()
                for t in range(NT):
                    act.wait_ge(s_sub, b * NT + t + 1)
                    if t:
                        act.wait_ge(sum_ok, b * NT + t)
                    for s in range(2):
                        r = slice(64 * s, 64 * s + 64)
                        ins = a.activation(prob[r, s:s + NH], shifted[r].rearrange("p a c k -> p (a c) k"), ACT.Exp, scale=DH ** -0.5)
                    ins.then_inc(p_ok, 1)
                    act.wait_ge(pT_mm, b * NT + t + 1)
                    if t:
                        act.wait_ge(pv_mm, b * NT + t)
                    a.activation(pT[0:64, :, 0:64], pT_ps[0:64, :, 0:64], ACT.Copy).then_inc(pT_a, 1)
                    if t >= 1:
                        act.wait_ge(aT_mm, b * NT + t)
                        if t >= 2:
                            act.wait_ge(wo_mm, b * NT + t - 1)
                        a.activation(attT[:], aT_ps, ACT.Copy).then_inc(aT_ok, 1)
                act.wait_ge(aT_mm, b * NT + NT)
                act.wait_ge(wo_mm, b * NT + NT - 1)
                a.activation(attT[:], aT_ps, ACT.Copy).then_inc(aT_ok, 1)

        @block.vector
        def _(dve):
            v = nc.vector
            ch = Chain(dve, v_c)
            v.memset(ones[:], 1.0).then_inc(slot_ok, 1)
            ch.mark(v.memset(mem[:, 0], 0.0))
            ch.mark(v.memset(pT[:], 0.0))
            ch.mark(v.memset(prob[:], 0.0))
            ch.mark(v.memset(vtok[:], 1.0))
            ch.link(v.memset(w5[:], 1.0))
            ch.link(v.memset(mem[:, 0, :, DH:VA], 1.0 / DH))
            with dve.Fori(0, B) as b:
                dve.wait_ge(ld_xs, b * 16 + 16)
                for s, (lo, hi) in enumerate(SEGS):
                    ins = v.tensor_reduce(sums[:, s, :, bass.ds(b, 1)].rearrange("p c a -> p (c a)"), xT[:, :, lo:hi], AX.X, ALU.add)
                ins.then_inc(summed, 1)
            dve.wait_ge(summed, B)
            ch.link(v.tensor_tensor(gin[:, 1], sums[:, 0], sums[:, 2], ALU.add))
            ch.link(v.tensor_tensor(gin[:, 2], sums[:, 1], sums[:, 2], ALU.add))
            ch.link(v.tensor_tensor(gin[:, 0], gin[:, 1], sums[:, 1], ALU.add))
            ch.link(v.tensor_scalar(gin[:, 0], gin[:, 0], 1.0 / L, None, ALU.mult))
            ch.link(v.tensor_scalar(gin[:, 1:3], gin[:, 1:3], 1.0 / (L - LH), None, ALU.mult))
            dve.wait_ge(a_pre, 1)
            ch.link(v.tensor_scalar(sil[:, 0], sil[:, 0], 1.0, None, ALU.add))
            ch.link(v.reciprocal(sil[:, 0], sil[:, 0]))
            v.tensor_tensor(sil[:, 1], sil[:, 0], condT[:], ALU.mult).then_inc(gin_ok, 1)
            dve.wait_ge(lg_ps, 1)
            ch.link(v.tensor_scalar(lg[:, 0], ps[0:B, 4, 8:8 + E], 1.0, None, ALU.add))
            ch.link(v.tensor_tensor(lg[:, 1], lg[:, 0], ps[0:B, 4, 0:E], ALU.mult))
            ch.link(v.tensor_tensor(lg[:, 2], lg[:, 1], ps[0:B, 4, 8 + E:8 + 2 * E], ALU.add))
            ch.link(v.tensor_reduce(col[:, 0:1], lg[:, 2], AX.X, ALU.max))
            v.tensor_scalar(lg[:, 4], lg[:, 2], col[:, 0:1], None, ALU.subtract).then_inc(lg_ex, 1)
            dve.wait_ge(a_pre, 2)
            ch.link(v.tensor_reduce(col[:, 1:2], lg[:, 5], AX.X, ALU.add))
            ch.link(v.reciprocal(col[:, 2:3], col[:, 1:2]))
            sc = lg[:, 6]
            ch.link(v.tensor_scalar(sc, lg[:, 5], col[:, 2:3], None, ALU.mult))
            for e in range(E):
                ch.link(v.tensor_scalar(lg[:, 7], sc, lg[:, 6, e:e + 1], None, ALU.is_gt))
                if e:
                    ch.link(v.tensor_scalar(lg[:, 7, 0:e], lg[:, 6, 0:e], lg[:, 6, e:e + 1], None, ALU.is_ge))
                ch.link(v.tensor_reduce(lg[:, 8, e:e + 1], lg[:, 7], AX.X, ALU.add))
            ch.link(v.memset(lg[:, 9, 0:1], 0.0))
            for e in range(1, E):
                ch.link(v.memset(lg[:, 9, e:e + 1], float(e)))
            for r in range(2):
                ch.link(v.tensor_scalar(cnt[:, r], lg[:, 8], float(r), None, ALU.is_equal))
                ch.link(v.tensor_tensor(junk[:, r], cnt[:, r], sc, ALU.mult))
                ch.link(v.tensor_reduce(col[:, 4 + r:5 + r], junk[:, r], AX.X, ALU.add))
                ch.link(v.tensor_tensor(lg[:, 10], cnt[:, r], lg[:, 9], ALU.mult))
                ch.link(v.tensor_reduce(col[:, 6 + r:7 + r], lg[:, 10], AX.X, ALU.add))
            v.tensor_copy(idx[:], col[:, 6:8]).then_inc(idx_ok, 1)
            ch.link(v.tensor_tensor(col[:, 8:9], col[:, 4:5], col[:, 5:6], ALU.add))
            ch.link(v.tensor_scalar(col[:, 8:9], col[:, 8:9], 1e-8, None, ALU.add))
            ch.link(v.reciprocal(col[:, 9:10], col[:, 8:9]))
            v.tensor_scalar(ohw[:], junk[:], col[:, 9:10], None, ALU.mult).then_inc(ohw_ok, 1)
            dve.wait_ge(ohwT, 1)
            ch.link(v.tensor_copy(slotw[:], ps[0:E, 5, 0:2 * B].rearrange("p (r b) -> p r b", r=2)))
            ch.link(v.tensor_tensor(w5[0:E], slotw[:, 0], slotw[:, 1], ALU.add))
            dve.wait_ge(a_pre, 3)
            ch.link(v.tensor_scalar(gate[:], gate1[:], 1.0, None, ALU.add))
            ch.link(v.reciprocal(gate[:], gate[:]))
            ch.link(v.tensor_scalar(gate1[:], gate[:], -1.0, 1.0, ALU.mult, ALU.add))

            LINKS = 5 * NT - 0
            with dve.Fori(0, B) as b:
                lc = Chain(dve, v_l, b * LINKS)
                dve.wait_ge(o_mm, b * J)
                for r in range(2):
                    v.tensor_scalar(wcol[:, r], ones[:], slotw[:, r, bass.ds(b, 1)], None, ALU.mult)
                v.tensor_scalar(wm5[:], mask5[:], w5[:, bass.ds(b, 1)], None, ALU.mult).then_inc(wcol_ok, 1)
                dve.wait_ge(wmb_ok, b + 1)
                for j in range(2 * M1):
                    dve.wait_ge(h_act, b * J + j + 1)
                    v.tensor_tensor(hid[:, j % 3], hid[:, j % 3], ps[:, 4 + j // M1], ALU.mult).then_inc(h_w, 1)
                dve.wait_ge(o_mm, b * J + J)
                v.tensor_copy(cT[:, 1], ps[:, 3]).then_inc(c_dve, 1)
                feats = [(qT[:, c], sqT[:, c], c + 1) for c in range(NC)] + \
                        [(ktok[:, t], sk[:, t], 5 + 2 * t) for t in range(NT)]

                def low(n):
                    dve.wait_ge(pp_ev, b * 16 + feats[n][2])
                    v.tensor_scalar(neg[:, n % 2], feats[n][0], 0.0, None, ALU.min).then_inc(mn_ok, 1)

                low(0)
                for n in range(8):
                    if n + 1 < 8:
                        if n:
                            dve.wait_ge(fm_ok, b * 8 + n)
                        low(n + 1)
                    dve.wait_ge(ex_ok, b * 8 + n + 1)
                    v.scalar_tensor_tensor(out=feats[n][1], in0=feats[n][0], scalar=0.0, in1=neg[:, n % 2],
                                           op0=ALU.max, op1=ALU.add).then_inc(fm_ok, 1)
                for n in range(NSEG - 1):
                    dve.wait_ge(u_mm, b * 7 + n + 1)
                    if n:
                        dve.wait_ge(mem_ok, b * 7 + n)
                    v.tensor_tensor(mem[:, n + 1], mem[:, n], ps[:, 4 + n % 2, 0:NC * VA].rearrange("p (c v) -> p c v", v=VA),
                                    ALU.add).then_inc(mem_ok, 1)

                def finish(t):
                    dve.wait_ge(wo_mm, b * NT + t + 1)
                    dve.wait_ge(st_x1[t % 2], b * 32 + 16 * (t // 2))
                    v.tensor_tensor(x1t[:, t % 2], xres[:, t], wo_ps, ALU.add).then_inc(x1_ok, 1)

                dve.wait_ge(ld_res, b * 16 + 16)
                for t in range(NT):
                    dve.wait_ge(s_mm, b * NT + t + 1)
                    lc.link(v.tensor_reduce(mx[:], s_ps, AX.X, ALU.max))
                    v.tensor_tensor(shifted[:], s_ps, mx[:].unsqueeze(3).broadcast_to([P, 2, 4, SEG]), ALU.subtract).then_inc(s_sub, 1)
                    if t >= 2:
                        finish(t - 2)
                    dve.wait_ge(p_ok, b * NT + t + 1)
                    v.tensor_reduce(rs9[:], prob[:], AX.X, ALU.add).then_inc(sum_ok, 1)
                    dve.wait_ge(sum_ok, b * NT + t + 1)
                    for s in range(2):
                        r = slice(64 * s, 64 * s + 64)
                        v.reciprocal(rsum[r], rs9[r, s:s + NH].rearrange("p (a c) -> p a c", a=2))
                    dve.wait_ge(pT_mm, b * NT + t + 1)
                    if t:
                        dve.wait_ge(pv_mm, b * NT + t)
                    v.tensor_copy(pT[64:128, :, 64:128], pT_ps[64:128, :, 64:128]).then_inc(pT_v, 1)
                    dve.wait_ge(am_mm, b * NT + t + 1)
                    v.reciprocal(rden[:, 0], am_ps[0][:, :, DH])
                    lc.link(v.reciprocal(rden[:, 1], am_ps[1][:, :, DH]))
                    am = attm[:].rearrange("p (a c v) -> p a c v", a=2, v=DH)
                    for par in range(2):
                        ins = v.tensor_tensor(am[:, par], am_ps[par][:, :, 0:DH],
                                              rden[:, par].unsqueeze(2).broadcast_to([P, 4, DH]), ALU.mult)
                    lc.link(ins)
                    lc.link(v.tensor_tensor(attm[:], attm[:], gate[:], ALU.mult))
                    dve.wait_ge(pv_mm, b * NT + t + 1)
                    if t >= 2:
                        dve.wait_ge(aT_mm, b * NT + t - 1)
                    o = att[:, t % 2].rearrange("p (h v) -> p h v", v=DH)
                    lc.link(v.tensor_tensor(o, pv_ps.rearrange("p (h v) -> p h v", v=DH),
                                            rsum[:].rearrange("p a c -> p (a c)").unsqueeze(2).broadcast_to([P, NH, DH]), ALU.mult))
                    v.tensor_tensor(att[:, t % 2], att[:, t % 2], gate1[:], ALU.mult).then_inc(att_ok, 1)
                    dve.wait_ge(att_ok, b * 2 * NT + 2 * t + 1)
                    v.tensor_tensor(att[:, t % 2], att[:, t % 2], attm[:], ALU.add).then_inc(att_ok, 1)
                finish(NT - 2)
                finish(NT - 1)
                assert lc.n == LINKS, lc.n

        @block.tensor
        def _(pe):
            te = nc.tensor
            pe.wait_ge(ld_route, 6 * 16)
            pe.wait_ge(gin_ok, 1)
            pe.wait_ge(slot_ok, 1)
            g = gin[:].rearrange("p s c b -> p (s c) b")
            for k in range(3 * KD):
                te.matmul(ps[0:B, 4, 0:E], g[:, k], gwt[:, k], start=(k == 0), stop=False)
            te.matmul(ps[0:B, 4, 0:E], ones[0:1, 0:B], gbt[:], start=False, stop=True)
            for k in range(KD):
                te.matmul(ps[0:B, 4, 8:8 + 2 * E], sil[:, 1, k], twt[:, k], start=(k == 0), stop=False)
            te.matmul(ps[0:B, 4, 8:8 + 2 * E], ones[0:1, 0:B], tbt[:], start=False, stop=True).then_inc(lg_ps, 1)
            pe.wait_ge(ohw_ok, 1)
            for r in range(2):
                ins = te.transpose(ps[0:E, 5, r * B:(r + 1) * B], ohw[:, r], ident[0:B, 0:B])
            ins.then_inc(ohwT, 1)
            pe.wait_ge(ld_w, 10 * 16)

            with pe.Fori(0, B) as b:
                pe.wait_ge(wcol_ok, b + 1)
                pe.wait_ge(x1_ok, b * NT)
                pe.wait_ge(aT_ok, b * NT)
                for r in range(2):
                    ins = te.matmul(ps[:, 4 + r], wcol[:, r], mask5[0:E], start=True, stop=True)
                ins.then_inc(wmb_ok, 1)
                for c in range(KD):
                    te.matmul(ps[:, 2 + c], eb2[:, c * P:(c + 1) * P], wm5[:], start=True, stop=False)
                pe.wait_ge(ld_x, b * 16 + 16)

                def second(j):
                    if j < 2 * M1:
                        pe.wait_ge(h_w, b * 2 * M1 + j + 1)
                    else:
                        pe.wait_ge(h_act, b * J + j + 1)
                    w2 = rw2[:, j // M1] if j < 2 * M1 else sw2
                    for c in range(KD):
                        ins = te.matmul(ps[:, 2 + c], w2[:, j % M1, c * P:(c + 1) * P], hid[:, j % 3],
                                        start=False, stop=(j == J - 1))
                    ins.then_inc(o_mm, 1)

                for j in range(J):
                    if j < 2 * M1 and j % M1 == 0:
                        pe.wait_ge(ld_r[j // M1], b * 48 + 48)
                    if j >= 2:
                        pe.wait_ge(h_act, b * J + j - 1)
                    w1 = rw1[:, j // M1] if j < 2 * M1 else sw1
                    for k in range(KD):
                        ins = te.matmul(ps[:, j % 2], w1[:, k, j % M1 * P:(j % M1 + 1) * P], xT[:, k],
                                        start=(k == 0), stop=(k == KD - 1))
                    ins.then_inc(h_mm, 1)
                    if j:
                        second(j - 1)
                second(J - 1)

                pe.wait_ge(c_act, b + 1)
                pe.wait_ge(c_dve, b + 1)
                for n in range(16):
                    if n >= 2:
                        pe.wait_ge(pp_ev, b * 16 + n - 1)
                    if n < 4:
                        for k in range(KD):
                            ins = te.matmul(ps[:, n % 2], wq[:, k, n * P:(n + 1) * P], cT[:, k],
                                            start=(k == 0), stop=(k == KD - 1))
                    elif n < 12:
                        t = (n - 4) // 2
                        w = wv if n % 2 else wk
                        for k in range(KD):
                            ins = te.matmul(ps[:, n % 2], cT[:, k, t * P:(t + 1) * P], w[:, k],
                                            start=(k == 0), stop=(k == KD - 1))
                    else:
                        t = n - 12
                        for c in range(NC):
                            ins = te.transpose(ps[:, n % 2, c * P:(c + 1) * P], ktok[:, t, c * P:(c + 1) * P], ident[:])
                    ins.then_inc(pp_mm, 1)

                def scores(t):
                    for s in range(2):
                        for h in range(NH):
                            r, c = 64 * (h % 2), h // 2
                            q = slice(t * P + s * SEG, t * P + (s + 1) * SEG)
                            rows, qs = slice(64 * s, 64 * s + 64), q
                            if s == 0 and h == 0:
                                rows, qs = slice(0, P), slice(t * P, (t + 1) * P)
                            ins = te.matmul(s_ps[rows, h % 2, c], qT[r:r + 64, c, qs], kT[r:r + 64, c, q],
                                            start=True, stop=True)
                    ins.then_inc(s_mm, 1)

                def memory_read(t):
                    for s in range(2):
                        for h in range(NH):
                            r, c = 64 * (h % 2), h // 2
                            q = slice(t * P + s * SEG, t * P + (s + 1) * SEG)
                            rows, qs = slice(64 * s, 64 * s + 64), q
                            if s == 0 and h == 0:
                                rows, qs = slice(0, P), slice(t * P, (t + 1) * P)
                            ins = te.matmul(am_ps[h % 2][rows, c], sqT[r:r + 64, c, qs],
                                            mem[r:r + 64, 2 * t + s, c], start=True, stop=True)
                    ins.then_inc(am_mm, 1)

                def project(t):
                    pe.wait_ge(att_ok, b * 2 * NT + 2 * t + 2)
                    if t:
                        pe.wait_ge(x1_ok, b * NT + t)
                    for k in range(NC):
                        ins = te.transpose(aT_ps[:, k], att[:, t % 2, k * P:(k + 1) * P], ident[:])
                    ins.then_inc(aT_mm, 1)
                    pe.wait_ge(aT_ok, b * NT + t + 1)
                    for k in range(NC):
                        ins = te.matmul(wo_ps, attT[:, k], wo[:, k], start=(k == 0), stop=(k == NC - 1))
                    ins.then_inc(wo_mm, 1)

                pe.wait_ge(pp_ev, b * 16 + 16)
                scores(0)
                for n in range(NSEG - 1):
                    s, t = n % 2, n // 2
                    if n % 2 == 0:
                        pe.wait_ge(fm_ok, b * 8 + 5 + t)
                    if n >= 2:
                        pe.wait_ge(mem_ok, b * 7 + n - 1)
                    for h in range(NH):
                        r, c = 64 * (h % 2), h // 2
                        m = P if h == 0 else DH
                        ins = te.matmul(ps[r:r + m, 4 + n % 2, c * VA:(c + 1) * VA],
                                        sk[64 * s:64 * s + 64, t, h * DH:h * DH + m],
                                        vtok[64 * s:64 * s + 64, t, h], start=True, stop=True)
                    ins.then_inc(u_mm, 1)
                pe.wait_ge(mem_ok, b * 7 + 7)
                memory_read(0)
                for t in range(NT):
                    pe.wait_ge(p_ok, b * NT + t + 1)
                    if t:
                        pe.wait_ge(pT_a, b * NT + t)
                        pe.wait_ge(pT_v, b * NT + t)
                    for o in range(NH):
                        ins = te.transpose(pT_ps[:, o], prob[:, o:o + 2].rearrange("p o k -> p (o k)"), ident[:])
                    ins.then_inc(pT_mm, 1)
                    if t + 1 < NT:
                        scores(t + 1)
                    pe.wait_ge(pT_a, b * NT + t + 1)
                    pe.wait_ge(pT_v, b * NT + t + 1)
                    if t:
                        pe.wait_ge(att_ok, b * 2 * NT + 2 * t)
                    for h in range(NH):
                        o = (h % 2) * 4 + h // 2
                        ins = te.matmul(pv_ps[:, o * DH:(o + 1) * DH], pT[:, o], vtok[:, t, h, 0:DH], start=True, stop=True)
                    ins.then_inc(pv_mm, 1)
                    if t:
                        project(t - 1)
                    if t + 1 < NT:
                        pe.wait_ge(att_ok, b * 2 * NT + 2 * t + 2)
                        memory_read(t + 1)
                project(NT - 1)


def _beta(a, b):
    return math.exp(math.lgamma(a) + math.lgamma(b) - math.lgamma(a + b))


def ball_block(nc, io, x1, xs):
    NH, DH = 16, 16
    FF = 1024
    MF = FF // P
    T = B * NT
    EPS = 1e-7
    BALL = float(np.float32(1.0 - 1e-5))
    C = math.atanh(BALL)
    R = _beta(DH / 2, 0.5) / _beta(D / 2, 0.5)
    assert math.sqrt(NH) * C / R < C * 0.999
    SL = 8
    U = NT * NH
    HW = 3 * NH + 3

    with ExitStack() as outer:
        def keep(name, shape, dt=F32):
            return outer.enter_context(nc.sbuf_tensor("b_" + name, shape, dt))

        x = keep("x", [P, T, D])
        w = keep("w", [P, T, D])
        mv = keep("mv", [P, T, 2])
        cols = keep("cols", [P, 24, T])
        ident = keep("ident", [P, P])
        identb = keep("identb", [P, P], BF16)
        ones = keep("ones", [P, 8])
        expo = keep("expo", [P, 2, HW])
        rin = keep("rin", [P, HW])
        rout = keep("rout", [P, HW])
        carrier = keep("carrier", [P, 1])
        wqkv = keep("wqkv", [P, KD, 3 * D])
        bqkv = keep("bqkv", [P, 3 * D])
        wo = keep("wo", [P, KD, D])
        bo = keep("bo", [P, D])
        ld_w, ld_m, ld_g, root_ask, root_ok, ln_ask, ln_ok, v_c = (
            outer.enter_context(nc.semaphore("b_" + name)) for name in
            ("ld_w", "ld_m", "ld_g", "root_ask", "root_ok", "ln_ask", "ln_ok", "v_c"))
        NW1, NW2 = 8, 4
        ROOTS1, ROOTS2 = 2, B * (1 + NT)
        ada_dram = nc.dram_tensor("ada", (B, 6 * D), F32, kind="Internal").ap()
        SCALE1, N2, YA2, W2, XW = cols[:, 10], cols[:, 11], cols[:, 13], cols[:, 14], cols[:, 15]
        FX, FW = cols[:, 20], cols[:, 21]

        class Steps:

            def __init__(self, dve, ch, base):
                self.dve, self.v, self.ch, self.asked = dve, nc.vector, ch, base

            def ts(self, out, in0, s1, s2, op0, op1=None):
                if op1 is None:
                    self.ch.link(self.v.tensor_scalar(out, in0, s1, None, op0))
                else:
                    self.ch.link(self.v.tensor_scalar(out, in0, s1, s2, op0, op1))

            def tt(self, out, in0, in1, op):
                self.ch.link(self.v.tensor_tensor(out, in0, in1, op))

            def ask(self, src, width, low, op=ALU.max):
                self.v.tensor_scalar(rin[:, 0:width], src, low, None, op).then_inc(root_ask, 1)
                self.asked = self.asked + 1

            def answer(self):
                self.dve.wait_ge(root_ok, self.asked)

            def root(self, src, width, low, op=ALU.max):
                self.ask(src, width, low, op)
                self.answer()

            def limit(self, out, n):
                self.ts(out, rout[:, 0:n], C, 1.0, ALU.mult, ALU.min)

        def row_factors(s, st, n):
            v, c = s.v, lambda k: cols[:, k]
            for t in range(T):
                last = s.ch.mark(v.bn_stats(st[:, t], x[:, t]))
            s.ch.wait(last)
            for t in range(T):
                last = s.ch.mark(v.bn_aggr(mv[:, t], st[:, t]))
            s.ch.wait(last)
            s.tt(c(0), mv[:, :, 0], mv[:, :, 0], ALU.mult)
            s.tt(c(0), c(0), mv[:, :, 1], ALU.add)
            s.ts(N2, c(0), float(D), None, ALU.mult)
            s.root(N2, T, EPS * EPS)
            s.ts(c(1), rout[:, 0:T], 1.0, None, ALU.mult)
            s.ts(c(2), c(1), BALL, None, ALU.min)
            s.ts(c(3), c(2), -1.0, 1.0, ALU.mult, ALU.add)
            s.ch.link(v.reciprocal(c(3), c(3)))
            s.ts(c(0), c(2), 1.0, None, ALU.add)
            v.tensor_tensor(c(4), c(0), c(3), ALU.mult).then_inc(ln_ask, 1)
            s.tt(c(6), c(2), c(2), ALU.mult)
            s.ts(c(7), c(6), 1.0 / 11, 1.0 / 9, ALU.mult, ALU.add)
            for k in (7, 5, 3, 1):
                s.tt(c(7), c(7), c(6), ALU.mult)
                s.ts(c(7), c(7), 1.0 / k, None, ALU.add)
            s.ts(c(8), c(1), 0.25, None, ALU.is_lt)
            s.ch.link(v.reciprocal(c(1), c(1)))
            s.dve.wait_ge(ln_ok, n)
            s.ts(c(9), c(5), 0.5, None, ALU.mult)
            s.tt(c(9), c(9), c(1), ALU.mult)
            s.tt(c(7), c(7), c(9), ALU.subtract)
            s.tt(c(7), c(7), c(8), ALU.mult)
            s.tt(c(9), c(9), c(7), ALU.add)
            s.tt(c(0), c(9), c(9), ALU.mult)
            s.tt(c(0), c(0), mv[:, :, 1], ALU.mult)
            s.root(c(0), T, 1e-6, ALU.add)
            s.tt(SCALE1, c(9), rout[:, 0:T], ALU.mult)

        def mobius(s, th_ask, th_ok, n):
            v, c = s.v, lambda k: cols[:, k]
            s.root(YA2, T, EPS * EPS)
            s.limit(c(18), T)
            s.tt(c(0), c(18), c(18), ALU.mult)
            s.tt(c(0), c(0), W2, ALU.mult)
            s.root(c(0), T, EPS * EPS)
            v.tensor_scalar(c(16), rout[:, 0:T], 1.0, None, ALU.mult).then_inc(th_ask, 1)
            s.dve.wait_ge(th_ask, n)
            s.ch.link(v.reciprocal(c(19), c(16)))
            s.tt(c(19), c(19), c(18), ALU.mult)
            s.dve.wait_ge(th_ok, n)
            s.tt(c(19), c(19), c(17), ALU.mult)
            s.tt(c(0), c(17), c(17), ALU.mult)
            s.tt(c(1), XW, c(19), ALU.mult)
            s.ts(c(1), c(1), 2.0, 1.0, ALU.mult, ALU.add)
            s.tt(c(2), N2, c(0), ALU.mult)
            s.tt(c(2), c(2), c(1), ALU.add)
            s.ts(c(2), c(2), EPS, None, ALU.max)
            s.ch.link(v.reciprocal(c(2), c(2)))
            s.tt(c(1), c(1), c(0), ALU.add)
            s.tt(FX, c(1), c(2), ALU.mult)
            s.ts(c(3), N2, -1.0, 1.0, ALU.mult, ALU.add)
            s.tt(c(3), c(3), c(2), ALU.mult)
            s.tt(FW, c(3), c(19), ALU.mult)

        def roots(pool, exponents, base):
            for n, (width, e) in enumerate(exponents):
                pool.wait_ge(root_ask, base + n + 1)
                nc.gpsimd.tensor_tensor(rout[:, 0:width], rin[:, 0:width], expo[:, int(e < 0), 0:width],
                                        ALU.pow).then_inc(root_ok, 1)

        chained = []

        with ExitStack() as ctx:
            def sb(name, shape, dt=F32):
                return ctx.enter_context(nc.sbuf_tensor("ba_" + name, shape, dt))

            def sem(name):
                return ctx.enter_context(nc.semaphore("ba_" + name))

            wada = sb("wada", [P, KD, 6 * D])
            bada = sb("bada", [1, 6 * D])
            condT = sb("condT", [P, KD, B])
            ada = sb("ada", [B, 6 * D])
            st = sb("st", [P, T, 6])
            ps = ctx.enter_context(nc.psum_tensor("ba_ps", [P, 8, 512], F32))
            ld_x, ada_mm, ada_ok, ada_st, const_ok = (sem(n) for n in ("ld_x", "ada_mm", "ada_ok", "ada_st", "const_ok"))
            block = ctx.enter_context(nc.Block())
            @block.sync
            def _(sp):
                sp.dma_start(x[:], x1.rearrange("a (t p) d -> p (a t) d", p=P)).then_inc(ld_x, 16)
                for dst, name in ((condT, "condT"), (wada, "wada"), (bada, "bada"), (ident, "ident"),
                                  (wqkv, "bwqkv"), (bqkv, "bqkv"), (wo, "bwo"), (bo, "bo")):
                    sp.dma_start(dst[:], io[name]).then_inc(ld_w, 16)
                sp.wait_ge(ada_ok, 1)
                sp.dma_start(ada_dram, ada[:]).then_inc(ada_st, 16)
                sp.wait_ge(ada_st, 16)

            @block.gpsimd
            def _(pool):
                g = nc.gpsimd
                g.memset(expo[:, 0], 0.5).then_inc(const_ok, 1)
                g.memset(expo[:, 1], -0.5).then_inc(const_ok, 1)
                g.memset(ones[:], 1.0).then_inc(const_ok, 1)
                pool.wait_ge(const_ok, 3)
                roots(pool, [(T, 0.5), (T, -0.5)], 0)

            @block.scalar
            def _(act):
                a = nc.scalar
                act.wait_ge(ada_mm, 1)
                a.activation(ada[:], ps[:].rearrange("p a n -> p (a n)")[0:B, 0:6 * D], ACT.Copy).then_inc(ada_ok, 1)
                act.wait_ge(ld_w, NW1 * 16)
                a.activation(identb[:], ident[:], ACT.Copy).then_inc(ada_ok, 1)
                act.wait_ge(ln_ask, 1)
                a.activation(cols[:, 5], cols[:, 4], ACT.Ln).then_inc(ln_ok, 1)
                act.wait_ge(ada_ok, 2)

            @block.vector
            def _(dve):
                dve.wait_ge(ld_x, 16)
                s = Steps(dve, Chain(dve, v_c), 0)
                row_factors(s, st, 1)
                chained.append(s.ch.n)

            @block.tensor
            def _(pe):
                te = nc.tensor
                pe.wait_ge(ld_w, NW1 * 16)
                pe.wait_ge(const_ok, 3)
                for s in range(3):
                    part = slice(512 * s, 512 * s + 512)
                    for k in range(KD):
                        te.matmul(ps[0:B, s], condT[:, k], wada[:, k, part], start=(k == 0), stop=False)
                    ins = te.matmul(ps[0:B, s], ones[0:1, 0:B], bada[:, part], start=False, stop=True)
                ins.then_inc(ada_mm, 1)

        with ExitStack() as ctx:
            def sb(name, shape, dt=F32):
                return ctx.enter_context(nc.sbuf_tensor("bb_" + name, shape, dt))

            def sem(name):
                return ctx.enter_context(nc.semaphore("bb_" + name))

            mod = sb("mod", [P, 2, D])
            gate = sb("gate", [P, D])
            u = sb("u", [P, NT, D])
            uT = sb("uT", [P, KD, P])
            y = sb("y", [P, 3 * D])
            ysq = sb("ysq", [P, 3 * NH, DH])
            z = sb("z", [P, 2, NH, DH])
            r1 = sb("r1", [P, 2, NH, DH])
            stack = sb("stack", [P, NT, 2, NH, SL, DH], BF16)
            nval = sb("nval", [P, NT, D])
            val = sb("val", [P, NT * NH // 2, 2, 2, DH])
            qS = sb("qS", [P, NH, L], BF16)
            kS = sb("kS", [P, NH, L], BF16)
            nmx = sb("nmx", [P, 4])
            pr = sb("pr", [P, 3, L])
            rs = sb("rs", [P, 2, NH])
            ri = sb("ri", [P, NH])
            rix = sb("rix", [P, D])
            pT = sb("pT", [P, 2, NT, P])
            xf = sb("xf", [P, D])
            oT = sb("oT", [P, KD, P])
            ya = sb("ya", [P, D])
            junk = sb("junk", [P, 2, D])
            junkv = sb("junkv", [P, D])
            usq = sb("usq", [P, NT])
            ulim = sb("ulim", [P, NT])
            hn = sb("hn", [P, HW])
            hf = sb("hf", [P, HW])
            ps = ctx.enter_context(nc.psum_tensor("bb_ps", [P, 8, 512], F32))
            ps_flat = ps[:].rearrange("p a n -> p (a n)")

            u_ok = sem("u_ok")
            usq_ok = sem("usq_ok")
            u_mm = sem("u_mm")
            uT_ok = sem("uT_ok")
            qkv_mm = sem("qkv_mm")
            y_ok = sem("y_ok")
            ysq_ok = sem("ysq_ok")
            z_ok = sem("z_ok")
            top_ok = sem("top_ok")
            r1_ok = sem("r1_ok")
            mid_ok = sem("mid_ok")
            low_ok = sem("low_ok")
            stk_mm = sem("stk_mm")
            stk_a, stk_v = sem("stk_a"), sem("stk_v")
            s_mm = sem("s_mm")
            mx_ok = sem("mx_ok")
            p_ok = sem("p_ok")
            pT_mm = sem("pT_mm")
            pT_a, pT_v = sem("pT_a"), sem("pT_v")
            pv_mm = sem("pv_mm")
            val_0 = sem("val_0")
            ri_ok = sem("ri_ok")
            ri_mm = sem("ri_mm")
            xf_ok = sem("xf_ok")
            oT_ok = sem("oT_ok")
            wo_mm = sem("wo_mm")
            w_ok = sem("w_ok")
            wsq_ok = sem("wsq_ok")
            block = ctx.enter_context(nc.Block())

            def by_act(n):
                return n % 3 == 0

            def stack_by_act(g):
                return g % 3 == 0

            NA = sum(by_act(n) for n in range(U))
            GA = sum(stack_by_act(g) for g in range(2 * NT))

            def tile(n, first):
                t, rest = divmod(n - first, 12)
                return t if rest == 0 and 0 <= t < NT else None

            @block.sync
            def _(sp):
                with sp.Fori(0, B) as b:
                    sp.wait_ge(u_ok, b * NT)
                    sp.dma_start(mod[:], ada_dram[bass.ds(b, 1), 0:2 * D].broadcast_to([P, 2 * D]).rearrange("p (s d) -> p s d", s=2)).then_inc(ld_m, 16)
                    sp.wait_ge(w_ok, b * NT)
                    sp.dma_start(gate[:], ada_dram[bass.ds(b, 1), 2 * D:3 * D].broadcast_to([P, D])).then_inc(ld_g, 16)

            @block.gpsimd
            def _(pool):
                nc.gpsimd.memset(val[:], 0.0).then_inc(val_0, 1)
                with pool.Fori(0, B) as b:
                    roots(pool, [(NT, -0.5)] + [(HW, -0.5)] * NT, ROOTS1 + b * (1 + NT))

            @block.scalar
            def _(act):
                a = nc.scalar

                def next_rows(f, n):
                    if 1 <= n <= NT:
                        act.wait_ge(u_ok, f * NT + n)
                        act.wait_ge(usq_ok, f * NT + n - 1)
                        a.activation(junk[:, 0], u[:, n - 1], ACT.Square, accum_out=usq[:, n - 1:n]).then_inc(usq_ok, 1)
                    t = tile(n, 7)
                    if t is not None:
                        act.wait_ge(u_mm, f * NT + t + 1)
                        a.activation(uT[:], ps[:, 6, 0:D].rearrange("p (k q) -> p k q", q=P), ACT.Copy).then_inc(uT_ok, 1)
                    t = tile(n, 12)
                    if t is not None:
                        act.wait_ge(y_ok, f * NT + t + 1)
                        act.wait_ge(z_ok, f * NT + t)
                        a.activation(ysq[:], y[:].rearrange("p (h v) -> p h v", v=DH), ACT.Square).then_inc(ysq_ok, 1)

                    def parts(t, src, slots, ready, done):
                        act.wait_ge(ready, f * NT + t + 1)
                        for qk in range(2):
                            dst = stack[:, t, qk][:, :, slots[qk]]
                            ins = a.activation(dst, src[:, qk].unsqueeze(2).broadcast_to([P, NH, dst.shape[2], DH]), ACT.Copy)
                        ins.then_inc(done, 1)

                    t = tile(n, 22)
                    if t is not None:
                        if t == 0:
                            act.wait_ge(stk_mm, f * 2 * NT)
                        parts(t, z, (slice(0, 3), slice(0, 8, 3)), z_ok, top_ok)
                    t = tile(n, 25)
                    if t is not None:
                        parts(t, r1, (slice(3, 6), slice(1, 8, 3)), r1_ok, mid_ok)

                def stacks(f):
                    for g in range(2 * NT):
                        if stack_by_act(g):
                            t, s = g // 2, g % 2
                            act.wait_ge(stk_mm, f * 2 * NT + g + 1)
                            a.activation((qS, kS)[s][:, :, t * P:(t + 1) * P],
                                         ps[:, (0, 2, 6)[g % 3]:(2, 4, 8)[g % 3]].bitcast(BF16).rearrange("p a (h q) -> p (a h) q", q=P),
                                         ACT.Copy).then_inc(stk_a, 1)

                def move(b, n):
                    if by_act(n):
                        act.wait_ge(pT_mm, b * U + n + 1)
                        if n >= 2:
                            act.wait_ge(pv_mm, b * U + n - 1)
                        a.activation(pT[:, n % 2], ps[:, 2 + n % 2].rearrange("p (k q) -> p k q", q=P), ACT.Copy).then_inc(pT_a, 1)

                def update_squares(b, t):
                    act.wait_ge(w_ok, b * NT + t + 1)
                    act.wait_ge(wsq_ok, b * NT + t)
                    col = bass.ds(b * NT + t, 1)
                    act.wait_ge(usq_ok, (b + 1) * NT)
                    a.activation(junk[:, 0], ya[:], ACT.Square, accum_out=YA2[:, col])
                    a.activation(junk[:, 1], w[:, col].rearrange("p a d -> p (a d)"), ACT.Square, accum_out=W2[:, col]).then_inc(wsq_ok, 1)

                def attention(b, f):
                    for n in range(U):
                        t, h = n // NH, n % NH
                        act.wait_ge(mx_ok, b * U + n + 1)
                        if n >= 3:
                            act.wait_ge(pT_mm, b * U + n - 2)
                        if t >= 2 and h == 0:
                            act.wait_ge(ri_ok, b * NT + t - 1)
                        a.activation(pr[:, n % 3], ps[:, n % 2], ACT.Exp, bias=nmx[:, n % 4:n % 4 + 1],
                                     accum_out=rs[:, t % 2, h:h + 1]).then_inc(p_ok, 1)
                        if n:
                            move(b, n - 1)
                        if t and h == 11:
                            update_squares(b, t - 1)
                        if f is not None:
                            next_rows(f, n)
                    move(b, U - 1)
                    update_squares(b, NT - 1)

                for n in range(U):
                    next_rows(0, n)
                stacks(0)
                with act.Fori(0, B - 1) as b:
                    attention(b, b + 1)
                    stacks(b + 1)
                attention(B - 1, None)

            @block.vector
            def _(dve):
                v = nc.vector

                class Next:

                    def __init__(self, f, ch):
                        self.f, self.s = f, Steps(dve, ch, ROOTS1 + f * (1 + NT))

                    def __call__(self, n):
                        f, s = self.f, self.s
                        ch = s.ch
                        if n == 0:
                            dve.wait_ge(ld_m, f * 16 + 16)
                            s.ts(mod[:, 1], mod[:, 1], 1.0, None, ALU.add)
                        if n < NT:
                            col = bass.ds(f * NT + n, 1)
                            row = x[:, col].rearrange("p a d -> p (a d)")
                            dve.wait_ge(u_mm, f * NT)
                            dve.wait_ge(usq_ok, f * NT)
                            ch.link(v.scalar_tensor_tensor(out=u[:, n], in0=row, scalar=mv[:, col, 0:1].rearrange("p a c -> p (a c)"), in1=mod[:, 1],
                                                           op0=ALU.subtract, op1=ALU.mult))
                            v.scalar_tensor_tensor(out=u[:, n], in0=u[:, n], scalar=SCALE1[:, col], in1=mod[:, 0],
                                                   op0=ALU.mult, op1=ALU.add).then_inc(u_ok, 1)
                        if n == 5:
                            dve.wait_ge(usq_ok, f * NT + NT)
                            s.ask(usq[:], NT, EPS * EPS)
                        if n == 7:
                            s.answer()
                            s.limit(ulim[:], NT)
                        t = tile(n, 11)
                        if t is not None:
                            dve.wait_ge(ysq_ok, f * NT + t)
                            dve.wait_ge(qkv_mm, f * NT + t + 1)
                            v.scalar_tensor_tensor(out=y[:], in0=ps_flat[:, 6 * 512:6 * 512 + 3 * D],
                                                   scalar=ulim[:, t:t + 1], in1=bqkv[:], op0=ALU.mult, op1=ALU.add).then_inc(y_ok, 1)
                        t = tile(n, 14)
                        if t is not None:
                            dve.wait_ge(ysq_ok, f * NT + t + 1)
                            ch.link(v.tensor_reduce(hn[:, 0:3 * NH], ysq[:], AX.X, ALU.add))
                            ch.link(v.tensor_reduce(hn[:, 3 * NH:], hn[:, 0:3 * NH].rearrange("p (s h) -> p s h", s=3), AX.X, ALU.add))
                            s.ask(hn[:], HW, EPS * EPS)
                        t = tile(n, 21)
                        if t is not None:
                            s.answer()
                            s.ts(hf[:], rout[:], C, None, ALU.mult)
                            s.ts(hf[:, 3 * NH:], hf[:, 3 * NH:], 1.0, R, ALU.min, ALU.mult)
                            s.tt(hf[:, 0:3 * NH].rearrange("p (s h) -> p s h", s=3), hf[:, 0:3 * NH].rearrange("p (s h) -> p s h", s=3),
                                 hf[:, 3 * NH:].unsqueeze(2).broadcast_to([P, 3, NH]), ALU.min)
                            s.ts(hf[:, 0:NH], hf[:, 0:NH], DH ** -0.5, None, ALU.mult)
                            dve.wait_ge(mid_ok, f * NT + t)
                            v.tensor_tensor(nval[:, t].rearrange("p (h v) -> p h v", v=DH),
                                            y[:, 2 * D:].rearrange("p (h v) -> p h v", v=DH),
                                            hf[:, 2 * NH:3 * NH].unsqueeze(2).broadcast_to([P, NH, DH]), ALU.mult)
                            v.tensor_tensor(z[:].rearrange("p a h v -> p (a h) v"), y[:, 0:2 * D].rearrange("p (h v) -> p h v", v=DH),
                                            hf[:, 0:2 * NH].unsqueeze(2).broadcast_to([P, 2 * NH, DH]), ALU.mult).then_inc(z_ok, 1)
                            dve.wait_ge(z_ok, f * NT + t + 1)
                        t = tile(n, 24)
                        if t is not None:
                            dve.wait_ge(top_ok, f * NT + t + 1)
                            v.tensor_tensor(r1[:], z[:], stack[:, t, :, :, 0], ALU.subtract).then_inc(r1_ok, 1)
                        t = tile(n, 27)
                        if t is not None:
                            dve.wait_ge(r1_ok, f * NT + t + 1)
                            dve.wait_ge(mid_ok, f * NT + t + 1)
                            sk = stack[:, t]
                            v.tensor_tensor(sk[:, 0, :, 6:8], r1[:, 0].unsqueeze(2).broadcast_to([P, NH, 2, DH]),
                                            sk[:, 0, :, 3:5], ALU.subtract)
                            v.tensor_tensor(sk[:, 1, :, 2:6:3], r1[:, 1].unsqueeze(2).broadcast_to([P, NH, 2, DH]),
                                            sk[:, 1, :, 1:5:3], ALU.subtract).then_inc(low_ok, 1)
                            dve.wait_ge(low_ok, f * NT + t + 1)

                def stacks(f, ch):
                    dve.wait_ge(pv_mm, f * U)
                    dve.wait_ge(val_0, 1)
                    v.tensor_copy(val[:, :, 0, 0], nval[:].rearrange("p t (h s v) -> p (t h) s v", s=2, v=DH)[:, :, 0])
                    ch.link(v.tensor_copy(val[:, :, 1, 1], nval[:].rearrange("p t (h s v) -> p (t h) s v", s=2, v=DH)[:, :, 1]))
                    for g in range(2 * NT):
                        if not stack_by_act(g):
                            t, s = g // 2, g % 2
                            dve.wait_ge(stk_mm, f * 2 * NT + g + 1)
                            v.tensor_copy((qS, kS)[s][:, :, t * P:(t + 1) * P],
                                          ps[:, (0, 2, 6)[g % 3]:(2, 4, 8)[g % 3]].bitcast(BF16).rearrange("p a (h q) -> p (a h) q", q=P)).then_inc(stk_v, 1)

                def maximum(b, n):
                    dve.wait_ge(s_mm, b * U + n + 1)
                    if n >= 4:
                        dve.wait_ge(p_ok, b * U + n - 3)
                    v.tensor_reduce(nmx[:, n % 4:n % 4 + 1], ps[:, n % 2], AX.X, ALU.max, negate=True).then_inc(mx_ok, 1)

                def move(b, n):
                    if not by_act(n):
                        dve.wait_ge(pT_mm, b * U + n + 1)
                        if n >= 2:
                            dve.wait_ge(pv_mm, b * U + n - 1)
                        v.tensor_copy(pT[:, n % 2], ps[:, 2 + n % 2].rearrange("p (k q) -> p k q", q=P)).then_inc(pT_v, 1)

                def inverse_sums(b, ch, t):
                    dve.wait_ge(p_ok, b * U + (t + 1) * NH)
                    ch.link(v.reciprocal(ri[:], rs[:, t % 2]))
                    v.tensor_scalar(rix[:].rearrange("p (h v) -> p h v", v=DH), ri[:].unsqueeze(2).broadcast_to([P, NH, DH]),
                                    1.0 / R, None, ALU.mult).then_inc(ri_ok, 1)

                def heads(b, t):
                    dve.wait_ge(ri_mm, b * NT + t + 1)
                    v.tensor_copy(xf[:], ps[:, 4 + t % 2, D:2 * D]).then_inc(xf_ok, 1)
                    dve.wait_ge(xf_ok, b * NT + t + 1)
                    v.tensor_tensor(oT[:].rearrange("p k q -> p (k q)"), ps[:, 4 + t % 2, 0:D], xf[:], ALU.mult).then_inc(oT_ok, 1)

                def update(b, ch, t):
                    col = bass.ds(b * NT + t, 1)
                    wt, xt = (r[:, col].rearrange("p a d -> p (a d)") for r in (w, x))
                    dve.wait_ge(wsq_ok, b * NT + t)
                    dve.wait_ge(wo_mm, b * NT + t + 1)
                    ch.link(v.tensor_tensor(ya[:], ps[:, 4 + t % 2, 0:D], bo[:], ALU.add))
                    dve.wait_ge(ld_g, b * 16 + 16)
                    v.tensor_tensor(wt, ya[:], gate[:], ALU.mult).then_inc(w_ok, 1)
                    dve.wait_ge(w_ok, b * NT + t + 1)
                    ch.link(v.tensor_tensor(junkv[:], xt, wt, ALU.mult))
                    ch.link(v.tensor_reduce(XW[:, col], junkv[:], AX.X, ALU.add))

                def attention(b, ch, following):
                    maximum(b, 0)
                    for n in range(U):
                        t, h = n // NH, n % NH
                        if n + 1 < U:
                            maximum(b, n + 1)
                        if n:
                            move(b, n - 1)
                        if t and h == 1:
                            inverse_sums(b, ch, t - 1)
                        if t and h == 4:
                            heads(b, t - 1)
                        if t and h == 9:
                            update(b, ch, t - 1)
                        if following:
                            following(n)
                    move(b, U - 1)
                    inverse_sums(b, ch, NT - 1)
                    heads(b, NT - 1)
                    update(b, ch, NT - 1)

                ch = Chain(dve, v_c, chained[0])
                rows = Next(0, ch)
                for n in range(U):
                    rows(n)
                stacks(0, ch)
                FRONT, base = ch.n, chained[0] + ch.n
                LINKS = FRONT + 4 * NT
                with dve.Fori(0, B - 1) as b:
                    ch = Chain(dve, v_c, base + b * LINKS)
                    attention(b, ch, Next(b + 1, ch))
                    stacks(b + 1, ch)
                    assert ch.n == LINKS, (ch.n, FRONT)
                ch = Chain(dve, v_c, base + (B - 1) * LINKS)
                attention(B - 1, ch, None)
                chained.append(base + (B - 1) * LINKS + ch.n)

            @block.tensor
            def _(pe):
                te = nc.tensor

                def next_rows(f, n):
                    t = tile(n, 6)
                    if t is not None:
                        pe.wait_ge(usq_ok, f * NT + NT)
                        pe.wait_ge(y_ok, f * NT + t)
                        for c in range(KD):
                            ins = te.transpose(ps[:, 6, c * P:(c + 1) * P], u[:, t, c * P:(c + 1) * P], ident[:])
                        ins.then_inc(u_mm, 1)
                    t = tile(n, 9)
                    if t is not None:
                        pe.wait_ge(uT_ok, f * NT + t + 1)
                        for lo, hi, bank in ((0, 512, 6), (512, 768, 7)):
                            for k in range(KD):
                                ins = te.matmul(ps[:, bank, 0:hi - lo], uT[:, k], wqkv[:, k, lo:hi],
                                                start=(k == 0), stop=(k == KD - 1))
                        ins.then_inc(qkv_mm, 1)

                def stacks(f):
                    for g in range(2 * NT):
                        t, s = g // 2, g % 2
                        if g == 0:
                            pe.wait_ge(p_ok, f * U)
                            pe.wait_ge(y_ok, f * NT + NT)
                        if g == 1:
                            pe.wait_ge(pT_v, f * (U - NA))
                            pe.wait_ge(pT_a, f * NA)
                        if g >= 3:
                            if stack_by_act(g - 3):
                                pe.wait_ge(stk_a, f * GA + (g - 3) // 3 + 1)
                            else:
                                pe.wait_ge(stk_v, f * (2 * NT - GA) + g - 3 - (g - 3) // 3)
                        if s == 0:
                            pe.wait_ge(low_ok, f * NT + t + 1)
                        dst = ps[:, (0, 2, 6)[g % 3]:(2, 4, 8)[g % 3]].bitcast(BF16).rearrange("p a (h q) -> p (a h) q", q=P)
                        for h in range(NH):
                            ins = te.transpose(dst[:, h], stack[:, t, s, h].rearrange("p s v -> p (s v)"), identb[:])
                        ins.then_inc(stk_mm, 1)

                def scores(b, n):
                    t, h = n // NH, n % NH
                    if n < 2:
                        pe.wait_ge(stk_a, b * GA + GA)
                        pe.wait_ge(stk_v, (b + 1) * (2 * NT - GA))
                    else:
                        pe.wait_ge(p_ok, b * U + n - 1)
                    te.matmul(ps[:, n % 2], qS[:, h, t * P:(t + 1) * P], kS[:, h], start=True, stop=True).then_inc(s_mm, 1)

                def values(b, n):
                    t, h = n // NH, n % NH
                    if h == 0:
                        if t >= 2:
                            pe.wait_ge(w_ok, b * NT + t - 1)
                        else:
                            pe.wait_ge(w_ok, b * NT)
                    if by_act(n):
                        pe.wait_ge(pT_a, b * NA + n // 3 + 1)
                    else:
                        pe.wait_ge(pT_v, b * (U - NA) + n - n // 3)
                    r, c = h // 2 % 4, h // 8
                    for k in range(NT):
                        ins = te.matmul(ps[32 * r:32 * r + 32, 4 + t % 2, c * P:(c + 1) * P],
                                        val[:, k * NH // 2 + h // 2, h % 2].rearrange("p s v -> p (s v)"), pT[:, n % 2, k],
                                        start=(h % 2 == 0 and k == 0), stop=(h % 2 == 1 and k == NT - 1))
                    ins.then_inc(pv_mm, 1)

                def turn_factors(b, t):
                    pe.wait_ge(ri_ok, b * NT + t + 1)
                    for k in range(KD):
                        ins = te.transpose(ps[:, 4 + t % 2, (KD + k) * P:(KD + k + 1) * P], rix[:, k * P:(k + 1) * P], ident[:])
                    ins.then_inc(ri_mm, 1)

                def project(b, t):
                    pe.wait_ge(oT_ok, b * NT + t + 1)
                    for k in range(KD):
                        ins = te.matmul(ps[:, 4 + t % 2, 0:D], oT[:, k], wo[:, k], start=(k == 0), stop=(k == KD - 1))
                    ins.then_inc(wo_mm, 1)

                def attention(b, f):
                    scores(b, 0)
                    scores(b, 1)
                    for n in range(U):
                        t, h = n // NH, n % NH
                        pe.wait_ge(p_ok, b * U + n + 1)
                        if n + 2 < U:
                            scores(b, n + 2)
                        if n >= 2:
                            if by_act(n - 2):
                                pe.wait_ge(pT_a, b * NA + (n - 2) // 3 + 1)
                            else:
                                pe.wait_ge(pT_v, b * (U - NA) + n - 2 - (n - 2) // 3)
                        for k in range(NT):
                            ins = te.transpose(ps[:, 2 + n % 2, k * P:(k + 1) * P], pr[:, n % 3, k * P:(k + 1) * P], ident[:])
                        ins.then_inc(pT_mm, 1)
                        if n:
                            values(b, n - 1)
                        if t and h == 3:
                            turn_factors(b, t - 1)
                        if t and h == 6:
                            project(b, t - 1)
                        if f is not None:
                            next_rows(f, n)
                    values(b, U - 1)
                    turn_factors(b, NT - 1)
                    project(b, NT - 1)

                for n in range(U):
                    next_rows(0, n)
                stacks(0)
                with pe.Fori(0, B - 1) as b:
                    attention(b, b + 1)
                    stacks(b + 1)
                attention(B - 1, None)

        with ExitStack() as ctx:
            def sb(name, shape, dt=F32):
                return ctx.enter_context(nc.sbuf_tensor("bc_" + name, shape, dt))

            def sem(name):
                return ctx.enter_context(nc.semaphore("bc_" + name))

            wf1 = sb("wf1", [P, KD, FF])
            wf2 = sb("wf2", [P, MF, D])
            bf1 = sb("bf1", [P, MF])
            bf2 = sb("bf2", [P, D])
            mod = sb("mod", [P, 2, D])
            gate = sb("gate", [P, D])
            st = sb("st", [P, T, 6])
            u = sb("u", [P, NT, D])
            uT = sb("uT", [P, KD, L])
            fT = sb("fT", [P, MF, L])
            fsq = sb("fsq", [P, MF, L])
            ya = sb("ya", [P, 2, D])
            junk = sb("junk", [P, 2, D])
            junkv = sb("junkv", [P, D])
            usq = sb("usq", [P, NT])
            ulim = sb("ulim", [P, NT])
            flim = sb("flim", [P, NT])
            ps = ctx.enter_context(nc.psum_tensor("bc_ps", [P, 8, 512], F32))
            HB = (2, 3, 7)
            th_ask, th_ok = sem("th_ask"), sem("th_ok")
            u_ok = sem("u_ok")
            usq_ok = sem("usq_ok")
            us_ok = sem("us_ok")
            u_mm = sem("u_mm")
            uT_a, uT_v = sem("uT_a"), sem("uT_v")
            f_mm = sem("f_mm")
            f_v = sem("f_v")
            f_a = sem("f_a")
            fn_mm = sem("fn_mm")
            f2_mm = sem("f2_mm")
            w_ok = sem("w_ok")
            wsq_ok = sem("wsq_ok")
            out_ok = sem("out_ok")
            st_x = sem("st_x")
            block = ctx.enter_context(nc.Block())
            R0 = ROOTS1 + ROOTS2

            @block.sync
            def _(sp):
                for dst, name in ((wf1, "wf1"), (bf1, "bf1"), (wf2, "wf2"), (bf2, "bf2")):
                    sp.dma_start(dst[:], io[name]).then_inc(ld_w, 16)
                with sp.Fori(0, B) as b:
                    sp.wait_ge(u_ok, b * NT)
                    sp.dma_start(mod[:], ada_dram[bass.ds(b, 1), 3 * D:5 * D].broadcast_to([P, 2 * D]).rearrange("p (s d) -> p s d", s=2)).then_inc(ld_m, 16)
                    sp.wait_ge(w_ok, b * NT)
                    sp.dma_start(gate[:], ada_dram[bass.ds(b, 1), 5 * D:6 * D].broadcast_to([P, D])).then_inc(ld_g, 16)
                for b in range(B):
                    sp.wait_ge(out_ok, b + 1)
                    sp.dma_start(xs[b].rearrange("(t p) d -> p t d", p=P), w[:, b * NT:(b + 1) * NT]).then_inc(st_x, 16)
                sp.wait_ge(st_x, 16 * B)

            @block.gpsimd
            def _(pool):
                roots(pool, [(T, -0.5), (T, 0.5), (T, 0.5), (T, -0.5), (NT, -0.5)], R0)
                with pool.Fori(0, B - 1) as b:
                    roots(pool, [(NT, -0.5)] * 2, R0 + 5 + b * 2)
                roots(pool, [(NT, -0.5), (T, -0.5), (T, 0.5)], R0 + 5 + (B - 1) * 2)

            @block.scalar
            def _(act):
                a = nc.scalar

                def row_squares(f, t):
                    act.wait_ge(u_ok, f * NT + t + 1)
                    act.wait_ge(usq_ok, f * NT + t)
                    a.activation(junk[:, 0], u[:, t], ACT.Square, accum_out=usq[:, t:t + 1]).then_inc(usq_ok, 1)

                def turned(f):
                    act.wait_ge(u_mm, f + 1)
                    a.activation(uT[:, 0], ps[:, 0], ACT.Copy).then_inc(uT_a, 1)

                def mlp(b, f):
                    for m in range(MF):
                        act.wait_ge(f_v, b * MF + m + 1)
                        if m == 0:
                            act.wait_ge(fn_mm, b)
                        a.activation(fsq[:, m], fT[:, m], ACT.Square).then_inc(f_a, 1)
                        if f is not None and m < NT:
                            row_squares(f, m)
                    if f is not None:
                        turned(f)
                    for t in range(NT):
                        act.wait_ge(w_ok, b * NT + t + 1)
                        act.wait_ge(wsq_ok, b * NT + t)
                        col = bass.ds(b * NT + t, 1)
                        if t == 0:
                            act.wait_ge(usq_ok, (b + 2) * NT if f is not None else B * NT)
                        a.activation(junk[:, 0], ya[:, t % 2], ACT.Square, accum_out=YA2[:, col])
                        a.activation(junk[:, 1], w[:, col].rearrange("p a d -> p (a d)"), ACT.Square, accum_out=W2[:, col]).then_inc(wsq_ok, 1)

                act.wait_ge(th_ask, 1)
                a.activation(cols[:, 17], cols[:, 16], ACT.Tanh).then_inc(th_ok, 1)
                act.wait_ge(ln_ask, 2)
                a.activation(cols[:, 5], cols[:, 4], ACT.Ln).then_inc(ln_ok, 1)
                for t in range(NT):
                    row_squares(0, t)
                turned(0)
                with act.Fori(0, B - 1) as b:
                    mlp(b, b + 1)
                mlp(B - 1, None)
                act.wait_ge(th_ask, 2)
                a.activation(cols[:, 17], cols[:, 16], ACT.Tanh).then_inc(th_ok, 1)

            @block.vector
            def _(dve):
                v = nc.vector

                def modulated(s, f, t):
                    if t == 0:
                        dve.wait_ge(ld_m, (B + f) * 16 + 16)
                        s.ts(mod[:, 1], mod[:, 1], 1.0, None, ALU.add)
                        dve.wait_ge(u_mm, f)
                    col = bass.ds(f * NT + t, 1)
                    s.ch.link(v.scalar_tensor_tensor(out=u[:, t], in0=x[:, col].rearrange("p a d -> p (a d)"),
                                                     scalar=mv[:, col, 0:1].rearrange("p a c -> p (a c)"), in1=mod[:, 1],
                                                     op0=ALU.subtract, op1=ALU.mult))
                    v.scalar_tensor_tensor(out=u[:, t], in0=u[:, t], scalar=SCALE1[:, col], in1=mod[:, 0],
                                           op0=ALU.mult, op1=ALU.add).then_inc(u_ok, 1)

                def limited(s):
                    s.answer()
                    s.limit(ulim[:], NT)
                    for t in range(NT):
                        v.tensor_scalar(u[:, t], u[:, t], ulim[:, t:t + 1], None, ALU.mult).then_inc(us_ok, 1)

                def turned(f):
                    dve.wait_ge(u_mm, f + 1)
                    v.tensor_copy(uT[:, 1], ps[:, 1]).then_inc(uT_v, 1)

                def mlp(s, b, f):
                    for m in range(MF):
                        dve.wait_ge(f_mm, b * MF + m + 1)
                        v.tensor_scalar(fT[:, m], ps[:, HB[m % 3]], bf1[:, m:m + 1], None, ALU.add).then_inc(f_v, 1)
                        if f is not None and m < NT:
                            modulated(s, f, m)
                        if f is not None and m == NT + 1:
                            dve.wait_ge(usq_ok, (f + 1) * NT)
                            s.ask(usq[:], NT, EPS * EPS)
                    if f is not None:
                        limited(s)
                        turned(f)
                    dve.wait_ge(fn_mm, b + 1)
                    s.root(ps[:, 4, 0:NT], NT, EPS * EPS)
                    s.limit(flim[:], NT)
                    dve.wait_ge(ld_g, (B + b) * 16 + 16)
                    for t in range(NT):
                        col = bass.ds(b * NT + t, 1)
                        wt, xt = (r[:, col].rearrange("p a d -> p (a d)") for r in (w, x))
                        if t >= 2:
                            dve.wait_ge(wsq_ok, b * NT + t - 1)
                        dve.wait_ge(f2_mm, b * NT + t + 1)
                        s.ch.link(v.scalar_tensor_tensor(out=ya[:, t % 2], in0=ps[:, 5 + t % 2, 0:D], scalar=flim[:, t:t + 1],
                                                         in1=bf2[:], op0=ALU.mult, op1=ALU.add))
                        v.tensor_tensor(wt, ya[:, t % 2], gate[:], ALU.mult).then_inc(w_ok, 1)
                        dve.wait_ge(w_ok, b * NT + t + 1)
                        s.tt(junkv[:], xt, wt, ALU.mult)
                        s.ch.link(v.tensor_reduce(XW[:, col], junkv[:], AX.X, ALU.add))
                    dve.wait_ge(wsq_ok, (b + 1) * NT)

                s = Steps(dve, Chain(dve, v_c, chained[1]), R0)
                mobius(s, th_ask, th_ok, 1)
                for t in range(T):
                    n = s.ch.mark(v.tensor_scalar(x[:, t], x[:, t], FX[:, t:t + 1], None, ALU.mult))
                s.ch.wait(n)
                for t in range(T):
                    n = s.ch.mark(v.scalar_tensor_tensor(out=x[:, t], in0=w[:, t], scalar=FW[:, t:t + 1], in1=x[:, t],
                                                         op0=ALU.mult, op1=ALU.add))
                s.ch.wait(n)
                row_factors(s, st, 2)
                dve.wait_ge(ld_w, (NW1 + NW2) * 16)
                for t in range(NT):
                    modulated(s, 0, t)
                dve.wait_ge(usq_ok, NT)
                s.ask(usq[:], NT, EPS * EPS)
                limited(s)
                turned(0)
                first = chained[1] + s.ch.n
                LINKS = 1 + NT + 1 + 1 + 3 * NT
                with dve.Fori(0, B - 1) as b:
                    r = Steps(dve, Chain(dve, v_c, first + b * LINKS), R0 + 5 + b * 2)
                    mlp(r, b, b + 1)
                    assert r.ch.n == LINKS, r.ch.n
                s = Steps(dve, Chain(dve, v_c, first + (B - 1) * LINKS), R0 + 5 + (B - 1) * 2)
                mlp(s, B - 1, None)
                mobius(s, th_ask, th_ok, 2)
                for t in range(T):
                    n = s.ch.mark(v.tensor_scalar(w[:, t], w[:, t], FW[:, t:t + 1], None, ALU.mult))
                s.ch.wait(n)
                for t in range(T):
                    ins = v.scalar_tensor_tensor(out=w[:, t], in0=x[:, t], scalar=FX[:, t:t + 1], in1=w[:, t],
                                                 op0=ALU.mult, op1=ALU.add)
                    if t % NT == NT - 1:
                        ins.then_inc(out_ok, 1)

            @block.tensor
            def _(pe):
                te = nc.tensor
                pe.wait_ge(ld_w, (NW1 + NW2) * 16)

                def turn_rows(f):
                    for t in range(NT):
                        pe.wait_ge(us_ok, f * NT + t + 1)
                        for c in range(KD):
                            ins = te.transpose(ps[:, c, t * P:(t + 1) * P], u[:, t, c * P:(c + 1) * P], ident[:])
                    ins.then_inc(u_mm, 1)

                def mlp(b, f):
                    pe.wait_ge(uT_a, b + 1)
                    pe.wait_ge(uT_v, b + 1)
                    for m in range(MF):
                        pe.wait_ge(f_v, b * MF + max(m - 2, 0))
                        for k in range(KD):
                            ins = te.matmul(ps[:, HB[m % 3]], wf1[:, k, m * P:(m + 1) * P], uT[:, k], start=(k == 0), stop=(k == KD - 1))
                        ins.then_inc(f_mm, 1)
                    if f is not None:
                        turn_rows(f)
                    pe.wait_ge(f_a, b * MF + MF)
                    for t in range(NT):
                        for m in range(MF):
                            ins = te.matmul(ps[:, 4, t:t + 1], fsq[:, m, t * P:(t + 1) * P], ones[:, 0:1], start=(m == 0), stop=(m == MF - 1))
                    ins.then_inc(fn_mm, 1)
                    for t in range(NT):
                        pe.wait_ge(w_ok, b * NT + max(t - 1, 0))
                        for m in range(MF):
                            ins = te.matmul(ps[:, 5 + t % 2, 0:D], fT[:, m, t * P:(t + 1) * P], wf2[:, m], start=(m == 0), stop=(m == MF - 1))
                        ins.then_inc(f2_mm, 1)

                turn_rows(0)
                with pe.Fori(0, B - 1) as b:
                    mlp(b, b + 1)
                mlp(B - 1, None)


def window_layers(nc, io, xs, x1, out):
    NL = 2
    NH, DH = 8, 64
    NC = NH * DH // P
    HID = int(D * 4 * 2 / 3)
    MH = -(-HID // P)
    LAST = HID - (MH - 1) * P
    U = 2 * NT
    QK_SCALE = 8.0

    with ExitStack() as ctx:
        def sb(name, shape, dt=F32):
            return ctx.enter_context(nc.sbuf_tensor(name, shape, dt))

        def sem(name):
            return ctx.enter_context(nc.semaphore(name))

        wqkv = sb("wqkv", [P, KD, 3 * NC * P])
        wo = sb("wwo", [P, NC, D])
        w1 = sb("w1", [P, KD, 2 * HID])
        w2 = sb("w2", [P, MH, D])
        b1 = sb("b1", [P, 2, MH])
        lnp = sb("lnp", [P, 2, KD])
        qks = sb("qks", [P, 2, 2, DH])
        rot = sb("rot", [P, 2, NT, 2, DH])
        rots = sb("rots", [P, 2, NT, 2, DH])
        wmask = sb("wmask", [P, 2 * P])
        ident = sb("wident", [P, P])
        last = sb("last", [P, NL])
        xin = sb("xin", [P, NT, D])
        xadd = sb("xadd", [P, NT, D])
        hT = sb("hT", [P, KD, L])
        sq = sb("sq", [P, 2 * NH, DH])
        n2 = sb("n2", [P, 2, 2 * NH])
        t1 = sb("t1", [P, 2, NH, DH])
        t2 = sb("t2", [P, 2, NH, DH])
        qk = sb("qk", [P, 2, 2, NH, DH])
        vt = sb("vt", [P, NT, NC * P])
        qT = sb("wqT", [P, NC, L])
        kT = sb("wkT", [P, NC, L])
        sm = sb("sm", [P, 2, 4, 2 * P])
        mx = sb("wmx", [P, 2, 4])
        nmx = sb("nmx", [P, 2, 4])
        pr = sb("pr", [P, 2, 4, 2 * P])
        rs = sb("rs", [P, 2, 2, 4])
        ri = sb("ri", [P, 2, 2, 4])
        pT = sb("wpT", [P, 4, 2, P])
        ot = sb("ot", [P, 2, NC, 2, DH])
        oT = sb("oT", [P, NC, P])
        xm = sb("xm", [P, NT, D])
        hs = sb("hs", [P, NT, P])
        st = sb("st", [P, NT, 2, 6])
        mv = sb("mv", [P, NT, 2])
        ve = sb("ve", [P, 2, NT])
        mhalf = sb("mhalf", [P, 2 * NH])
        xn = sb("xn", [P, NT, D])
        xnT = sb("xnT", [P, KD, L])
        gl = sb("gl", [P, 2, L])
        h2T = sb("h2T", [P, MH, L])
        yt = sb("yt", [P, 2, D])
        yl = sb("yl", [P, 2, D])
        carrier = sb("carrier", [P, 1])

        ps = ctx.enter_context(nc.psum_tensor("wps", [P, 8, 512], F32))
        NW = 6
        ld_c = sem("ld_c")
        ld_w = sem("wld_w")
        ld_x = sem("wld_x")
        ld_a = sem("ld_a")
        x_mm = sem("x_mm")
        hT_a = sem("hT_a")
        hT_v = sem("hT_v")
        qkv_mm = sem("qkv_mm")
        v_ev = sem("v_ev")
        sq_ok = sem("sq_ok")
        qk_rd = sem("qk_rd")
        qk_ok = sem("qk_ok")
        qk_mm = sem("qk_mm")
        qT_ok = sem("qT_ok")
        kT_ok = sem("kT_ok")
        s_mm = sem("ws_mm")
        sm_ok = sem("sm_ok")
        p_ok = sem("wp_ok")
        pT_mm = sem("wpT_mm")
        pT_a = sem("wpT_a")
        pT_v = sem("wpT_v")
        pv_mm = sem("wpv_mm")
        o_ok = sem("o_ok")
        oT_mm = sem("oT_mm")
        oT_ok = sem("oT_ok")
        wo_mm = sem("wwo_mm")
        xm_ok = sem("xm_ok")
        sh_ok = sem("sh_ok")
        xn_ok = sem("xn_ok")
        xn_mm = sem("xn_mm")
        xnT_ok = sem("xnT_ok")
        g_mm = sem("g_mm")
        g_act = sem("g_act")
        h2_ok = sem("h2_ok")
        y_mm = sem("y_mm")
        y_ok = sem("y_ok")
        st_y = [sem("st_y0"), sem("st_y1")]
        st_o = [sem("st_o0"), sem("st_o1")]
        n2_ok = sem("n2_ok")
        nr_ok = sem("nr_ok")
        mh_ok = sem("mh_ok")
        v_w = sem("v_w")
        v_t = sem("v_t")
        block = ctx.enter_context(nc.Block())

        @block.sync
        def _(sp):
            for dst, name in ((rot, "rot"), (wmask, "wmask"), (ident, "ident"), (last, "last")):
                sp.dma_start(dst[:], io[name]).then_inc(ld_c, 16)
            with sp.Fori(0, NL) as l:
                for s in range(2):
                    sp.wait_ge(st_y[s], l * (16 * B * NT // 2))
                for dst, name in ((wqkv, "wqkv"), (wo, "wwo"), (w1, "w1"), (b1, "b1"), (lnp, "lnp"), (qks, "qks")):
                    d = dst[:]
                    if len(d.shape) > 3:
                        d = d.rearrange("p a b c -> p a (b c)")
                    src = io[name][bass.ds(l, 1)]
                    sp.dma_start(d, src.rearrange("l p a b -> p (l a) b")).then_inc(ld_w, 16)
                sp.dma_start(w2[:, 0:MH - 1], io["w2"][bass.ds(l, 1)].rearrange("l p a b -> p (l a) b")[:, 0:MH - 1]).then_inc(ld_w, 16)
                sp.dma_start(w2[0:LAST + 1, MH - 1], io["w2"][bass.ds(l, 1)].rearrange("l p a b -> p (l a) b")[0:LAST + 1, MH - 1]).then_inc(ld_w, 16)
                with sp.Fori(0, B) as b:
                    i = l * B + b
                    sp.wait_ge(xm_ok, i * NT)
                    sp.dma_start(xin[:], xs[bass.ds(i, 1)].rearrange("a (t p) d -> p (a t) d", p=P)).then_inc(ld_x, 16)
                    sp.wait_ge(y_ok, i * NT)
                    sp.dma_start(xadd[:], x1[bass.ds(b, 1)].rearrange("a (t p) d -> p (a t) d", p=P)).then_inc(ld_a, 16)
                    for t in range(NT):
                        sp.wait_ge(xm_ok, i * NT + t + 1)
                        sp.dma_start(hs[1:P, t], xm[0:P - 1, t, P:D]).then_inc(sh_ok, 16)
                        if t:
                            sp.dma_start(hs[0:1, t], xm[P - 1:P, t - 1, P:D]).then_inc(sh_ok, 16)
                    for t in range(NT):
                        sp.wait_ge(y_ok, i * NT + t + 1)
                        sp.dma_start(xs[bass.ds(i + B, 1)].rearrange("a (t p) d -> t p (a d)", p=P)[t], yt[:, t % 2]).then_inc(st_y[t % 2], 16)
                        sp.dma_start(out[bass.ds(b, 1)].rearrange("a (t p) d -> t p (a d)", p=P)[t], yl[:, t % 2]).then_inc(st_o[t % 2], 16)
            for s in st_y + st_o:
                sp.wait_ge(s, NL * 16 * B * NT // 2)

        @block.scalar
        def _(act):
            a = nc.scalar
            with act.Fori(0, NL) as l:
                with act.Fori(0, B) as b:
                    i = l * B + b
                    act.wait_ge(ld_w, (l + 1) * (16 * 8))
                    act.wait_ge(x_mm, i + 1)
                    a.activation(hT[:, 0], ps[:, 6], ACT.Copy).then_inc(hT_a, 1)

                    def turned_q(t):
                        act.wait_ge(qk_mm, i * NT + t + 1)
                        a.activation(qT[:, :, t * P:(t + 1) * P], ps[:, 6].rearrange("p (c q) -> p c q", q=P),
                                     ACT.Copy).then_inc(qT_ok, 1)

                    for t in range(NT):
                        act.wait_ge(qkv_mm, i * NT + t + 1)
                        act.wait_ge(qk_rd, i * NT + t)
                        k0 = 3 * (t % 2)
                        a.activation(sq[:], ps[:, k0:k0 + 2].rearrange("p a (h v) -> p (a h) v", v=DH), ACT.Square).then_inc(sq_ok, 1)
                        a.activation(vt[:, t], ps[:, k0 + 2], ACT.Copy).then_inc(v_ev, 1)
                        if t:
                            turned_q(t - 1)
                    turned_q(NT - 1)

                    def heads_out(t):
                        act.wait_ge(oT_mm, i * NT + t + 1)
                        if t:
                            act.wait_ge(wo_mm, i * NT + t)
                        a.activation(oT[:], ps[:, 7].rearrange("p (c q) -> p c q", q=P), ACT.Copy).then_inc(oT_ok, 1)

                    for u in range(U):
                        t, g = u // 2, u % 2
                        lo = P if t == 0 else 0
                        act.wait_ge(sm_ok, i * U + u + 1)
                        if u >= 2:
                            act.wait_ge(pT_mm, i * U + u - 1)
                        if t >= 2:
                            act.wait_ge(o_ok, i * U + u - 3)
                        for h in range(4):
                            ins = a.activation(pr[:, g, h, lo:], sm[:, g, h, lo:], ACT.Exp, bias=nmx[:, g, h:h + 1],
                                               scale=QK_SCALE, accum_out=rs[:, t % 2, g, h:h + 1])
                        ins.then_inc(p_ok, 1)
                        act.wait_ge(pT_mm, i * U + u + 1)
                        if u:
                            act.wait_ge(pv_mm, i * U + u)
                        a.activation(pT[:, 0:2, lo // P:], ps[:, 4].rearrange("p (h k q) -> p h k q", h=2, k=2)[:, :, lo // P:],
                                     ACT.Copy).then_inc(pT_a, 1)
                        if u >= 2 and g == 0:
                            heads_out(t - 1)
                    heads_out(NT - 1)
                    for m in range(MH):
                        n = P if m < MH - 1 else LAST
                        act.wait_ge(g_mm, i * MH + m + 1)
                        if m >= 2:
                            act.wait_ge(h2_ok, i * MH + m - 1)
                        a.activation(gl[0:n, m % 2], ps[0:n, m % 2], ACT.Gelu, bias=b1[0:n, 1, m:m + 1]).then_inc(g_act, 1)

        @block.vector
        def _(dve):
            v = nc.vector
            pre = Chain(dve, v_w)
            pre.mark(v.memset(hT[:, 1, 0:1], 0.0))
            pre.mark(v.memset(hs[:, 0], 0.0))
            pre.link(v.memset(h2T[0:64, MH - 1], 1.0))
            dve.wait_ge(ld_c, 4 * 16)
            LL = 3

            def carry_wait():
                v.memset(carrier[:], 0.0)

            with dve.Fori(0, NL) as l:
                lw = Chain(dve, v_w, l * LL + pre.n)
                dve.wait_ge(ld_w, (l + 1) * (16 * 8))
                for s in range(2):
                    ins = v.tensor_tensor(rots[:, s], rot[:, s],
                                          qks[:, s].unsqueeze(1).broadcast_to([P, NT, 2, DH]), ALU.mult)
                    lw.mark(ins)
                lw.mark(v.memset(st[:], 0.0))
                with dve.Fori(0, B) as b:
                    i = l * B + b
                    dve.wait_ge(v_w, l * LL + LL + pre.n)
                    LINKS = 3 * NT + 2 * U + NT + 1 + NT
                    ch = Chain(dve, v_t, i * LINKS)
                    dve.wait_ge(x_mm, i + 1)
                    v.tensor_copy(hT[:, 1, 1:L], ps[:, 7, 0:L - 1]).then_inc(hT_v, 1)

                    def turned_k(t):
                        dve.wait_ge(qk_mm, i * NT + t + 1)
                        v.tensor_copy(kT[:, :, t * P:(t + 1) * P], ps[:, 7].rearrange("p (c q) -> p c q", q=P)).then_inc(kT_ok, 1)

                    for t in range(NT):
                        k0 = 3 * (t % 2)
                        dve.wait_ge(sq_ok, i * NT + t + 1)
                        ch.link(v.tensor_reduce(n2[:, 0], sq[:], AX.X, ALU.add))
                        v.tensor_scalar(n2[:, 0], n2[:, 0], 1e-24, None, ALU.max).then_inc(n2_ok, 1)
                        if t:
                            turned_k(t - 1)
                        dve.wait_ge(nr_ok, i * (NT + 1) + t + 1)
                        v.tensor_tensor(t1[:], ps[:, k0:k0 + 2].rearrange("p a (h v) -> p a h v", v=DH),
                                        n2[:, 1].rearrange("p (a h) -> p a h", a=2).unsqueeze(3).broadcast_to([P, 2, NH, DH]),
                                        ALU.mult).then_inc(qk_rd, 1)
                        dve.wait_ge(qk_rd, i * NT + t + 1)
                        if t >= 2:
                            dve.wait_ge(qk_mm, i * NT + t - 1)
                        q = qk[:, t % 2]
                        ch.mark(v.tensor_tensor(q, t1[:], rots[:, 0, t].unsqueeze(2).broadcast_to([P, 2, NH, DH]), ALU.mult))
                        hf = DH // 2
                        for s in range(2):
                            ins = v.tensor_tensor(t2[:, :, :, s * hf:(s + 1) * hf], t1[:, :, :, (1 - s) * hf:(2 - s) * hf],
                                                  rots[:, 1, t, :, s * hf:(s + 1) * hf].unsqueeze(2).broadcast_to([P, 2, NH, hf]), ALU.mult)
                        ch.link(ins)
                        v.tensor_tensor(q, q, t2[:], ALU.add).then_inc(qk_ok, 1)
                    turned_k(NT - 1)

                    def rows_after_attention(t):
                        dve.wait_ge(wo_mm, i * NT + t + 1)
                        v.tensor_tensor(xm[:, t], xin[:, t], ps[:, 7, 0:D], ALU.add).then_inc(xm_ok, 1)

                    def scores_max(u):
                        t, g = u // 2, u % 2
                        lo = P if t == 0 else 0
                        dve.wait_ge(s_mm, i * U + u + 1)
                        if u >= 2:
                            dve.wait_ge(p_ok, i * U + u - 1)
                        sp_ = ps[:, 2 * g:2 * g + 2].rearrange("p a (h k) -> p (a h) k", k=2 * P)
                        carry_wait()
                        for h in range(4):
                            ins = v.tensor_tensor_reduce(out=sm[:, g, h, lo:], in0=sp_[:, h, lo:], in1=wmask[:, lo:],
                                                         scale=1.0, scalar=-3.0e38, op0=ALU.add, op1=ALU.max,
                                                         accum_out=mx[:, g, h:h + 1])
                        ch.link(ins)
                        v.tensor_scalar(nmx[:, g], mx[:, g], -QK_SCALE, None, ALU.mult).then_inc(sm_ok, 1)

                    scores_max(0)
                    for u in range(U):
                        t, g = u // 2, u % 2
                        lo = P if t == 0 else 0
                        if u + 1 < U:
                            scores_max(u + 1)
                        dve.wait_ge(pT_mm, i * U + u + 1)
                        if u:
                            dve.wait_ge(pv_mm, i * U + u)
                        v.tensor_copy(pT[:, 2:4, lo // P:], ps[:, 5].rearrange("p (h k q) -> p h k q", h=2, k=2)[:, :, lo // P:]).then_inc(pT_v, 1)
                        dve.wait_ge(p_ok, i * U + u + 1)
                        ch.mark(v.reciprocal(ri[:, t % 2, g], rs[:, t % 2, g]))
                        dve.wait_ge(pv_mm, i * U + u + 1)
                        ch.wait(ch.n)
                        if t >= 2:
                            dve.wait_ge(oT_mm, i * NT + t - 1)
                        v.tensor_tensor(ot[:, t % 2, :, g], ps[:, 6, g * 256:(g + 1) * 256].rearrange("p (c v) -> p c v", v=DH),
                                        ri[:, t % 2, g].unsqueeze(2).broadcast_to([P, 4, DH]), ALU.mult).then_inc(o_ok, 1)
                        if g == 0 and t:
                            rows_after_attention(t - 1)
                    rows_after_attention(NT - 1)
                    dve.wait_ge(sh_ok, i * (16 * 7) + 16 * 7)
                    for t in range(NT):
                        if t == 0:
                            carry_wait()
                        v.bn_stats(st[:, t, 0], xm[:, t, 0:P])
                        n = ch.mark(v.bn_stats(st[:, t, 1], hs[:, t]))
                    ch.wait(n)
                    carry_wait()
                    for t in range(NT):
                        ins = v.bn_aggr(mv[:, t], st[:, t].rearrange("p a b -> p (a b)"))
                    ch.link(ins)
                    v.tensor_scalar(ve[:, 0], mv[:, :, 1], 1e-5, None, ALU.add).then_inc(n2_ok, 1)
                    dve.wait_ge(nr_ok, (i + 1) * (NT + 1))
                    for t in range(NT):
                        v.tensor_scalar(xn[:, t, 0:P], xm[:, t, 0:P], mv[:, t, 0:1], ve[:, 1, t:t + 1], ALU.subtract, ALU.mult)
                        v.tensor_scalar(xn[:, t, P:D], hs[:, t], mv[:, t, 0:1], ve[:, 1, t:t + 1], ALU.subtract, ALU.mult).then_inc(xn_ok, 1)
                    dve.wait_ge(xn_mm, i + 1)
                    for c in range(KD):
                        ins = v.tensor_scalar(xnT[:, c], ps[:, 4 + c], lnp[:, 0, c:c + 1], lnp[:, 1, c:c + 1], ALU.mult, ALU.add)
                    ins.then_inc(xnT_ok, 1)
                    for m in range(MH):
                        n = P if m < MH - 1 else LAST
                        dve.wait_ge(g_act, i * MH + m + 1)
                        v.scalar_tensor_tensor(out=h2T[0:n, m], in0=ps[0:n, 2 + m % 2], scalar=b1[0:n, 0, m:m + 1],
                                               in1=gl[0:n, m % 2], op0=ALU.add, op1=ALU.mult).then_inc(h2_ok, 1)
                    dve.wait_ge(ld_a, i * 16 + 16)
                    for t in range(NT):
                        dve.wait_ge(y_mm, i * NT + t + 1)
                        for s in (st_y, st_o):
                            dve.wait_ge(s[t % 2], i * 32 + 16 * (t // 2))
                        ch.link(v.tensor_tensor(yt[:, t % 2], xm[:, t], ps[:, 6 + t % 2, 0:D], ALU.add))
                        v.scalar_tensor_tensor(out=yl[:, t % 2], in0=xadd[:, t], scalar=last[:, bass.ds(l, 1)], in1=yt[:, t % 2],
                                               op0=ALU.mult, op1=ALU.add).then_inc(y_ok, 1)
                    assert ch.n == LINKS, ch.n

        @block.tensor
        def _(pe):
            te = nc.tensor
            pe.wait_ge(ld_c, 4 * 16)
            with pe.Fori(0, NL) as l:
                with pe.Fori(0, B) as b:
                    i = l * B + b
                    pe.wait_ge(ld_w, (l + 1) * (16 * 8))
                    pe.wait_ge(ld_x, i * 16 + 16)
                    pe.wait_ge(y_ok, i * NT)
                    for c in range(KD):
                        for t in range(NT):
                            ins = te.transpose(ps[:, 6 + c, t * P:(t + 1) * P], xin[:, t, c * P:(c + 1) * P], ident[:])
                    ins.then_inc(x_mm, 1)
                    pe.wait_ge(hT_a, i + 1)
                    pe.wait_ge(hT_v, i + 1)

                    def qkv(t):
                        if t >= 2:
                            pe.wait_ge(qk_rd, i * NT + t - 1)
                            pe.wait_ge(v_ev, i * NT + t - 1)
                        for s in range(3):
                            for k in range(KD):
                                ins = te.matmul(ps[:, 3 * (t % 2) + s], hT[:, k, t * P:(t + 1) * P], wqkv[:, k, s * 512:(s + 1) * 512],
                                                start=(k == 0), stop=(k == KD - 1))
                        ins.then_inc(qkv_mm, 1)

                    def turn(t):
                        pe.wait_ge(qk_ok, i * NT + t + 1)
                        pe.wait_ge(qT_ok, i * NT + t)
                        pe.wait_ge(kT_ok, i * NT + t)
                        for s in range(2):
                            flat = qk[:, t % 2, s].rearrange("p h v -> p (h v)")
                            for c in range(NC):
                                ins = te.transpose(ps[:, 6 + s, c * P:(c + 1) * P], flat[:, c * P:(c + 1) * P], ident[:])
                        ins.then_inc(qk_mm, 1)

                    qkv(0)
                    for t in range(NT):
                        if t + 1 < NT:
                            qkv(t + 1)
                        turn(t)

                    def scores(u):
                        t, g = u // 2, u % 2
                        lo = P if t == 0 else 0
                        if u >= 2:
                            pe.wait_ge(sm_ok, i * U + u - 1)
                        if u == 0:
                            pe.wait_ge(qk_rd, i * NT + NT)
                            pe.wait_ge(v_ev, i * NT + NT)
                            pe.wait_ge(qT_ok, i * NT + NT)
                            pe.wait_ge(kT_ok, i * NT + NT)
                        sp_ = ps[:, 2 * g:2 * g + 2].rearrange("p a (h k) -> p (a h) k", k=2 * P)
                        for h in range(4):
                            ins = te.matmul(sp_[:, h, lo:], qT[64 * g:64 * g + 64, h, t * P:(t + 1) * P],
                                            kT[64 * g:64 * g + 64, h, t * P - P + lo:(t + 1) * P], start=True, stop=True)
                        ins.then_inc(s_mm, 1)

                    def project(t):
                        pe.wait_ge(o_ok, i * U + 2 * t + 2)
                        if t:
                            pe.wait_ge(xm_ok, i * NT + t)
                        flat = ot[:, t % 2].rearrange("p c g v -> p (c g v)")
                        for c in range(NC):
                            ins = te.transpose(ps[:, 7, c * P:(c + 1) * P], flat[:, c * P:(c + 1) * P], ident[:])
                        ins.then_inc(oT_mm, 1)
                        pe.wait_ge(oT_ok, i * NT + t + 1)
                        for c in range(NC):
                            ins = te.matmul(ps[:, 7, 0:D], oT[:, c], wo[:, c], start=(c == 0), stop=(c == NC - 1))
                        ins.then_inc(wo_mm, 1)

                    scores(0)
                    scores(1)
                    for u in range(U):
                        t, g = u // 2, u % 2
                        k0 = 1 if t == 0 else 0
                        pe.wait_ge(p_ok, i * U + u + 1)
                        if u:
                            pe.wait_ge(pT_a, i * U + u)
                            pe.wait_ge(pT_v, i * U + u)
                        for h in range(4):
                            for k in range(k0, 2):
                                ins = te.transpose(ps[:, 4 + h // 2, (h % 2 * 2 + k) * P:(h % 2 * 2 + k + 1) * P],
                                                   pr[:, g, h, k * P:(k + 1) * P], ident[:])
                        ins.then_inc(pT_mm, 1)
                        if u + 2 < U:
                            scores(u + 2)
                        pe.wait_ge(pT_a, i * U + u + 1)
                        pe.wait_ge(pT_v, i * U + u + 1)
                        if u:
                            pe.wait_ge(o_ok, i * U + u)
                        for h in range(4):
                            for k in range(k0, 2):
                                c0 = (2 * h + g) * DH
                                ins = te.matmul(ps[:, 6, g * 256 + h * DH:g * 256 + (h + 1) * DH], pT[:, h, k],
                                                vt[:, t - 1 + k, c0:c0 + DH], start=(k == k0), stop=(k == 1))
                        ins.then_inc(pv_mm, 1)
                        if g == 0 and t:
                            project(t - 1)
                    project(NT - 1)
                    for t in range(NT):
                        pe.wait_ge(xn_ok, i * NT + t + 1)
                        for c in range(KD):
                            ins = te.transpose(ps[:, 4 + c, t * P:(t + 1) * P], xn[:, t, c * P:(c + 1) * P], ident[:])
                    ins.then_inc(xn_mm, 1)
                    pe.wait_ge(xnT_ok, i + 1)
                    for m in range(MH):
                        n = P if m < MH - 1 else LAST
                        if m >= 2:
                            pe.wait_ge(h2_ok, i * MH + m - 1)
                        for part, bank in ((1, m % 2), (0, 2 + m % 2)):
                            for k in range(KD):
                                ins = te.matmul(ps[0:n, bank], w1[:, k, part * HID + m * P:part * HID + m * P + n], xnT[:, k],
                                                start=(k == 0), stop=(k == KD - 1))
                        ins.then_inc(g_mm, 1)
                    pe.wait_ge(h2_ok, i * MH + MH)
                    pe.wait_ge(xm_ok, i * NT + NT)
                    for t in range(NT):
                        if t >= 2:
                            pe.wait_ge(y_ok, i * NT + t - 1)
                        for m in range(MH):
                            n = P if m < MH - 1 else LAST + 1
                            ins = te.matmul(ps[:, 6 + t % 2, 0:D], h2T[0:n, m, t * P:(t + 1) * P], w2[0:n, m],
                                            start=(m == 0), stop=(m == MH - 1))
                        ins.then_inc(y_mm, 1)

        @block.gpsimd
        def _(pool):
            g = nc.gpsimd
            g.memset(mhalf[:], -0.5).then_inc(mh_ok, 1)
            pool.wait_ge(mh_ok, 1)
            with pool.Fori(0, NL * B) as i:
                for t in range(NT):
                    pool.wait_ge(n2_ok, i * (NT + 1) + t + 1)
                    g.tensor_tensor(n2[:, 1], n2[:, 0], mhalf[:], ALU.pow).then_inc(nr_ok, 1)
                pool.wait_ge(n2_ok, (i + 1) * (NT + 1))
                g.tensor_tensor(ve[:, 1], ve[:, 0], mhalf[:, 0:NT], ALU.pow).then_inc(nr_ok, 1)


def _chunks(w):
    k, n = w.shape
    return np.ascontiguousarray(w.reshape(k // P, P, n).transpose(1, 0, 2))


def _tokens_mask():
    m = np.ones((5, L), np.float32)
    m[1, L // 3:2 * (L // 3)] = 0
    m[2, :L // 3] = 0
    return m


def lay_out(i):
    g = {}
    g["x"] = i["x"]
    g["xT"] = np.ascontiguousarray(i["x"].reshape(B, L, KD, P).transpose(0, 3, 2, 1))
    g["condT"] = np.ascontiguousarray(i["cond_1024"].reshape(B, KD, P).transpose(2, 1, 0))
    g["gate_w"] = _chunks(i["L0_cond_gate_w"])
    g["gate_b"] = i["L0_cond_gate_b"][None]
    g["time_w"] = _chunks(i["L0_cond_time_w"])
    g["time_b"] = i["L0_cond_time_b"][None]
    g["ident"] = np.eye(P, dtype=np.float32)
    g["ew1"] = np.stack([_chunks(w) for w in i["L0_cond_ew1"]])
    g["ew2"] = np.stack([_chunks(w) for w in i["L0_cond_ew2"]])
    g["eb1"] = np.ascontiguousarray(i["L0_cond_eb1"].reshape(4, 8, P).transpose(0, 2, 1))
    g["sw1"] = _chunks(i["L0_cond_sw1"])
    g["sw2"] = _chunks(i["L0_cond_sw2"])
    g["sb1"] = np.ascontiguousarray(i["L0_cond_sb1"].reshape(8, P).T)
    g["eb2"] = np.concatenate([i["L0_cond_eb2"], i["L0_cond_sb2"][None]])
    g["mask5"] = _tokens_mask()
    order = [0, 2, 4, 6, 1, 3, 5, 7]
    g["wq"], g["wk"], g["wv"] = (_chunks(i[f"L0_attn_W{n}"]) for n in "qkv")
    g["wo"] = _chunks(i["L0_attn_Wo"].reshape(8, 64, D)[order].reshape(512, D))
    g["betas"] = np.ascontiguousarray(np.broadcast_to(i["L0_attn_betas"].reshape(8, 64)[order].reshape(1, 512), (P, 512)))
    c2 = {k[9:]: v for k, v in i.items() if k.startswith("L0_cond2_")}
    g["wada"], g["bada"] = _chunks(c2["w_ada"]), c2["b_ada"][None]
    g["bwqkv"] = _chunks(np.concatenate([c2["w_q"], c2["w_k"], c2["w_v"]], 1))
    g["bqkv"] = np.broadcast_to(np.concatenate([c2["b_q"], c2["b_k"], c2["b_v"]]), (P, 3 * D))
    g["bwo"], g["wf1"], g["wf2"] = (_chunks(c2[n]) for n in ("w_o", "w_f1", "w_f2"))
    g["bo"], g["bf2"] = (np.broadcast_to(c2[n], (P, D)) for n in ("b_o", "b_f2"))
    g["bf1"] = np.ascontiguousarray(c2["b_f1"].reshape(8, P).T)
    def pad(v, n=6 * P):
        return np.concatenate([v, np.zeros((n - v.shape[0],) + v.shape[1:], v.dtype)])

    hid = i["L0_ffn_w2"].shape[1]
    g["wqkv"] = np.stack([_chunks(w) for w in i["L0_ffn_wqkv"]])
    g["wwo"] = np.stack([_chunks(w) for w in i["L0_ffn_wo"]])
    g["w1"] = np.stack([_chunks(w) for w in i["L0_ffn_w1"]])
    g["b1"] = np.stack([np.stack([pad(v[:hid]).reshape(6, P).T, pad(v[hid:]).reshape(6, P).T], 1) for v in i["L0_ffn_b1"]])
    g["w2"] = np.stack([_chunks(pad(np.concatenate([w, v[None]]))) for w, v in zip(i["L0_ffn_w2"], i["L0_ffn_b2"])])
    g["lnp"] = np.stack([np.stack([w.reshape(2, P).T, v.reshape(2, P).T], 1) for w, v in zip(i["L0_ffn_ln_g"], i["L0_ffn_ln_b"])])
    qk = np.stack([i["L0_ffn_q_scale"], i["L0_ffn_k_scale"]], 1)
    qk = np.stack([qk, np.roll(qk, 32, axis=2)], 1).reshape(2, 1, 2, 128)
    g["qks"] = np.broadcast_to(qk, (2, P, 2, 128))
    g.update(_window_constants())
    return g


def _window_constants():
    f = np.float32
    half = np.arange(0, 64, 2, dtype=f)
    inv_freq = (f(1.0) / f(10000.0) ** (half / f(64))).astype(f)
    t = np.arange(L, dtype=f)
    freqs = t[:, None] * inv_freq[None]
    freqs = np.concatenate([freqs, freqs], -1)
    base = (half + f(0.4 * 64)) / f(1.4 * 64)
    scale = base[None] ** ((t - L // 2) / f(64))[:, None]
    scale = np.concatenate([scale, scale], -1).astype(f)
    sign = np.concatenate([-np.ones(32, f), np.ones(32, f)])
    cos, sin = np.cos(freqs), np.sin(freqs) * sign
    rot = np.stack([np.stack([cos * scale, cos / scale], 1), np.stack([sin * scale, sin / scale], 1)])
    rot = rot.reshape(2, NT, P, 2, 64).transpose(2, 0, 1, 3, 4).astype(f)
    q, k = np.arange(P)[:, None], np.arange(P)[None]
    mask = np.concatenate([np.where(k >= q, 0, -1e30), np.where(k <= q, 0, -1e30)], 1).astype(f)
    return {"rot": np.ascontiguousarray(rot), "wmask": mask, "last": np.broadcast_to(np.array([[0, 1]], f), (P, 2))}


STAGES = "123"


def program(nc, io, out):
    x1 = nc.dram_tensor("x1", (B, L, D), F32, kind="Internal").ap() if "x1" not in io else io["x1"]
    xs = nc.dram_tensor("xs", (3 * B, L, D), F32, kind="Internal").ap() if "xs" not in io else io["xs"]
    if "1" in STAGES:
        moe_attention(nc, io, x1)
    if "2" in STAGES:
        ball_block(nc, io, x1, xs)
    if "3" in STAGES:
        window_layers(nc, io, xs, x1, out)


def kernel(**inputs):
    import concourse.bacc as bacc
    from concourse.bass_utils import run_bass_kernel_spmd

    nc = bacc.Bacc("TRN2", target_bir_lowering=False, num_devices=1)
    arrays = {f"in_{k}": np.ascontiguousarray(v) for k, v in lay_out({k: np.asarray(v) for k, v in inputs.items()}).items()}
    io = {k[3:]: nc.dram_tensor(k, v.shape, mybir.dt.from_np(v.dtype), kind="ExternalInput").ap() for k, v in arrays.items()}
    out = nc.dram_tensor("out_x", (B, L, D), F32, kind="ExternalOutput").ap()
    program(nc, io, out)
    r = run_bass_kernel_spmd(nc, [arrays], core_ids=[0])
    return r.results[0]["out_x"]
```
